# Optimizing a Trainium2 kernel written in Bass

```python
import numpy as np
import jax
import jax.numpy as jnp

def _softmax(x, axis=-1):
    return jax.nn.softmax(x, axis=axis)

def _gelu(x):
    return jax.nn.gelu(x, approximate=True)

def _silu(x):
    return jax.nn.silu(x)

def _sigmoid(x):
    return jax.nn.sigmoid(x)

def _layernorm(x, axis=-1, eps=1e-05):
    m = jnp.mean(x, axis=axis, keepdims=True)
    v = jnp.var(x, axis=axis, keepdims=True)
    return (x - m) / jnp.sqrt(v + eps)

def _scatter_add(tgt, idx, src, axis=0):
    return tgt.at[idx].add(src)

def _segment_sum(src, seg, n):
    return jax.ops.segment_sum(src, seg, n)
kernel_name = 'mk_prb_d1_jaxref_r4_92c536'

def setup_inputs(seed: int=0):
    np.random.seed(seed)
    _w = jnp.asarray

    def _L0_attn_setup():
        import jax, jax.numpy as jnp
        import numpy as np
        EMBED_DIM = 256
        NUM_HEADS = 16
        HEAD_DIM = EMBED_DIM // NUM_HEADS
        ROPE_BASE = 10000.0

        def rotate_half(x):
            d = x.shape[-1] // 2
            x1, x2 = (x[..., :d], x[..., d:])
            return jnp.concatenate((-x2, x1), axis=-1)
        key = jax.random.key(seed)
        k_x, k_wqkv, k_bqkv, k_wo, k_bo = jax.random.split(key, 5)
        C = EMBED_DIM
        x = jax.random.normal(k_x, (4, 512, C), dtype=jnp.float32)
        s = 1.0 / np.sqrt(C)
        W_qkv = jax.random.uniform(k_wqkv, (C, 3 * C), minval=-s, maxval=s, dtype=jnp.float32)
        b_qkv = jax.random.uniform(k_bqkv, (3 * C,), minval=-s, maxval=s, dtype=jnp.float32)
        W_out = jax.random.uniform(k_wo, (C, C), minval=-s, maxval=s, dtype=jnp.float32)
        b_out = jax.random.uniform(k_bo, (C,), minval=-s, maxval=s, dtype=jnp.float32)
        return {'x': x, 'W_qkv': W_qkv, 'b_qkv': b_qkv, 'W_out': W_out, 'b_out': b_out}
    _L0_attn_in = _L0_attn_setup()

    def _L0_ffn_setup():
        import jax, jax.numpy as jnp
        import numpy as np
        B, S, H = (2, 256, 256)
        E, F = (16, 128)
        G, TOPK_G, TOPK = (4, 2, 4)
        N_SHARED = 2
        ROUTE_SCALE = 1.0
        FS = N_SHARED * F

        def _gate(x, w_gate):
            T = x.shape[0]
            scores = jax.nn.sigmoid(x @ w_gate.T)
            sv = scores.reshape(T, G, E // G)
            group_scores = jax.lax.top_k(sv, 2)[0].sum(-1)
            top_groups = jax.lax.top_k(group_scores, TOPK_G)[1]
            allowed = jnp.zeros((T, G), dtype=bool).at[jnp.arange(T)[:, None], top_groups].set(True)
            masked = jnp.where(allowed[:, :, None], sv, -jnp.inf).reshape(T, E)
            _, idx = jax.lax.top_k(masked, TOPK)
            w = jnp.take_along_axis(scores, idx, axis=1)
            w = w / (w.sum(-1, keepdims=True) + 1e-06) * ROUTE_SCALE
            return (w, idx)

        def _swiglu(x, w1, w3, w2):
            return jax.nn.silu(x @ w1.T) * (x @ w3.T) @ w2.T
        key = jax.random.key(seed)
        ks = jax.random.split(key, 8)
        scale = 0.02
        return {'hidden_states': jax.random.normal(ks[0], (B, S, H), dtype=jnp.float32), 'w_gate': jax.random.normal(ks[1], (E, H), dtype=jnp.float32) * scale, 'w1_e': jax.random.normal(ks[2], (E, F, H), dtype=jnp.float32) * scale, 'w3_e': jax.random.normal(ks[3], (E, F, H), dtype=jnp.float32) * scale, 'w2_e': jax.random.normal(ks[4], (E, H, F), dtype=jnp.float32) * scale, 'w1_s': jax.random.normal(ks[5], (FS, H), dtype=jnp.float32) * scale, 'w3_s': jax.random.normal(ks[6], (FS, H), dtype=jnp.float32) * scale, 'w2_s': jax.random.normal(ks[7], (H, FS), dtype=jnp.float32) * scale}
    _L0_ffn_in = _L0_ffn_setup()
    _d = {'L0_attn_x': _L0_attn_in['x'], 'L0_attn_W_qkv': _L0_attn_in['W_qkv'], 'L0_attn_b_qkv': _L0_attn_in['b_qkv'], 'L0_attn_W_out': _L0_attn_in['W_out'], 'L0_attn_b_out': _L0_attn_in['b_out'], 'L0_ffn_w_gate': _L0_ffn_in['w_gate'], 'L0_ffn_w1_e': _L0_ffn_in['w1_e'], 'L0_ffn_w3_e': _L0_ffn_in['w3_e'], 'L0_ffn_w2_e': _L0_ffn_in['w2_e'], 'L0_ffn_w1_s': _L0_ffn_in['w1_s'], 'L0_ffn_w3_s': _L0_ffn_in['w3_s'], 'L0_ffn_w2_s': _L0_ffn_in['w2_s']}
    _x0 = _d['L0_attn_x']
    _d['L0_attn_x'] = jax.random.normal(jax.random.fold_in(jax.random.key(seed), 1), (4, 1024, 256), dtype=_x0.dtype)
    del _x0
    return _d

def reference(L0_attn_x, L0_attn_W_qkv, L0_attn_b_qkv, L0_attn_W_out, L0_attn_b_out, L0_ffn_w_gate, L0_ffn_w1_e, L0_ffn_w3_e, L0_ffn_w2_e, L0_ffn_w1_s, L0_ffn_w3_s, L0_ffn_w2_s):

    def _L0_attn_ref(x, W_qkv, b_qkv, W_out, b_out):
        import jax, jax.numpy as jnp
        import numpy as np
        EMBED_DIM = 256
        NUM_HEADS = 16
        HEAD_DIM = EMBED_DIM // NUM_HEADS
        ROPE_BASE = 10000.0

        def rotate_half(x):
            d = x.shape[-1] // 2
            x1, x2 = (x[..., :d], x[..., d:])
            return jnp.concatenate((-x2, x1), axis=-1)
        B, T, C = x.shape
        H, Dh = (NUM_HEADS, HEAD_DIM)
        qkv = (x @ W_qkv + b_qkv).reshape(B, T, 3, H, Dh).transpose(2, 0, 3, 1, 4)
        q, k, v = (qkv[0], qkv[1], qkv[2])
        inv_freq = 1.0 / ROPE_BASE ** (jnp.arange(0, Dh, 2, dtype=jnp.float32) / Dh)
        freqs = jnp.arange(T, dtype=jnp.float32)[:, None] * inv_freq[None, :]
        emb = jnp.concatenate((freqs, freqs), axis=-1)
        cos, sin = (jnp.cos(emb), jnp.sin(emb))
        q = q * cos + rotate_half(q) * sin
        k = k * cos + rotate_half(k) * sin
        scale = 1.0 / np.sqrt(Dh)
        attn = jax.nn.softmax(jnp.einsum('bhqd,bhkd->bhqk', q, k) * scale, axis=-1)
        out = jnp.einsum('bhqk,bhkd->bhqd', attn, v)
        out = out.transpose(0, 2, 1, 3).reshape(B, T, C)
        return out @ W_out + b_out

    def _L0_ffn_ref(hidden_states, w_gate, w1_e, w3_e, w2_e, w1_s, w3_s, w2_s):
        import jax, jax.numpy as jnp
        import numpy as np
        B, S, H = (2, 256, 256)
        E, F = (16, 128)
        G, TOPK_G, TOPK = (4, 2, 4)
        N_SHARED = 2
        ROUTE_SCALE = 1.0
        FS = N_SHARED * F

        def _gate(x, w_gate):
            T = x.shape[0]
            scores = jax.nn.sigmoid(x @ w_gate.T)
            sv = scores.reshape(T, G, E // G)
            group_scores = jax.lax.top_k(sv, 2)[0].sum(-1)
            top_groups = jax.lax.top_k(group_scores, TOPK_G)[1]
            allowed = jnp.zeros((T, G), dtype=bool).at[jnp.arange(T)[:, None], top_groups].set(True)
            masked = jnp.where(allowed[:, :, None], sv, -jnp.inf).reshape(T, E)
            _, idx = jax.lax.top_k(masked, TOPK)
            w = jnp.take_along_axis(scores, idx, axis=1)
            w = w / (w.sum(-1, keepdims=True) + 1e-06) * ROUTE_SCALE
            return (w, idx)

        def _swiglu(x, w1, w3, w2):
            return jax.nn.silu(x @ w1.T) * (x @ w3.T) @ w2.T
        shape = hidden_states.shape
        x = hidden_states.reshape(-1, H)
        weights, idx = _gate(x, w_gate)
        combine = (jax.nn.one_hot(idx, E, dtype=x.dtype) * weights[..., None]).sum(1)
        g = jax.nn.silu(jnp.einsum('th,efh->tef', x, w1_e))
        u = jnp.einsum('th,efh->tef', x, w3_e)
        routed = jnp.einsum('tef,ehf,te->th', g * u, w2_e, combine)
        shared = _swiglu(x, w1_s, w3_s, w2_s)
        return (routed + shared).reshape(shape)
    x = L0_attn_x
    xn = _layernorm(x, axis=-1)
    x = x + _L0_attn_ref(xn, L0_attn_W_qkv, L0_attn_b_qkv, L0_attn_W_out, L0_attn_b_out) + _L0_ffn_ref(xn, L0_ffn_w_gate, L0_ffn_w1_e, L0_ffn_w3_e, L0_ffn_w2_e, L0_ffn_w1_s, L0_ffn_w3_s, L0_ffn_w2_s)
    return x

_drawn_inputs = setup_inputs


def setup_inputs(seed=0):
    import zlib

    import numpy as np

    out = dict(_drawn_inputs(seed))
    spreads = {}
    factors = {'L0_attn_W_qkv': 5.048,
     'L0_ffn_w_gate': 8.0,
     'L0_ffn_w1_e': 8.0,
     'L0_ffn_w3_e': 8.0,
     'L0_ffn_w2_e': 8.0,
     'L0_ffn_w1_s': 3.383,
     'L0_ffn_w3_s': 3.348,
     'L0_ffn_w2_s': 3.351,
     'L0_attn_b_qkv': 3.683,
     'L0_attn_b_out': 7.065}
    for name, (base, spread) in spreads.items():
        noise = np.random.default_rng([zlib.crc32(name.encode()), seed]).standard_normal(out[name].shape)
        drawn = base * np.exp(spread * noise) if base else spread * noise
        out[name] = jnp.asarray(drawn.astype(out[name].dtype))
    for name, factor in factors.items():
        out[name] = (out[name] * factor).astype(out[name].dtype)
    return out
```

```python
from contextlib import ExitStack

import numpy as np

import concourse.bass as bass
from concourse import mybir

F32 = mybir.dt.float32
BF16 = mybir.dt.bfloat16
ALU = mybir.AluOpType
ACT = mybir.ActivationFunctionType
AX = mybir.AxisListType

P = 128
B, T, C = 4, 1024, 256
N = B * T
H, D = 16, 16
NT = N // P
TPB = T // P
CC = C // P
E, F = 16, 128
NS = 2
EPS = 1e-5
ROPE_BASE = 10000.0

HG = 4
NG = B * H // HG
GR = HG * D
QH = T // 2
VW = D + 1
Q_PART = [0, 0, 0, 1, 1, 2]
K_PART = [0, 1, 2, 0, 1, 0]
TERMS = len(Q_PART)
KR = TERMS * D
MR = 3
SCALE = D ** -0.5


def need(eng, sem, n):
    if isinstance(n, int) and n <= 0:
        return
    eng.wait_ge(sem, n)


def wait_alone(eng, sem, n, passed):
    eng.wait_ge(sem, n)
    eng.sem_inc(passed, 1)


class Chain:

    def __init__(self, eng, sem, passed=None):
        self.eng, self.sem, self.passed, self.base, self.n, self.per = eng, sem, passed, 0, 0, 0

    def link(self, ins):
        self.n += 1
        ins.then_inc(self.sem, 1)
        if self.passed is None:
            self.eng.wait_ge(self.sem, self.base + self.n)
        else:
            wait_alone(self.eng, self.sem, self.base + self.n, self.passed)


def rounds(eng, n, emit):
    emit(0)
    with eng.Fori(1, n) as j:
        emit(j)


def stage_a(nc, x, w_qkvg, b_qkv, rope, s_q, s_v, s_xn, comb):
    W = 3 * C + E
    with ExitStack() as ctx:
        sb = lambda n, s, d=F32: ctx.enter_context(nc.sbuf_tensor(n, s, d))
        ps = lambda n, s: ctx.enter_context(nc.psum_tensor(n, s, F32))
        sem = lambda n: ctx.enter_context(nc.semaphore(n))

        xs = sb("xs", [P, NT, C])
        wsb = sb("wsb", [P, CC, W])
        brow = sb("brow", [1, W])
        brest = sb("brest", [1, W])
        bparts = [sb(f"bpart{n}", [1, W], BF16) for n in range(3)]
        bias3 = sb("bias3", [3, W], BF16)
        ones3 = sb("ones3", [3, P], BF16)
        ropesb = sb("ropesb", [P, TPB, 2, D])
        ident = sb("ident_a", [P, P])
        bnst = sb("bnst", [P, TPB, 6])
        mv = sb("mv", [P, TPB, 2])
        var = sb("var", [P, TPB])
        std = sb("std", [P, TPB])
        rstd = sb("rstd", [P, TPB])
        nwt = sb("nwt", [P, TPB])
        xn = sb("xn_a", [P, 2, C])
        xt = sb("xt_a", [P, 2, CC, P])
        qks = sb("qks", [P, 2, 2 * C])
        rc = sb("rc", [P, 2, 2 * C])
        rs = sb("rs", [P, 2, 2 * C])
        qr = sb("qr", [P, 2, 2 * C])
        r1 = sb("r1", [P, 2, 4, P])
        stg = sb("stg", [P, 2, 3, 4, 4 * P], BF16)
        vst = sb("vst", [P, 2, H, VW])
        lg = sb("lg", [P, NT, E])

        gate_bufs = {}
        for name, shape in dict(ex=[P, NT, E], sc=[P, NT, E], hi=[P, NT * 4, 2], lo=[P, NT * 4, 2], m1=[P, NT * 4],
                                m2=[P, NT * 4], gs=[P, NT, 4], gt=[P, NT, 4, 4], ge=[P, NT, 4, 4],
                                lt4=[P, 4, 4], rank=[P, NT, 4], ok=[P, NT, 4], ms=[P, NT, E], top=[P, NT, 8],
                                a=[P, NT, E], bq=[P, NT, E], c=[P, NT, E], cnt=[P, NT], ws=[P, NT]).items():
            gate_bufs[name] = sb("g_" + name, shape)

        pT = [ps(f"pT{i}", [P, 512]) for i in range(2)]
        pQ = [ps(f"pQ{i}", [P, 512]) for i in range(2)]
        pV = [ps(f"pV{i}", [P, 512]) for i in range(2)]
        pR = [ps(f"pR{i}", [P, 512]) for i in range(2)]

        x_in = [sem(f"x_in{b}") for b in range(B)]
        w_in, c_in, b_in, b3_in = sem("w_in"), sem("c_in"), sem("b_in"), sem("b3_in")
        id_ok, ones_ok, bp_ok = sem("id_ok"), sem("ones_ok"), sem("bp_ok")
        dve_own, pool_own = sem("dve_own_a"), sem("pool_own_a")
        var_ok, std_ok = sem("var_ok"), sem("std_ok")
        xn_ok, xT_ok, xt_ok = sem("xn_ok"), sem("xT_ok"), sem("xt_ok")
        qk_ok, qks_ok, vg_ok, vs_ok = sem("qk_ok"), sem("qks_ok"), sem("vg_ok"), sem("vs_ok")
        rc_ok, rs_ok, qr_ok, qrT_ok = sem("rc_ok"), sem("rs_ok"), sem("qr_ok"), sem("qrT_ok")
        p1_ok, r1_ok, p3_ok = sem("p1_ok"), sem("r1_ok"), sem("p3_ok")
        st_out = [sem(f"st_out{i}") for i in range(2)]
        v_out = [sem(f"v_out{i}") for i in range(2)]
        xn_out = [sem(f"xn_out{i}") for i in range(2)]
        lg_ok, ex_ok = sem("lg_ok"), sem("ex_ok")
        passed, passed_dve = sem("passed_a"), sem("passed_dve_a")
        block = ctx.enter_context(nc.Block())

        x_tiles = x.rearrange("b (n p) c -> b p n c", p=P)

        @block.sync
        def _(sp):
            sp.dma_start(brow[:, 0:3 * C], b_qkv.rearrange("(a c) -> a c", a=1)).then_inc(b_in, 16)
            for b in range(B):
                sp.dma_start(xs[:, b * TPB:(b + 1) * TPB, :], x_tiles[b]).then_inc(x_in[b], 16)
                if b == 0:
                    sp.dma_start(wsb[:], w_qkvg.rearrange("(c p) n -> p c n", p=P)).then_inc(w_in, 16)
                    sp.dma_start(ropesb[:], rope.rearrange("(n p) a d -> p n a d", p=P)).then_inc(c_in, 16)
            sp.wait_ge(bp_ok, 3)
            for n in range(3):
                sp.dma_start(bias3[n:n + 1, :], bparts[n][:]).then_inc(b3_in, 16)

            def batch(b):
                for hh in range(2):
                    for s in range(4):
                        t = hh * 4 + s
                        row = b * T + t * P
                        sp.wait_ge(xn_ok, b * TPB + t + 1)
                        sp.dma_start(s_xn[bass.ds(row, P), :], xn[:, t % 2, :]).then_inc(xn_out[t % 2], 16)
                        sp.wait_ge(vs_ok, b * TPB + t + 1)
                        sp.dma_start(s_v[bass.ds(row, P), :, :], vst[:, t % 2, :, :]).then_inc(v_out[t % 2], 16)
                    sp.wait_ge(p3_ok, b * TPB + hh * 4 + 4)
                    for part in range(3):
                        for blk in range(4):
                            rows = b * C + (blk % 2) * P
                            sp.dma_start(s_q[blk // 2, part, bass.ds(rows, P), hh * 512:(hh + 1) * 512],
                                         stg[:, hh, part, blk, :]).then_inc(st_out[hh], 16)
            rounds(sp, B, batch)
            for i in range(2):
                sp.wait_ge(st_out[i], 12 * 16 * B)
                sp.wait_ge(v_out[i], 16 * NT // 2)
                sp.wait_ge(xn_out[i], 16 * NT // 2)

        @block.gpsimd
        def _(pool):
            own = Chain(pool, pool_own)
            own.link(nc.gpsimd.memset(ident[:], 0.0))
            nc.gpsimd.affine_select(out=ident[:], in_=ident[:], compare_op=ALU.not_equal, fill=1.0, base=0,
                                    pattern=[[-1, P]], channel_multiplier=1).then_inc(id_ok, 1)
            nc.gpsimd.memset(ones3[:], 1.0).then_inc(ones_ok, 1)
            nc.gpsimd.memset(vst[:], 1.0).then_inc(ones_ok, 1)
            own.link(nc.gpsimd.memset(brow[:, 3 * C:W], 0.0))
            pool.wait_ge(b_in, 16)
            nc.gpsimd.tensor_copy(bparts[0][:], brow[:]).then_inc(bp_ok, 1)
            pool.wait_ge(bp_ok, 1)
            own.link(nc.gpsimd.tensor_tensor(brest[:], brow[:], bparts[0][:], ALU.subtract))
            nc.gpsimd.tensor_copy(bparts[1][:], brest[:]).then_inc(bp_ok, 1)
            pool.wait_ge(bp_ok, 2)
            nc.gpsimd.tensor_tensor(bparts[2][:], brest[:], bparts[1][:], ALU.subtract).then_inc(bp_ok, 1)
            pool.wait_ge(c_in, 16)
            heads = lambda a: a.rearrange("p (h d) -> p h d", d=D)

            def sines(b, t):
                sl = t % 2
                pool.wait_ge(qks_ok, b * TPB + t + 1)
                need(pool, qr_ok, b * TPB + t - 1)
                src, dst = heads(qks[:, sl, :]), heads(rs[:, sl, :])
                sn = ropesb[:, t, 1:2, :]
                hd = D // 2
                nc.gpsimd.tensor_tensor(dst[:, :, 0:hd], src[:, :, hd:D],
                                        sn[:, :, 0:hd].to_broadcast([P, 2 * H, hd]), ALU.mult)
                nc.gpsimd.tensor_tensor(dst[:, :, hd:D], src[:, :, 0:hd],
                                        sn[:, :, hd:D].to_broadcast([P, 2 * H, hd]), ALU.mult).then_inc(rs_ok, 1)

            def parts(b, t):
                sl, hh = t % 2, t // 4
                c0 = (t % 4) * P
                wait_alone(pool, r1_ok, b * TPB + t + 1, passed)
                own.link(nc.gpsimd.tensor_copy(stg[:, hh, 1, :, c0:c0 + P], r1[:, sl, :, :]))
                nc.gpsimd.tensor_tensor(stg[:, hh, 2, :, c0:c0 + P], r1[:, sl, :, :],
                                        stg[:, hh, 1, :, c0:c0 + P], ALU.subtract).then_inc(p3_ok, 1)

            setup = own.n

            def batch(b):
                own.n, own.base = 0, setup + b * TPB
                for s in range(TPB + 1):
                    if s < TPB:
                        sines(b, s)
                    if s >= 1:
                        parts(b, s - 1)
            rounds(pool, B, batch)

        @block.vector
        def _(dve):
            own = Chain(dve, dve_own)
            dve.wait_ge(c_in, 16)

            def batch(b):
                own.n = 0
                own.base = b * own.per
                for bb in range(B):
                    if isinstance(b, int):
                        if bb == b:
                            dve.wait_ge(x_in[bb], 16)
                    else:
                        if bb > 0:
                            dve.wait_ge(x_in[bb], 16)
                xb = xs[:, bass.ds(b * TPB, TPB), :]
                for t in range(TPB):
                    nc.vector.bn_stats(bnst[:, t, :], xb[:, t, :]).then_inc(dve_own, 1)
                    own.n += 1
                wait_alone(dve, dve_own, own.base + own.n, passed_dve)
                for t in range(TPB):
                    nc.vector.bn_aggr(mv[:, t, :], bnst[:, t, :]).then_inc(dve_own, 1)
                    own.n += 1
                dve.wait_ge(dve_own, own.base + own.n)
                own.link(nc.vector.tensor_scalar(var[:], mv[:, :, 1], EPS, None, ALU.add))
                nc.vector.tensor_copy(nwt[:], var[:]).then_inc(var_ok, 1)
                dve.wait_ge(std_ok, b + 1)
                own.link(nc.vector.reciprocal(rstd[:], std[:]))
                own.link(nc.vector.tensor_tensor(nwt[:], rstd[:], rstd[:], ALU.mult))
                own.link(nc.vector.tensor_tensor(nwt[:], nwt[:], var[:], ALU.mult))
                own.link(nc.vector.tensor_scalar(nwt[:], nwt[:], -0.5, 1.5, ALU.mult, ALU.add))
                own.link(nc.vector.tensor_tensor(rstd[:], rstd[:], nwt[:], ALU.mult))

                def normalise(t):
                    k = b * TPB + t
                    need(dve, xT_ok, k - 1)
                    need(dve, xn_out[t % 2], (b * TPB // 2 + t // 2) * 16)
                    nc.vector.tensor_scalar(xn[:, t % 2, :], xb[:, t, :], mv[:, t, 0:1], rstd[:, t:t + 1],
                                            ALU.subtract, ALU.mult).then_inc(xn_ok, 1)

                def cosines(t):
                    k = b * TPB + t
                    dve.wait_ge(qks_ok, k + 1)
                    q3 = qks[:, t % 2, :].rearrange("p (h d) -> p h d", d=D)
                    o3 = rc[:, t % 2, :].rearrange("p (h d) -> p h d", d=D)
                    own.link(nc.vector.tensor_tensor(o3, q3, ropesb[:, t, 0:1, :].to_broadcast([P, 2 * H, D]),
                                                     ALU.mult))
                    dve.wait_ge(rs_ok, k + 1)
                    need(dve, qrT_ok, k - 1)
                    nc.vector.tensor_tensor(qr[:, t % 2, :], rc[:, t % 2, :], rs[:, t % 2, :],
                                            ALU.add).then_inc(qr_ok, 1)

                def rest(t):
                    k = b * TPB + t
                    dve.wait_ge(p1_ok, k + 1)
                    need(dve, p3_ok, k - 1)
                    c0 = (t % 4) * P
                    nc.vector.tensor_tensor(r1[:, t % 2, :, :], pR[t % 2][:, :].rearrange("p (k n) -> p k n", k=4),
                                            stg[:, t // 4, 0, :, c0:c0 + P], ALU.subtract).then_inc(r1_ok, 1)

                for s in range(TPB + 2):
                    if s < TPB:
                        normalise(s)
                    if 1 <= s <= TPB:
                        cosines(s - 1)
                    if s >= 2:
                        rest(s - 2)
                own.per = own.per or own.n
            rounds(dve, B, batch)
            gate(nc, dve, gate_bufs, lg, comb, lg_ok, ex_ok, dve_own, B * own.per)

        @block.scalar
        def _(act):
            act.wait_ge(ones_ok, 2)

            def batch(b):
                act.wait_ge(var_ok, b + 1)
                nc.scalar.activation(std[:], var[:], ACT.Sqrt).then_inc(std_ok, 1)

                def turn(t):
                    k = b * TPB + t
                    act.wait_ge(xT_ok, k + 1)
                    need(act, qk_ok, k - 1)
                    need(act, vg_ok, k - 1)
                    nc.scalar.activation(xt[:, t % 2, :, :], pT[t % 2][:, 0:C].rearrange("p (c n) -> p c n", c=CC),
                                         ACT.Copy).then_inc(xt_ok, 1)

                def take(t):
                    k = b * TPB + t
                    act.wait_ge(qk_ok, k + 1)
                    need(act, qr_ok, k - 1)
                    nc.scalar.activation(qks[:, t % 2, :], pQ[t % 2][:, :], ACT.Copy).then_inc(qks_ok, 1)
                    act.wait_ge(vg_ok, k + 1)
                    need(act, v_out[t % 2], (b * TPB // 2 + t // 2) * 16)
                    nc.scalar.activation(vst[:, t % 2, :, 0:D],
                                         pV[t % 2][:, 0:C].rearrange("p (h d) -> p h d", d=D), ACT.Copy)\
                        .then_inc(vs_ok, 1)
                    nc.scalar.activation(lg[:, bass.ds(k, 1), :], pV[t % 2][:, C:C + E].unsqueeze(1), ACT.Copy)\
                        .then_inc(lg_ok, 1)

                def part1(t):
                    k = b * TPB + t
                    act.wait_ge(qrT_ok, k + 1)
                    if t % 4 == 0:
                        need(act, st_out[t // 4], b * 12 * 16)
                    c0 = (t % 4) * P
                    nc.scalar.activation(stg[:, t // 4, 0, :, c0:c0 + P],
                                         pR[t % 2][:, :].rearrange("p (k n) -> p k n", k=4), ACT.Copy)\
                        .then_inc(p1_ok, 1)

                for s in range(TPB + 2):
                    if s < TPB:
                        turn(s)
                    if 1 <= s <= TPB:
                        take(s - 1)
                    if s >= 2:
                        part1(s - 2)
            rounds(act, B, batch)
            act.wait_ge(lg_ok, NT)
            nc.scalar.activation(gate_bufs["ex"][:], lg[:], ACT.Exp, scale=-1.0).then_inc(ex_ok, 1)

        @block.tensor
        def _(pe):
            pe.wait_ge(id_ok, 1)
            pe.wait_ge(ones_ok, 1)
            pe.wait_ge(w_in, 16)

            def batch(b):
                def turn(t):
                    k = b * TPB + t
                    pe.wait_ge(xn_ok, k + 1)
                    need(pe, xt_ok, k - 1)
                    for c in range(CC):
                        mm = pe.transpose(pT[t % 2][:, c * P:(c + 1) * P], xn[:, t % 2, c * P:(c + 1) * P], ident[:])
                    mm.then_inc(xT_ok, 1)

                def project(t):
                    k = b * TPB + t
                    pe.wait_ge(xt_ok, k + 1)
                    if t == 0:
                        pe.wait_ge(b3_in, 48)
                    need(pe, qks_ok, k - 1)
                    pe.matmul(pQ[t % 2][:, :], ones3[:], bias3[:, 0:2 * C], start=True, stop=False)
                    for c in range(CC):
                        mm = pe.matmul(pQ[t % 2][:, :], xt[:, t % 2, c, :], wsb[:, c, 0:2 * C],
                                       start=False, stop=(c == CC - 1))
                    mm.then_inc(qk_ok, 1)
                    need(pe, lg_ok, k - 1)
                    pe.matmul(pV[t % 2][:, 0:C + E], ones3[:], bias3[:, 2 * C:W], start=True, stop=False)
                    for c in range(CC):
                        mm = pe.matmul(pV[t % 2][:, 0:C + E], xt[:, t % 2, c, :], wsb[:, c, 2 * C:W],
                                       start=False, stop=(c == CC - 1))
                    mm.then_inc(vg_ok, 1)

                def turn_qk(t):
                    k = b * TPB + t
                    pe.wait_ge(qr_ok, k + 1)
                    need(pe, r1_ok, k - 1)
                    for blk in range(4):
                        mm = pe.transpose(pR[t % 2][:, blk * P:(blk + 1) * P], qr[:, t % 2, blk * P:(blk + 1) * P],
                                          ident[:])
                    mm.then_inc(qrT_ok, 1)

                for s in range(TPB + 2):
                    if s < TPB:
                        turn(s)
                    if 1 <= s <= TPB:
                        project(s - 1)
                    if s >= 2:
                        turn_qk(s - 2)
            rounds(pe, B, batch)


def gate(nc, dve, buf, lg, comb, lg_ok, ex_ok, own_sem, base):
    own = Chain(dve, own_sem)
    own.base = base
    b = lambda n: buf[n]
    v = nc.vector
    G = 4
    tt = lambda o, x, y, op: own.link(v.tensor_tensor(o, x, y, op))
    own.link(v.memset(b("lt4")[:], 0.0))
    for g in range(1, G):
        own.link(v.memset(b("lt4")[:, g, 0:g], 1.0))
    own.link(v.memset(comb[:, :, E:E + NS], 1.0))
    dve.wait_ge(ex_ok, 1)
    own.link(v.tensor_scalar(b("ex")[:], b("ex")[:], 1.0, None, ALU.add))
    own.link(v.reciprocal(b("sc")[:], b("ex")[:]))
    s2 = b("sc")[:].rearrange("p n (g q r) -> p (n g) q r", g=G, q=2)
    hi, lo = b("hi"), b("lo")
    tt(hi[:], s2[:, :, :, 0], s2[:, :, :, 1], ALU.max)
    tt(lo[:], s2[:, :, :, 0], s2[:, :, :, 1], ALU.min)
    tt(b("m1")[:], hi[:, :, 0], hi[:, :, 1], ALU.max)
    tt(b("m2")[:], hi[:, :, 0], hi[:, :, 1], ALU.min)
    tt(lo[:, :, 0], lo[:, :, 0], lo[:, :, 1], ALU.max)
    tt(b("m2")[:], b("m2")[:], lo[:, :, 0], ALU.max)
    gs = b("gs")
    tt(gs[:].rearrange("p n g -> p (n g)"), b("m1")[:], b("m2")[:], ALU.add)
    own_g = gs[:].unsqueeze(3).to_broadcast([P, NT, G, G])
    other = gs[:].unsqueeze(2).to_broadcast([P, NT, G, G])
    tt(b("gt")[:], other, own_g, ALU.is_gt)
    tt(b("ge")[:], other, own_g, ALU.is_equal)
    tt(b("ge")[:], b("ge")[:], b("lt4")[:].unsqueeze(1).to_broadcast([P, NT, G, G]), ALU.mult)
    tt(b("gt")[:], b("gt")[:], b("ge")[:], ALU.add)
    own.link(v.tensor_reduce(b("rank")[:], b("gt")[:], AX.X, ALU.add))
    own.link(v.tensor_scalar(b("ok")[:], b("rank")[:], 2.0, None, ALU.is_lt))
    ok16 = b("ok")[:].unsqueeze(3).to_broadcast([P, NT, G, E // G])
    g4 = lambda n: b(n)[:].rearrange("p n (g q) -> p n g q", g=G)
    tt(g4("ms"), g4("sc"), ok16, ALU.mult)
    tt(g4("ms"), g4("ms"), ok16, ALU.add)
    own.link(v.tensor_scalar(b("ms")[:], b("ms")[:], -1.0, None, ALU.add))
    for t in range(NT):
        last = v.max(b("top")[:, t, :], b("ms")[:, t, :])
        own.n += 1
        last.then_inc(own_sem, 1)
    dve.wait_ge(own_sem, own.base + own.n)
    fourth = b("top")[:, :, 3:4].to_broadcast([P, NT, E])
    tt(b("a")[:], b("ms")[:], fourth, ALU.is_gt)
    tt(b("bq")[:], b("ms")[:], fourth, ALU.is_equal)
    own.link(v.tensor_reduce(b("cnt")[:], b("a")[:], AX.X, ALU.add))
    own.link(v.tensor_scalar(b("cnt")[:], b("cnt")[:], -1.0, 4.0, ALU.mult, ALU.add))
    for sh, src, dst in ((1, "bq", "c"), (2, "c", "ex"), (4, "ex", "c"), (8, "c", "ex")):
        own.link(v.tensor_copy(b(dst)[:, :, 0:sh], b(src)[:, :, 0:sh]))
        tt(b(dst)[:, :, sh:E], b(src)[:, :, sh:E], b(src)[:, :, 0:E - sh], ALU.add)
    tt(b("c")[:], b("ex")[:], b("cnt")[:].unsqueeze(2).to_broadcast([P, NT, E]), ALU.is_le)
    tt(b("bq")[:], b("bq")[:], b("c")[:], ALU.mult)
    tt(b("a")[:], b("a")[:], b("bq")[:], ALU.add)
    tt(b("a")[:], b("a")[:], b("sc")[:], ALU.mult)
    own.link(v.tensor_reduce(b("ws")[:], b("a")[:], AX.X, ALU.add))
    own.link(v.tensor_scalar(b("ws")[:], b("ws")[:], 1e-6, None, ALU.add))
    own.link(v.reciprocal(b("ws")[:], b("ws")[:]))
    tt(comb[:, :, 0:E], b("a")[:], b("ws")[:].unsqueeze(2).to_broadcast([P, NT, E]), ALU.mult)


QUADS = 16
KC = T // P
LOAD = 16 * 3 * TERMS


def stage_b(nc, s_q, s_v, s_o):
    with ExitStack() as ctx:
        sb = lambda n, s, d=F32: ctx.enter_context(nc.sbuf_tensor(n, s, d))
        sem = lambda n: ctx.enter_context(nc.semaphore(n))
        qt = [sb(f"qt{i}", [P, 2, HG, QH], BF16) for i in range(2)]
        kt = [sb(f"kt{i}", [P, HG, T], BF16) for i in range(2)]
        vt = [sb(f"vt{i}", [P, KC, HG * VW]) for i in range(2)]
        pr = sb("pr", [P, 8, QH])
        mx = sb("mx", [P, 2, 16])
        mrest = sb("mrest", [P, 16])
        mp = sb("mp", [P, 2, 3, 16], BF16)
        mrow = sb("mrow", [48, 2, P], BF16)
        osb = sb("osb", [P, QH])
        rec = sb("rec", [P, 16])
        on = sb("on", [P, 2, 4, HG, D])
        identb = sb("identb", [P, P], BF16)
        ident = sb("ident_b", [P, P])

        pm = [ctx.enter_context(nc.psum_tensor(f"pm{i}", [P, 2, 512], F32)) for i in range(2)]
        pst = [ctx.enter_context(nc.psum_tensor(f"pst{i}", [P, 512], F32)) for i in range(2)]
        po = [ctx.enter_context(nc.psum_tensor(f"po{i}", [P, 512], F32)) for i in range(2)]

        id_ok, row1_ok, po_ok = sem("idb_ok"), sem("row1_ok"), sem("po_ok")
        qk_in = [sem(f"qk_in{i}") for i in range(2)]
        v_in = [sem(f"v_in{i}") for i in range(2)]
        st_ok, exp_ok, pv_ok = sem("st_ok"), sem("exp_ok"), sem("pv_ok")
        mx_full, mx_free = sem("mx_full"), sem("mx_free")
        mp_ok = sem("mp_ok")
        mrow_in = [sem(f"mrow_in{i}") for i in range(2)]
        osb_ok, rec_ok = sem("osb_ok"), sem("rec_ok")
        o_out = [sem(f"o_out{i}") for i in range(2)]
        pool_own, passed = sem("pool_own_b"), sem("passed_b")
        block = ctx.enter_context(nc.Block())

        def uses(k):
            tasks = [28 + 2 * k, 29 + 2 * k] if k < 2 else [2 * k - 4, 2 * k - 3]
            more = {2: ["out"], 10: ["out"], 3: ["rows"], 11: ["rows"]}.get(k, [])
            return tasks + more
        FIRST = 28 + 1
        before = [sum(len(uses(i)) for i in range(k)) for k in range(QUADS + 1)]
        PER = before[QUADS]

        def place(g, k, i):
            return FIRST + g * PER + before[k] + i

        @block.sync
        def _(sp):
            def load(buf, gi):
                part = lambda which, n: s_q[which, n, bass.ds(gi * GR, GR), :].rearrange("(h d) t -> d h t", d=D)
                for n in range(TERMS):
                    rows = slice(n * D, (n + 1) * D)
                    for half in range(2):
                        sp.dma_start(qt[buf][rows, half, :, :], part(0, Q_PART[n])[:, :, half * QH:(half + 1) * QH])\
                            .then_inc(qk_in[buf], 16)
                    sp.dma_start(kt[buf][rows, :, :], part(1, K_PART[n])).then_inc(qk_in[buf], 16)

            def load_v(buf, j, gg):
                sp.dma_start(vt[buf][:, :, :],
                             s_v[bass.ds((j // 2) * T, T), bass.ds((j % 2) * 2 * HG + gg * HG, HG), :]
                             .rearrange("(n p) h w -> p n (h w)", p=P)).then_inc(v_in[buf], 16)

            def rows(use, half, buf):
                sp.wait_ge(mx_free, use + 1)
                sp.dma_start(qt[buf][KR:KR + MR, half, :, :], mrow[:, half, :]).then_inc(mrow_in[half], 16)

            def store(use, half, j, gg):
                sp.wait_ge(mx_free, use + 1)
                dst = s_o[bass.ds((j // 2) * T + half * QH, QH), bass.ds((j % 2) * 2 * GR + gg * GR, GR)]
                sp.dma_start(dst.rearrange("(n p) c -> p n c", p=P),
                             on[:, half, :, :, :].rearrange("p n h d -> p n (h d)")).then_inc(o_out[half], 16)

            load(0, 0)
            load_v(0, 0, 0)
            rows(28, 0, 0)

            def body(j):
                for gg in range(2):
                    g = j * 2 + gg
                    need(sp, st_ok, g * 64)
                    load(1 - gg, (g + 1) % NG)
                    need(sp, pv_ok, g * QUADS)
                    if gg == 0:
                        load_v(1, j, 1)
                    else:
                        load_v(0, (j + 1) % (NG // 2), 0)
                    if gg == 1:
                        store(place(g, 2, 2), 1, j, 0)
                    elif not (isinstance(j, int) and j == 0):
                        store(place(g, 2, 2), 1, j - 1, 1)
                    rows(place(g, 3, 2), 1, gg)
                    store(place(g, 10, 2), 0, j, gg)
                    rows(place(g, 11, 2), 0, 1 - gg)

            rounds(sp, NG // 2, body)
            store(FIRST + NG * PER, 1, NG // 2 - 1, 1)
            for i in range(2):
                sp.wait_ge(o_out[i], 16 * NG)
            sp.wait_ge(mrow_in[0], 16 * (NG + 1))

        @block.gpsimd
        def _(pool):
            own = Chain(pool, pool_own, passed)
            own.link(nc.gpsimd.memset(ident[:], 0.0))
            nc.gpsimd.affine_select(out=ident[:], in_=ident[:], compare_op=ALU.not_equal, fill=1.0, base=0,
                                    pattern=[[-1, P]], channel_multiplier=1).then_inc(id_ok, 1)
            own.link(nc.gpsimd.memset(identb[:], 0.0))
            nc.gpsimd.affine_select(out=identb[:], in_=identb[:], compare_op=ALU.not_equal, fill=1.0, base=0,
                                    pattern=[[-1, P]], channel_multiplier=1).then_inc(id_ok, 1)
            start = own.n

            def split(n, half, last_use):
                own.base, own.n = start + n * 4, 0
                wait_alone(pool, mx_free, last_use + 1, passed)
                own.link(nc.gpsimd.tensor_scalar(mp[:, half, 0, :], mx[:, half, :], -1.0, 0.0, ALU.mult, ALU.add))
                own.link(nc.gpsimd.tensor_tensor(mrest[:], mx[:, half, :], mp[:, half, 0, :], ALU.add))
                own.link(nc.gpsimd.tensor_scalar(mp[:, half, 1, :], mrest[:], -1.0, 0.0, ALU.mult, ALU.add))
                own.link(nc.gpsimd.tensor_tensor(mrest[:], mrest[:], mp[:, half, 1, :], ALU.add))
                nc.gpsimd.tensor_scalar(mp[:, half, 2, :], mrest[:], -1.0, 0.0, ALU.mult, ALU.add).then_inc(mp_ok, 1)

            split(0, 0, 15)

            def body(j):
                for gg in range(2):
                    g = j * 2 + gg
                    split(2 * g + 1, 1, place(g, 1, 1))
                    split(2 * g + 2, 0, place(g, 9, 1))
            rounds(pool, NG // 2, body)

        @block.scalar
        def _(act):
            def body(j):
                for gg in range(2):
                    g = j * 2 + gg
                    for k in range(QUADS):
                        q = g * QUADS + k
                        need(act, pv_ok, q - 1)
                        for i in range(4):
                            act.wait_ge(st_ok, q * 4 + i + 1)
                            nc.scalar.activation(pr[:, (k % 2) * 4 + i, :], pst[i % 2][:, :], ACT.Exp, scale=SCALE)\
                                .then_inc(exp_ok, 1)
                            if k % 8 == 1 and i == 1:
                                u = 2 * g + k // 8 - 1
                                if not (isinstance(u, int) and u < 0):
                                    take_o(u, (k // 8 + 1) % 2)

            def take_o(u, half):
                act.wait_ge(pv_ok, 8 * (u + 1))
                nc.scalar.activation(osb[:, :], po[half][:, :], ACT.Copy).then_inc(osb_ok, 1)

            act.wait_ge(po_ok, 1)
            rounds(act, NG // 2, body)
            take_o(2 * NG - 1, 1)

        @block.vector
        def _(dve):
            for i in range(2):
                nc.vector.memset(kt[i][KR:KR + MR, :, :], 1.0).then_inc(row1_ok, 1)
            nc.vector.memset(po[0][:, :], 0.0)
            nc.vector.memset(po[1][:, :], 0.0).then_inc(po_ok, 1)

            def maximum(use, slot, half, col):
                dve.wait_ge(mx_full, use + 1)
                nc.vector.tensor_reduce(mx[:, half, col:col + 1], pm[slot][:, :, :].rearrange("p a n -> p (a n)"),
                                        AX.X, ALU.max).then_inc(mx_free, 1)

            def maxrows(use, slot, half, sent):
                dve.wait_ge(mx_full, use + 1)
                need(dve, mrow_in[half], 16 * sent)
                nc.vector.tensor_copy(mrow[:, half, :], pm[slot][0:48, 0, 0:P]).then_inc(mx_free, 1)

            def normalise(use, slot, half, u, outs):
                dve.wait_ge(mx_full, use + 1)
                o = pm[slot][:, 0, :].rearrange("p (m w) -> p m w", w=32)
                nc.vector.reciprocal(rec[:].unsqueeze(2), o[:, :, D:VW]).then_inc(rec_ok, 1)
                dve.wait_ge(rec_ok, u + 1)
                need(dve, o_out[half], outs * 16)
                nc.vector.tensor_tensor(on[:, half, :, :, :].rearrange("p n h d -> p (n h) d"), o[:, :, 0:D],
                                        rec[:].unsqueeze(2).to_broadcast([P, 16, D]), ALU.mult).then_inc(mx_free, 1)

            for n in range(28):
                maximum(n, n % 2, n // 16, n % 16)
                if n == 27:
                    maxrows(28, 0, 0, 0)

            def body(j):
                for gg in range(2):
                    g = j * 2 + gg
                    for k in range(QUADS):
                        if k in (2, 10):
                            need(dve, mp_ok, 2 * g + 1 + k // 8)
                        for i, what in enumerate(uses(k)):
                            use = place(g, k, i)
                            slot = (FIRST + before[k] + i) % 2
                            if what == "out":
                                u = 2 * g + k // 8 - 1
                                half = (k // 8 + 1) % 2
                                if isinstance(u, int) and u < 0:
                                    dve.wait_ge(mx_full, use + 1)
                                    nc.vector.memset(rec[:], 1.0).then_inc(mx_free, 1)
                                    continue
                                normalise(use, slot, half, u, g - (1 if half else 0))
                            elif what == "rows":
                                half = 1 if k == 3 else 0
                                maxrows(use, slot, half, g if half else g + 1)
                            else:
                                maximum(use, slot, what // 16, what % 16)
            rounds(dve, NG // 2, body)
            normalise(FIRST + NG * PER, (FIRST + NG * PER) % 2, 1, 2 * NG - 1, NG - 1)

        @block.tensor
        def _(pe):
            def scores_max(buf, task, slot, use):
                half, h, qi = task // 16, task % 16 // 4, task % 4
                need(pe, mx_free, use - 1)
                for kk in range(2):
                    mm = pe.matmul(pm[slot][:, kk, :], qt[buf][0:KR, half, h, qi * P:(qi + 1) * P],
                                   kt[buf][0:KR, h, kk * 512:(kk + 1) * 512], start=True, stop=True)
                mm.then_inc(mx_full, 1)

            def turn_rows(slot, use, half, n):
                need(pe, mx_free, use - 1)
                pe.wait_ge(mp_ok, n + 1)
                pe.matmul(pm[slot][0:48, 0, 0:P], mp[:, half, :, :].rearrange("p a c -> p (a c)"), identb[:],
                          start=True, stop=True).then_inc(mx_full, 1)

            def turn_out(slot, use, u):
                need(pe, mx_free, use - 1)
                pe.wait_ge(osb_ok, u + 1)
                for n in range(4):
                    mm = pe.transpose(pm[slot][:, 0, n * P:(n + 1) * P], osb[:, n * P:(n + 1) * P], ident[:])
                mm.then_inc(mx_full, 1)

            def scores(buf, half, kc, h, s):
                need(pe, exp_ok, s - 1)
                pe.matmul(pst[h % 2][:, :], kt[buf][0:KR + MR, h, kc * P:(kc + 1) * P],
                          qt[buf][0:KR + MR, half, h, :], start=True, stop=True)\
                    .then_inc(st_ok, 1)

            def pv(buf, k, q, u):
                pe.wait_ge(exp_ok, 4 * (q + 1))
                if k % 8 == 0:
                    need(pe, osb_ok, u - 1)
                for h in range(HG):
                    mm = pe.matmul(po[k // 8][32 * h:32 * h + VW, :], vt[buf][:, k % 8, h * VW:(h + 1) * VW],
                                   pr[:, (k % 2) * 4 + h, :], start=(k % 8 == 0), stop=(k % 8 == 7),
                                   tile_position=(0, 32 * h))
                mm.then_inc(pv_ok, 1)

            pe.wait_ge(id_ok, 2)
            pe.wait_ge(row1_ok, 2)
            pe.wait_ge(qk_in[0], LOAD)
            for n in range(28):
                scores_max(0, n, n % 2, n)
            turn_rows(0, 28, 0, 0)
            pe.wait_ge(po_ok, 1)

            def body(j):
                for gg in range(2):
                    g = j * 2 + gg
                    for k in range(QUADS):
                        q = g * QUADS + k
                        half, kc = k // 8, k % 8
                        if k == 0:
                            pe.wait_ge(mrow_in[0], 16 * (g + 1))
                            pe.wait_ge(v_in[gg], 16 * (j + 1))
                        if k == 8:
                            pe.wait_ge(mrow_in[1], 16 * (g + 1))
                        if k == 2:
                            pe.wait_ge(qk_in[1 - gg], LOAD * (j + 1 + gg))
                        mbuf = gg if k < 2 else 1 - gg
                        us = uses(k)
                        slots = [(FIRST + before[k] + i) % 2 for i in range(len(us))]
                        scores(gg, half, kc, 0, 4 * q)
                        scores_max(mbuf, us[0], slots[0], place(g, k, 0))
                        scores(gg, half, kc, 1, 4 * q + 1)
                        scores(gg, half, kc, 2, 4 * q + 2)
                        scores_max(mbuf, us[1], slots[1], place(g, k, 1))
                        scores(gg, half, kc, 3, 4 * q + 3)
                        if not (isinstance(q, int) and q == 0):
                            pb, pk = (gg, k - 1) if k else (1 - gg, QUADS - 1)
                            pv(pb, pk, q - 1, 2 * g + pk // 8 if k else 2 * g - 1)
                        if len(us) == 3:
                            if us[2] == "out":
                                u = 2 * g + k // 8 - 1
                                if isinstance(u, int) and u < 0:
                                    need(pe, mx_free, place(g, k, 2) - 1)
                                    pe.matmul(pm[slots[2]][:, 0, 0:P], identb[:], identb[:], start=True,
                                              stop=True).then_inc(mx_full, 1)
                                else:
                                    turn_out(slots[2], place(g, k, 2), u)
                            else:
                                turn_rows(slots[2], place(g, k, 2), 1 if k == 3 else 0,
                                          2 * g + (1 if k == 3 else 2))
            rounds(pe, NG // 2, body)
            pv(1, QUADS - 1, NG * QUADS - 1, 2 * NG - 1)
            end = FIRST + NG * PER
            turn_out(end % 2, end, 2 * NG - 1)


def stage_c(nc, x, w13, w2, w_out, b_out, s_xn, s_o, comb, out):
    NE = E + NS
    with ExitStack() as ctx:
        sb = lambda n, s, d=F32: ctx.enter_context(nc.sbuf_tensor(n, s, d))
        ps = lambda n, s: ctx.enter_context(nc.psum_tensor(n, s, F32))
        sem = lambda n: ctx.enter_context(nc.semaphore(n))
        w13s = sb("w13s", [P, CC, NE, 2 * F])
        w2s = sb("w2s", [P, NE, C])
        wos = sb("wos", [P, CC, C])
        bos = sb("bos", [P, C])
        xr = sb("xr", [P, 2, C])
        xo = sb("xo", [P, 2, 2, C])
        xot = sb("xot", [P, 2, 4, P])
        xb = sb("xb", [P, 2, C])
        sg = sb("sg", [P, 2, F])
        hb = sb("hb", [P, 2, F])
        ht = sb("ht", [P, 2, P])
        ys = sb("ys", [P, 2, C])
        ident = sb("ident_c", [P, P])
        pt = [ps(f"pt{i}", [P, 512]) for i in range(2)]
        pg = [ps(f"pg{i}", [P, 512]) for i in range(2)]
        ph = [ps(f"ph{i}", [P, 512]) for i in range(2)]
        pa = [ps(f"pa{i}", [P, 512]) for i in range(2)]
        id_ok, w_in = sem("idc_ok"), sem("wc_in")
        in_ok = [sem(f"in_ok{i}") for i in range(2)]
        y_out = [sem(f"y_out{i}") for i in range(2)]
        pt_ok, xot_ok, xb_ok = sem("pt_ok"), sem("xot_ok"), sem("xb_ok")
        gu_ok, sg_ok, hb_ok, hT_ok, ht_ok, w2_ok = (sem(n) for n in ("gu_ok", "sg_ok", "hb_ok", "hT_ok", "ht_ok", "w2_ok"))
        y_ok, pool_own = sem("y_ok"), sem("pool_own_c")
        block = ctx.enter_context(nc.Block())

        xd = x.rearrange("b t c -> (b t) c")
        od = out.rearrange("b t c -> (b t) c")

        @block.sync
        def _(sp):
            sp.dma_start(w13s[:], w13.rearrange("(c p) e n -> p c e n", p=P)).then_inc(w_in, 16)
            sp.dma_start(w2s[:], w2).then_inc(w_in, 16)
            sp.dma_start(wos[:], w_out.rearrange("(c p) n -> p c n", p=P)).then_inc(w_in, 16)
            sp.dma_start(bos[:], b_out.rearrange("(a c) -> a c", a=1).to_broadcast([P, C])).then_inc(w_in, 16)

            def body(j):
                for a in range(2):
                    t = 2 * j + a
                    need(sp, pt_ok, t - 1)
                    need(sp, xb_ok, t - 1)
                    row = t * P
                    sp.dma_start(xr[:, a, :], xd[bass.ds(row, P), :]).then_inc(in_ok[a], 16)
                    sp.dma_start(xo[:, a, 0, :], s_xn[bass.ds(row, P), :]).then_inc(in_ok[a], 16)
                    sp.dma_start(xo[:, a, 1, :], s_o[bass.ds(row, P), :]).then_inc(in_ok[a], 16)
                    if not (isinstance(t, int) and t == 0):
                        store(t - 1, 1 - a)

            def store(t, a):
                sp.wait_ge(y_ok, t + 1)
                sp.dma_start(od[bass.ds(t * P, P), :], ys[:, a, :]).then_inc(y_out[a], 16)

            rounds(sp, NT // 2, body)
            store(NT - 1, 1)
            for a in range(2):
                sp.wait_ge(y_out[a], 16 * NT // 2)

        @block.gpsimd
        def _(pool):
            own = Chain(pool, pool_own)
            own.link(nc.gpsimd.memset(ident[:], 0.0))
            nc.gpsimd.affine_select(out=ident[:], in_=ident[:], compare_op=ALU.not_equal, fill=1.0, base=0,
                                    pattern=[[-1, P]], channel_multiplier=1).then_inc(id_ok, 1)
            pool.wait_ge(w_in, 64)

            def body(j):
                for a in range(2):
                    t = 2 * j + a
                    pool.wait_ge(in_ok[a], 48 * (j + 1))
                    need(pool, y_ok, t - 1)
                    nc.gpsimd.tensor_tensor(xb[:, a, :], xr[:, a, :], bos[:], ALU.add).then_inc(xb_ok, 1)
            rounds(pool, NT // 2, body)

        @block.scalar
        def _(act):
            def body(j):
                for a in range(2):
                    t = 2 * j + a
                    act.wait_ge(pt_ok, t + 1)
                    need(act, w2_ok, (t - 1) * NE)
                    nc.scalar.activation(xot[:, a, :, :], pt[a][:, :].rearrange("p (k n) -> p k n", k=4), ACT.Copy)\
                        .then_inc(xot_ok, 1)
                    for s in range(NE + 1):
                        if s < NE:
                            n = t * NE + s
                            act.wait_ge(gu_ok, n + 1)
                            need(act, hb_ok, n - 1)
                            nc.scalar.activation(sg[:, s % 2, :], pg[s % 2][:, 0:F], ACT.Silu).then_inc(sg_ok, 1)
                        if s >= 1:
                            n = t * NE + s - 1
                            act.wait_ge(hT_ok, n + 1)
                            need(act, w2_ok, n - 1)
                            nc.scalar.activation(ht[:, (s - 1) % 2, :], ph[(s - 1) % 2][:, 0:P], ACT.Copy)\
                                .then_inc(ht_ok, 1)
            rounds(act, NT // 2, body)

        @block.vector
        def _(dve):
            def body(j):
                for a in range(2):
                    t = 2 * j + a
                    for s in range(NE):
                        n = t * NE + s
                        dve.wait_ge(sg_ok, n + 1)
                        need(dve, hT_ok, n - 1)
                        w = comb[:, bass.ds(t, 1), s:s + 1].rearrange("p a b -> p (a b)")
                        nc.vector.scalar_tensor_tensor(out=hb[:, s % 2, :], in0=pg[s % 2][:, F:2 * F], scalar=w,
                                                       in1=sg[:, s % 2, :], op0=ALU.mult, op1=ALU.mult)\
                            .then_inc(hb_ok, 1)
                    dve.wait_ge(w2_ok, (t + 1) * NE)
                    dve.wait_ge(xb_ok, t + 1)
                    need(dve, y_out[a], j * 16)
                    nc.vector.tensor_tensor(ys[:, a, :], pa[a][:, 0:C], xb[:, a, :], ALU.add).then_inc(y_ok, 1)
            rounds(dve, NT // 2, body)

        @block.tensor
        def _(pe):
            pe.wait_ge(id_ok, 1)
            pe.wait_ge(w_in, 64)

            def body(j):
                for a in range(2):
                    t = 2 * j + a
                    pe.wait_ge(in_ok[a], 48 * (j + 1))
                    need(pe, xot_ok, t - 1)
                    for k in range(4):
                        mm = pe.transpose(pt[a][:, k * P:(k + 1) * P], xo[:, a, k // 2, (k % 2) * P:(k % 2 + 1) * P],
                                          ident[:])
                    mm.then_inc(pt_ok, 1)
                    pe.wait_ge(xot_ok, t + 1)
                    need(pe, y_ok, t - 1)
                    for c in range(CC):
                        pe.matmul(pa[a][:, 0:C], xot[:, a, 2 + c, :], wos[:, c, :], start=(c == 0), stop=False)
                    for s in range(NE + 2):
                        if s < NE:
                            n = t * NE + s
                            need(pe, hb_ok, n - 1)
                            for c in range(CC):
                                mm = pe.matmul(pg[s % 2][:, 0:2 * F], xot[:, a, c, :], w13s[:, c, s, :],
                                               start=(c == 0), stop=(c == CC - 1))
                            mm.then_inc(gu_ok, 1)
                        if 1 <= s <= NE:
                            n = t * NE + s - 1
                            pe.wait_ge(hb_ok, n + 1)
                            need(pe, ht_ok, n - 1)
                            pe.transpose(ph[(s - 1) % 2][:, 0:P], hb[:, (s - 1) % 2, :], ident[:]).then_inc(hT_ok, 1)
                        if s >= 2:
                            n = t * NE + s - 2
                            pe.wait_ge(ht_ok, n + 1)
                            pe.matmul(pa[a][:, 0:C], ht[:, (s - 2) % 2, :], w2s[:, s - 2, :], start=False,
                                      stop=(s == NE + 1)).then_inc(w2_ok, 1)
            rounds(pe, NT // 2, body)


def program(nc, x, w_qkvg, b_qkv, rope, w13, w2, w_out, b_out, out):
    s_q = nc.dram_tensor("s_q", [2, 3, B * C, T], BF16).ap()
    s_v = nc.dram_tensor("s_v", [N, H, VW], F32).ap()
    s_xn = nc.dram_tensor("s_xn", [N, C], F32).ap()
    s_o = nc.dram_tensor("s_o", [N, C], F32).ap()
    with nc.sbuf_tensor("comb", [P, NT, E + NS], F32) as comb:
        stage_a(nc, x, w_qkvg, b_qkv, rope, s_q, s_v, s_xn, comb)
        stage_b(nc, s_q, s_v, s_o)
        stage_c(nc, x, w13, w2, w_out, b_out, s_xn, s_o, comb, out)


def rope_table():
    inv = (1.0 / ROPE_BASE ** (np.arange(0, D, 2, dtype=np.float32) / np.float32(D))).astype(np.float32)
    angle = (np.arange(T, dtype=np.float32)[:, None] * inv[None, :]).astype(np.float64)
    cos, sin = np.cos(angle), np.sin(angle)
    return np.stack([np.concatenate([cos, cos], 1), np.concatenate([-sin, sin], 1)], 1).astype(np.float32)


def kernel(L0_attn_x, L0_attn_W_qkv, L0_attn_b_qkv, L0_attn_W_out, L0_attn_b_out, L0_ffn_w_gate, L0_ffn_w1_e,
           L0_ffn_w3_e, L0_ffn_w2_e, L0_ffn_w1_s, L0_ffn_w3_s, L0_ffn_w2_s):
    import concourse.bacc as bacc
    from concourse.bass_utils import run_bass_kernel_spmd

    a = lambda v: np.ascontiguousarray(v)
    up = lambda e, s: np.concatenate([np.asarray(e), np.asarray(s).reshape(NS, F, C)], 0).transpose(2, 0, 1)
    arrays = {
        "x": a(L0_attn_x),
        "w_qkvg": a(np.concatenate([np.asarray(L0_attn_W_qkv), np.asarray(L0_ffn_w_gate).T], 1)),
        "b_qkv": a(L0_attn_b_qkv),
        "rope": rope_table(),
        "w13": a(np.concatenate([up(L0_ffn_w1_e, L0_ffn_w1_s), up(L0_ffn_w3_e, L0_ffn_w3_s)], 2)),
        "w2": a(np.concatenate([np.asarray(L0_ffn_w2_e).transpose(2, 0, 1),
                                np.asarray(L0_ffn_w2_s).reshape(C, NS, F).transpose(2, 1, 0)], 1)),
        "w_out": a(L0_attn_W_out),
        "b_out": a(L0_attn_b_out),
    }
    nc = bacc.Bacc("TRN2", target_bir_lowering=False, num_devices=1)
    aps = {n: nc.dram_tensor(n, v.shape, mybir.dt.from_np(v.dtype), kind="ExternalInput").ap()
           for n, v in arrays.items()}
    out = nc.dram_tensor("out", [B, T, C], F32, kind="ExternalOutput").ap()
    program(nc, **aps, out=out)
    return run_bass_kernel_spmd(nc, [arrays], core_ids=[0]).results[0]["out"]
```

```python
from contextlib import ExitStack

import numpy as np

import concourse.bass as bass
from concourse import mybir

F32 = mybir.dt.float32
BF16 = mybir.dt.bfloat16
I32, U32 = mybir.dt.int32, mybir.dt.uint32
ALU = mybir.AluOpType
ACT = mybir.ActivationFunctionType
AX = mybir.AxisListType

P = 128
B, T, C = 4, 1024, 256
N = B * T
H, D = 16, 16
NT = N // P
TPB = T // P
CC = C // P
E, F = 16, 128
NS = 2
G, TOPG, TOPK = 4, 2, 4
NX = N * TOPK // P + E
EPS = 1e-5
ROPE_BASE = 10000.0

HG = 4
NG = B * H // HG
GR = HG * D
QH = T // 2
VW = D + 1
Q_PART = [0, 0, 0, 1, 1, 2]
K_PART = [0, 1, 2, 0, 1, 0]
TERMS = len(Q_PART)
KR = TERMS * D
MR = 3
SCALE = D ** -0.5


def need(eng, sem, n):
    if isinstance(n, int) and n <= 0:
        return
    eng.wait_ge(sem, n)


def wait_alone(eng, sem, n, passed):
    eng.wait_ge(sem, n)
    eng.sem_inc(passed, 1)


class Chain:

    def __init__(self, eng, sem, passed=None):
        self.eng, self.sem, self.passed, self.base, self.n = eng, sem, passed, 0, 0

    def link(self, ins):
        self.n += 1
        ins.then_inc(self.sem, 1)
        self.follow(self.passed)

    def link_alone(self, ins, passed):
        self.n += 1
        ins.then_inc(self.sem, 1)
        self.follow(passed)

    def follow(self, passed):
        if passed is None:
            self.eng.wait_ge(self.sem, self.base + self.n)
        else:
            wait_alone(self.eng, self.sem, self.base + self.n, passed)


def rounds(eng, n, emit):
    emit(0)
    with eng.Fori(1, n) as j:
        emit(j)


def steps(eng, n, per, total, work):
    deepest = max(lag for lag, _ in work)

    def round_(j, count=per):
        for s in range(count):
            for lag, part in work:
                k = j * per + s - lag
                if isinstance(k, int) and not 0 <= k < total:
                    continue
                part(k, (s - lag) % per, j + (s - lag) // per)
    round_(0)
    with eng.Fori(1, n) as j:
        round_(j)
    round_(n, deepest)


def stage_a(nc, x, w_qkvg, b_qkv, rope, s_q, s_k, s_v, s_xn, keep):
    W = 3 * C + E
    with ExitStack() as ctx:
        sb = lambda n, s, d=F32: ctx.enter_context(nc.sbuf_tensor(n, s, d))
        ps = lambda n, s: ctx.enter_context(nc.psum_tensor(n, s, F32))
        sem = lambda n: ctx.enter_context(nc.semaphore(n))

        xs = sb("xs", [P, NT, C])
        wsb = sb("wsb", [P, CC, W])
        brow = sb("brow", [1, W])
        brest = sb("brest", [1, W])
        bparts = [sb(f"bpart{n}", [1, W], BF16) for n in range(3)]
        bias3 = sb("bias3", [3, W], BF16)
        ones3 = sb("ones3", [3, P], BF16)
        ropesb = sb("ropesb", [P, TPB, 2, D])
        ident = sb("ident_a", [P, P])
        ones = sb("ones_a", [P, P], BF16)
        below = sb("below", [P, P], BF16)
        bnst = sb("bnst", [P, TPB, 6])
        mv = sb("mv", [P, NT, 2])
        var = sb("var", [P, NT])
        std = sb("std", [P, NT])
        rstd = sb("rstd", [P, NT])
        nwt = sb("nwt", [P, NT])
        xn = sb("xn_a", [P, 2, C])
        xt = sb("xt_a", [P, 2, CC, P])
        qks = sb("qks", [P, 2, 2 * C])
        rc = sb("rc", [P, 2, 2 * C])
        rs = sb("rs", [P, 2, 2 * C])
        qr = sb("qr", [P, 2, 2 * C])
        r1 = sb("r1", [P, 2, 4, P])
        stg = sb("stg", [P, 2, 3, 4, 4 * P], BF16)
        vst = sb("vst", [P, 2, H, VW])
        lg = sb("lg", [P, NT, E])
        gb = {n: sb("g_" + n, sh) for n, sh in dict(
            ex=[P, TPB, E], sc=[P, TPB, E], hi=[P, TPB * G, 2], lo=[P, TPB * G, 2], m1=[P, TPB * G],
            m2=[P, TPB * G], gs=[P, TPB, G], gt=[P, TPB, G, G], ge=[P, TPB, G, G], lt4=[P, G, G],
            rank=[P, TPB, G], ok=[P, TPB, G], ms=[P, TPB, E], top=[P, TPB, 8], a=[P, TPB, E], bq=[P, TPB, E],
            c=[P, TPB, E], ex2=[P, TPB, E], cnt=[P, TPB], ws=[P, TPB], kth=[P, TOPK], mw=[P, TPB, TOPK, E]).items()}
        cnt = sb("cnt", [P, E], BF16)

        pT = [ps(f"pT{i}", [P, 512]) for i in range(2)]
        pQ = [ps(f"pQ{i}", [P, 512]) for i in range(2)]
        pV = [ps(f"pV{i}", [P, 512]) for i in range(2)]
        pR = [ps(f"pR{i}", [P, 512]) for i in range(2)]

        x_in = [sem(f"x_in{b}") for b in range(B)]
        w_in, c_in, b_in, b3_in = sem("w_in"), sem("c_in"), sem("b_in"), sem("b3_in")
        id_ok, ones_ok, bp_ok, mats_ok = sem("id_ok"), sem("ones_ok"), sem("bp_ok"), sem("mats_ok")
        dve_own, pool_own = sem("dve_own_a"), sem("pool_own_a")
        var_ok, std_ok = sem("var_ok"), sem("std_ok")
        xn_ok, xT_ok, xt_ok = sem("xn_ok"), sem("xT_ok"), sem("xt_ok")
        qk_ok, qks_ok, vg_ok, vs_ok = sem("qk_ok"), sem("qks_ok"), sem("vg_ok"), sem("vs_ok")
        rc_ok, rs_ok, qr_ok, qrT_ok = sem("rc_ok"), sem("rs_ok"), sem("qr_ok"), sem("qrT_ok")
        p1_ok, r1_ok, p2_ok, p3_ok = sem("p1_ok"), sem("r1_ok"), sem("p2_ok"), sem("p3_ok")
        st_out = [sem(f"st_out{i}") for i in range(2)]
        v_out = [sem(f"v_out{i}") for i in range(2)]
        xn_out = [sem(f"xn_out{i}") for i in range(2)]
        lg_ok, ex_ok, ex_used = sem("lg_ok"), sem("ex_ok"), sem("ex_used")
        sel_ok, cnt_ok, pre_ok, keep_ok = sem("sel_ok"), sem("cnt_ok"), sem("pre_ok"), sem("keep_ok")
        passed, passed_dve = sem("passed_a"), sem("passed_dve_a")
        block = ctx.enter_context(nc.Block())

        x_tiles = x.rearrange("b (n p) c -> b p n c", p=P)

        TURN, PROJ, BACK, SPLIT = 1, 2, 4, 5

        @block.sync
        def _(sp):
            sp.dma_start(xs[:, 0:TPB, :], x_tiles[0]).then_inc(x_in[0], 16)
            sp.dma_start(brow[:, 0:3 * C], b_qkv.rearrange("(a c) -> a c", a=1)).then_inc(b_in, 16)
            sp.dma_start(wsb[:], w_qkvg.rearrange("(c p) n -> p c n", p=P)).then_inc(w_in, 16)
            for b in range(1, B):
                sp.dma_start(xs[:, b * TPB:(b + 1) * TPB, :], x_tiles[b]).then_inc(x_in[b], 16)
            sp.dma_start(ropesb[:], rope.rearrange("(n p) a d -> p n a d", p=P)).then_inc(c_in, 16)
            sp.wait_ge(bp_ok, 3)
            for n in range(3):
                sp.dma_start(bias3[n:n + 1, :], bparts[n][:]).then_inc(b3_in, 16)

            def store_xn(k, t, b):
                sp.wait_ge(xn_ok, k + 1)
                sp.dma_start(s_xn[bass.ds(k * P, P), :], xn[:, t % 2, :]).then_inc(xn_out[t % 2], 16)

            def store_v(k, t, b):
                sp.wait_ge(vs_ok, k + 1)
                sp.dma_start(s_v[bass.ds(k * P, P), :, :], vst[:, t % 2, :, :]).then_inc(v_out[t % 2], 16)

            def store_parts(k, t, b):
                if t % 4 != 3:
                    return
                hh = t // 4
                sp.wait_ge(p3_ok, k + 1)
                sp.wait_ge(p2_ok, k + 1)
                for part in range(3):
                    for blk in range(4):
                        heads = slice((blk % 2) * H // 2, (blk % 2 + 1) * H // 2)
                        if blk < 2:
                            dst = s_q[hh, bass.ds(b, 1), part, :, heads, :]
                        else:
                            dst = s_k[bass.ds(b, 1), part, :, heads, hh * QH:(hh + 1) * QH]
                        sp.dma_start(dst.rearrange("b d h t -> (b h) d t"), stg[:, hh, part, blk, :])\
                            .then_inc(st_out[hh], 16)

            steps(sp, B, TPB, NT, [(0, store_xn), (PROJ, store_v), (SPLIT, store_parts)])
            for i in range(2):
                sp.wait_ge(st_out[i], 12 * 16 * B)
                sp.wait_ge(v_out[i], 16 * NT // 2)
                sp.wait_ge(xn_out[i], 16 * NT // 2)

        @block.gpsimd
        def _(pool):
            own = Chain(pool, pool_own)
            own.link(nc.gpsimd.memset(ident[:], 0.0))
            nc.gpsimd.affine_select(out=ident[:], in_=ident[:], compare_op=ALU.not_equal, fill=1.0, base=0,
                                    pattern=[[-1, P]], channel_multiplier=1).then_inc(id_ok, 1)
            nc.gpsimd.memset(ones3[:], 1.0).then_inc(ones_ok, 1)
            nc.gpsimd.memset(vst[:], 1.0).then_inc(ones_ok, 1)
            own.link(nc.gpsimd.memset(brow[:, 3 * C:W], 0.0))
            pool.wait_ge(b_in, 16)
            nc.gpsimd.tensor_copy(bparts[0][:], brow[:]).then_inc(bp_ok, 1)
            pool.wait_ge(bp_ok, 1)
            own.link(nc.gpsimd.tensor_tensor(brest[:], brow[:], bparts[0][:], ALU.subtract))
            nc.gpsimd.tensor_copy(bparts[1][:], brest[:]).then_inc(bp_ok, 1)
            pool.wait_ge(bp_ok, 2)
            nc.gpsimd.tensor_tensor(bparts[2][:], brest[:], bparts[1][:], ALU.subtract).then_inc(bp_ok, 1)
            nc.gpsimd.memset(ones[:], 1.0).then_inc(mats_ok, 1)
            own.link(nc.gpsimd.memset(below[:], 1.0))
            nc.gpsimd.affine_select(out=below[:], in_=below[:], compare_op=ALU.is_gt, fill=0.0, base=0,
                                    pattern=[[1, P]], channel_multiplier=-1).then_inc(mats_ok, 1)
            pool.wait_ge(c_in, 16)

            def sines(k, t, b):
                sl = t % 2
                pool.wait_ge(qks_ok, k + 1)
                need(pool, qr_ok, k - 1)
                src = qks[:, sl, :].rearrange("p (h d) -> p h d", d=D)
                dst = rs[:, sl, :].rearrange("p (h d) -> p h d", d=D)
                sn = ropesb[:, t, 1:2, :]
                hd = D // 2
                nc.gpsimd.tensor_tensor(dst[:, :, 0:hd], src[:, :, hd:D],
                                        sn[:, :, 0:hd].to_broadcast([P, 2 * H, hd]), ALU.mult)
                nc.gpsimd.tensor_tensor(dst[:, :, hd:D], src[:, :, 0:hd],
                                        sn[:, :, hd:D].to_broadcast([P, 2 * H, hd]), ALU.mult).then_inc(rs_ok, 1)

            def part3(k, t, b):
                sl, hh, c0 = t % 2, t // 4, (t % 4) * P
                pool.wait_ge(p2_ok, k + 1)
                nc.gpsimd.tensor_tensor(stg[:, hh, 2, :, c0:c0 + P], r1[:, sl, :, :],
                                        stg[:, hh, 1, :, c0:c0 + P], ALU.subtract).then_inc(p3_ok, 1)

            steps(pool, B, TPB, NT, [(PROJ, sines), (SPLIT, part3)])

        @block.vector
        def _(dve):
            own = Chain(dve, dve_own)
            v = nc.vector
            for b in range(B):
                dve.wait_ge(x_in[b], 16)
                for t in range(TPB):
                    last = v.bn_stats(bnst[:, t, :], xs[:, b * TPB + t, :])
                own.link(last)
                for t in range(TPB):
                    last = v.bn_aggr(mv[:, b * TPB + t, :], bnst[:, t, :])
                own.link(last)
            own.link(v.tensor_scalar(var[:], mv[:, :, 1], EPS, None, ALU.add))
            v.tensor_copy(nwt[:], var[:]).then_inc(var_ok, 1)
            dve.wait_ge(std_ok, 1)
            own.link(v.reciprocal(rstd[:], std[:]))
            own.link(v.tensor_tensor(nwt[:], rstd[:], rstd[:], ALU.mult))
            own.link(v.tensor_tensor(nwt[:], nwt[:], var[:], ALU.mult))
            own.link(v.tensor_scalar(nwt[:], nwt[:], -0.5, 1.5, ALU.mult, ALU.add))
            own.link(v.tensor_tensor(rstd[:], rstd[:], nwt[:], ALU.mult))
            own.link(v.memset(gb["lt4"][:], 0.0))
            for g in range(1, G):
                own.link(v.memset(gb["lt4"][:, g, 0:g], 1.0))
            for n in range(TOPK):
                own.link(v.memset(gb["kth"][:, n:n + 1], n + 1.0))
            dve.wait_ge(c_in, 16)
            setup = own.n

            def normalise(k, t, b):
                need(dve, xT_ok, k - 1)
                need(dve, xn_out[t % 2], (b * TPB // 2 + t // 2) * 16)
                pick = lambda a: a.rearrange("p a b -> p (a b)")
                v.tensor_scalar(xn[:, t % 2, :], pick(xs[:, bass.ds(k, 1), :]),
                                pick(mv[:, bass.ds(k, 1), 0:1]), rstd[:, bass.ds(k, 1)],
                                ALU.subtract, ALU.mult).then_inc(xn_ok, 1)

            def rotate(k, t, b):
                dve.wait_ge(qks_ok, k + 1)
                q3 = qks[:, t % 2, :].rearrange("p (h d) -> p h d", d=D)
                o3 = rc[:, t % 2, :].rearrange("p (h d) -> p h d", d=D)
                v.tensor_tensor(o3, q3, ropesb[:, t, 0:1, :].to_broadcast([P, 2 * H, D]), ALU.mult)\
                    .then_inc(rc_ok, 1)
                dve.wait_ge(rc_ok, k + 1)
                dve.wait_ge(rs_ok, k + 1)
                need(dve, qrT_ok, k - 1)
                v.tensor_tensor(qr[:, t % 2, :], rc[:, t % 2, :], rs[:, t % 2, :], ALU.add).then_inc(qr_ok, 1)

            def rest(k, t, b):
                dve.wait_ge(p1_ok, k + 1)
                need(dve, p3_ok, k - 1)
                need(dve, p2_ok, k - 1)
                c0 = (t % 4) * P
                v.tensor_tensor(r1[:, t % 2, :, :], pR[t % 2][:, :].rearrange("p (k n) -> p k n", k=4),
                                stg[:, t // 4, 0, :, c0:c0 + P], ALU.subtract).then_inc(r1_ok, 1)

            def routing(k, t, b):
                if t == 2:
                    own.base, own.n = setup + b * ROUTE_LINKS, 0
                for piece in {2: (0, 1), 3: (2,), 4: (3,), 5: (4, 5), 6: (6,), 7: (7,)}.get(t, ()):
                    route(nc, dve, own, gb, keep, b, piece, ex_ok, ex_used, sel_ok, passed_dve)
                assert t != TPB - 1 or own.n == ROUTE_LINKS, own.n

            steps(dve, B, TPB, NT, [(0, normalise), (BACK, rest), (PROJ, rotate), (TPB, routing)])
            own.base, own.n = setup + B * ROUTE_LINKS, 0
            dve.wait_ge(sel_ok, B)
            own.link(v.tensor_reduce(keep["cntf"][:], keep["sel"][:].rearrange("p n e -> p e n"), AX.X, ALU.add))
            v.tensor_copy(cnt[:], keep["cntf"][:]).then_inc(cnt_ok, 1)

        @block.scalar
        def _(act):
            act.wait_ge(ones_ok, 2)
            act.wait_ge(var_ok, 1)
            nc.scalar.activation(std[:], var[:], ACT.Sqrt).then_inc(std_ok, 1)

            def turn(k, t, b):
                act.wait_ge(xT_ok, k + 1)
                need(act, vg_ok, k - 1)
                nc.scalar.activation(xt[:, t % 2, :, :], pT[t % 2][:, 0:C].rearrange("p (c n) -> p c n", c=CC),
                                     ACT.Copy).then_inc(xt_ok, 1)

            def take(k, t, b):
                act.wait_ge(qk_ok, k + 1)
                need(act, qr_ok, k - 1)
                nc.scalar.activation(qks[:, t % 2, :], pQ[t % 2][:, :], ACT.Copy).then_inc(qks_ok, 1)
                act.wait_ge(vg_ok, k + 1)
                need(act, v_out[t % 2], (b * TPB // 2 + t // 2) * 16)
                nc.scalar.activation(vst[:, t % 2, :, 0:D],
                                     pV[t % 2][:, 0:C].rearrange("p (h d) -> p h d", d=D), ACT.Copy)\
                    .then_inc(vs_ok, 1)
                nc.scalar.activation(lg[:, bass.ds(k, 1), :], pV[t % 2][:, C:C + E].unsqueeze(1), ACT.Copy)\
                    .then_inc(lg_ok, 1)
                if t == TPB - 1:
                    act.wait_ge(lg_ok, k + 1)
                    need(act, ex_used, b)
                    nc.scalar.activation(gb["ex"][:], lg[:, bass.ds(b * TPB, TPB), :], ACT.Exp, scale=-1.0)\
                        .then_inc(ex_ok, 1)

            def part1(k, t, b):
                act.wait_ge(qrT_ok, k + 1)
                if t % 4 == 0:
                    need(act, st_out[t // 4], b * 12 * 16)
                c0 = (t % 4) * P
                nc.scalar.activation(stg[:, t // 4, 0, :, c0:c0 + P],
                                     pR[t % 2][:, :].rearrange("p (k n) -> p k n", k=4), ACT.Copy)\
                    .then_inc(p1_ok, 1)

            def part2(k, t, b):
                act.wait_ge(r1_ok, k + 1)
                c0 = (t % 4) * P
                nc.scalar.activation(stg[:, t // 4, 1, :, c0:c0 + P], r1[:, t % 2, :, :], ACT.Copy).then_inc(p2_ok, 1)

            steps(act, B, TPB, NT, [(BACK, part1), (TURN, turn), (SPLIT, part2), (PROJ, take)])
            act.wait_ge(pre_ok, 2)
            nc.scalar.activation(keep["pre"][:].rearrange("p n e -> p (n e)"), pQ[0][:, :], ACT.Copy)
            nc.scalar.activation(keep["tot"][:], pQ[1][:, 0:E], ACT.Copy).then_inc(keep_ok, 1)

        @block.tensor
        def _(pe):
            pe.wait_ge(id_ok, 1)
            pe.wait_ge(ones_ok, 1)
            pe.wait_ge(w_in, 16)
            pe.wait_ge(b3_in, 48)

            def turn(k, t, b):
                pe.wait_ge(xn_ok, k + 1)
                need(pe, xt_ok, k - 1)
                for c in range(CC):
                    mm = pe.transpose(pT[t % 2][:, c * P:(c + 1) * P], xn[:, t % 2, c * P:(c + 1) * P], ident[:])
                mm.then_inc(xT_ok, 1)

            def project(k, t, b):
                pe.wait_ge(xt_ok, k + 1)
                need(pe, qks_ok, k - 1)
                pe.matmul(pQ[t % 2][:, :], ones3[:], bias3[:, 0:2 * C], start=True, stop=False)
                for c in range(CC):
                    mm = pe.matmul(pQ[t % 2][:, :], xt[:, t % 2, c, :], wsb[:, c, 0:2 * C],
                                   start=False, stop=(c == CC - 1))
                mm.then_inc(qk_ok, 1)
                need(pe, lg_ok, k - 1)
                pe.matmul(pV[t % 2][:, 0:C + E], ones3[:], bias3[:, 2 * C:W], start=True, stop=False)
                for c in range(CC):
                    mm = pe.matmul(pV[t % 2][:, 0:C + E], xt[:, t % 2, c, :], wsb[:, c, 2 * C:W],
                                   start=False, stop=(c == CC - 1))
                mm.then_inc(vg_ok, 1)

            def back(k, t, b):
                pe.wait_ge(qr_ok, k + 1)
                need(pe, r1_ok, k - 1)
                for blk in range(4):
                    mm = pe.transpose(pR[t % 2][:, blk * P:(blk + 1) * P], qr[:, t % 2, blk * P:(blk + 1) * P],
                                      ident[:])
                mm.then_inc(qrT_ok, 1)

            steps(pe, B, TPB, NT, [(BACK, back), (TURN, turn), (PROJ, project)])
            pe.wait_ge(mats_ok, 2)
            pe.wait_ge(sel_ok, B)
            pe.wait_ge(qks_ok, NT)
            sel, pre = keep["sel"], pQ[0][:, :].rearrange("p (n e) -> p n e", e=E)
            pe.matmul(pre, below[:], sel[:], start=True, stop=True)
            for n in range(NT - 1):
                rest_n = NT - 1 - n
                mm = pe.matmul(pre[:, n + 1:NT, :], ones[:], sel[:, n:n + 1, :].to_broadcast([P, rest_n, E]),
                               start=False, stop=True, skip_group_check=True)
            mm.then_inc(pre_ok, 1)
            pe.wait_ge(cnt_ok, 1)
            pe.matmul(pQ[1][:, 0:E], ones[:], cnt[:], start=True, stop=True).then_inc(pre_ok, 1)


ROUTE_LINKS = 51


def route(nc, dve, own, gb, keep, b, piece, ex_ok, ex_used, sel_ok, passed):
    v = nc.vector
    tt = lambda o, x, y, op: own.link(v.tensor_tensor(o, x, y, op))
    bc = lambda a, shape: a.to_broadcast(shape)
    hi, lo, gs = gb["hi"], gb["lo"], gb["gs"]
    rows = bass.ds(b * TPB, TPB)
    if piece == 0:
        dve.wait_ge(ex_ok, b + 1)
        own.link(v.tensor_scalar(gb["sc"][:], gb["ex"][:], 1.0, None, ALU.add))
        v.reciprocal(gb["sc"][:], gb["sc"][:]).then_inc(ex_used, 1)
        dve.wait_ge(ex_used, b + 1)
        s2 = gb["sc"][:].rearrange("p n (g q r) -> p (n g) q r", g=G, q=2)
        tt(hi[:], s2[:, :, :, 0], s2[:, :, :, 1], ALU.max)
        tt(lo[:], s2[:, :, :, 0], s2[:, :, :, 1], ALU.min)
    if piece == 1:
        tt(gb["m1"][:], hi[:, :, 0], hi[:, :, 1], ALU.max)
        tt(gb["m2"][:], hi[:, :, 0], hi[:, :, 1], ALU.min)
        tt(lo[:, :, 0], lo[:, :, 0], lo[:, :, 1], ALU.max)
        tt(gb["m2"][:], gb["m2"][:], lo[:, :, 0], ALU.max)
        tt(gs[:].rearrange("p n g -> p (n g)"), gb["m1"][:], gb["m2"][:], ALU.add)
    if piece == 2:
        mine = bc(gs[:].unsqueeze(3), [P, TPB, G, G])
        other = bc(gs[:].unsqueeze(2), [P, TPB, G, G])
        tt(gb["gt"][:], other, mine, ALU.is_gt)
        tt(gb["ge"][:], other, mine, ALU.is_equal)
        tt(gb["ge"][:], gb["ge"][:], bc(gb["lt4"][:].unsqueeze(1), [P, TPB, G, G]), ALU.mult)
        tt(gb["gt"][:], gb["gt"][:], gb["ge"][:], ALU.add)
        own.link(v.tensor_reduce(gb["rank"][:], gb["gt"][:], AX.X, ALU.add))
        own.link(v.tensor_scalar(gb["ok"][:], gb["rank"][:], float(TOPG), None, ALU.is_lt))
    if piece == 3:
        ok = bc(gb["ok"][:].unsqueeze(3), [P, TPB, G, E // G])
        g4 = lambda n: gb[n][:].rearrange("p n (g q) -> p n g q", g=G)
        tt(g4("ms"), g4("sc"), ok, ALU.mult)
        own.link(v.tensor_scalar(gb["ok"][:], gb["ok"][:], -1.0, None, ALU.add))
        own.link_alone(v.tensor_tensor(g4("ms"), g4("ms"), ok, ALU.add), passed)
        for t in range(TPB):
            last = v.max(gb["top"][:, t, :], gb["ms"][:, t, :])
        own.link(last)
    if piece == 4:
        fourth = bc(gb["top"][:, :, TOPK - 1:TOPK], [P, TPB, E])
        tt(gb["a"][:], gb["ms"][:], fourth, ALU.is_gt)
        tt(gb["bq"][:], gb["ms"][:], fourth, ALU.is_equal)
        own.link(v.tensor_reduce(gb["cnt"][:], gb["a"][:], AX.X, ALU.add))
        own.link(v.tensor_scalar(gb["cnt"][:], gb["cnt"][:], -1.0, float(TOPK), ALU.mult, ALU.add))
    if piece == 5:
        running_count(v, own, gb, "bq")
        tt(gb["c"][:], gb["ms"][:], bc(gb["cnt"][:].unsqueeze(2), [P, TPB, E]), ALU.is_le)
        tt(gb["bq"][:], gb["bq"][:], gb["c"][:], ALU.mult)
        tt(gb["a"][:], gb["a"][:], gb["bq"][:], ALU.add)
        v.tensor_copy(keep["sel"][:, rows, :], gb["a"][:]).then_inc(sel_ok, 1)
    if piece == 6:
        running_count(v, own, gb, "a")
        mk, k3 = keep["mk"][:, rows, :, :], [P, TPB, TOPK, E]
        own.link(v.tensor_tensor(gb["mw"][:], bc(gb["ms"][:].unsqueeze(2), k3),
                                 bc(gb["kth"][:].unsqueeze(1).unsqueeze(3), k3), ALU.is_equal))
        tt(gb["mw"][:], gb["mw"][:], bc(gb["a"][:].unsqueeze(2), k3), ALU.mult)
        own.link(v.tensor_copy(mk, gb["mw"][:]))
    if piece == 7:
        k3 = [P, TPB, TOPK, E]
        tt(gb["a"][:], gb["a"][:], gb["sc"][:], ALU.mult)
        own.link(v.tensor_reduce(gb["ws"][:], gb["a"][:], AX.X, ALU.add))
        own.link(v.tensor_scalar(gb["ws"][:], gb["ws"][:], 1e-6, None, ALU.add))
        own.link(v.reciprocal(gb["ws"][:], gb["ws"][:]))
        tt(gb["a"][:], gb["a"][:], bc(gb["ws"][:].unsqueeze(2), [P, TPB, E]), ALU.mult)
        tt(gb["mw"][:], gb["mw"][:], bc(gb["a"][:].unsqueeze(2), k3), ALU.mult)
        own.link(v.tensor_reduce(keep["wk"][:, rows, :], gb["mw"][:], AX.X, ALU.add))


def running_count(v, own, gb, name):
    for sh, src, dst in ((1, name, "c"), (2, "c", "ex2"), (4, "ex2", "c"), (8, "c", "ms")):
        own.link(v.tensor_copy(gb[dst][:, :, 0:sh], gb[src][:, :, 0:sh]))
        own.link(v.tensor_tensor(gb[dst][:, :, sh:E], gb[src][:, :, sh:E], gb[src][:, :, 0:E - sh], ALU.add))


QUADS = 16
KC = T // P
LOAD = 16 * 9


AHEAD = 22
SWITCH = (32 - AHEAD) // 2
ROWS1, ROWS0 = SWITCH + 1, SWITCH + 9
def halve(nc, own, a, width):
    while width > 1:
        width //= 2
        own.link(nc.gpsimd.tensor_tensor(a[..., 0:width], a[..., 0:width], a[..., width:2 * width], ALU.add))


def plan_counters(nc, own, plan, s_idx, zero_out, counters_ok):
    g = nc.gpsimd
    own.link(g.memset(plan["zero"][:], 0.0))
    g.dma_start(s_idx.rearrange("(p n) a -> p (n a)", p=P), plan["zero"][:]).then_inc(zero_out, 16)
    own.link(g.iota(plan["itok"][:], [[P, NT]], base=0, channel_multiplier=1))
    own.link(g.tensor_copy(plan["tok"][:], plan["itok"][:]))
    own.link(g.iota(plan["itile"][:], [[1, NX]], base=0, channel_multiplier=0))
    own.link(g.tensor_copy(plan["tile"][:], plan["itile"][:]))
    g.tensor_scalar(plan["filled"][:], plan["tile"][:, 0:NT], float(P), 0.0, ALU.mult, ALU.add)        .then_inc(counters_ok, 1)


def plan_counts(nc, own, plan, keep, counters_ok, nt_ok):
    full = [P, E, NT]
    own.eng.wait_ge(counters_ok, 1)
    own.link(nc.vector.tensor_tensor(plan["full"][:], keep["tot"][:].unsqueeze(2).to_broadcast(full),
                                     plan["filled"][:].unsqueeze(1).to_broadcast(full), ALU.is_gt))
    nc.vector.tensor_reduce(plan["nt"][:], plan["full"][:], AX.X, ALU.add).then_inc(nt_ok, 1)


def plan_offsets(nc, own, plan, nt_ok, sums_ok):
    g = nc.gpsimd
    wait_alone(own.eng, nt_ok, 1, own.passed)
    for sh, src, dst in ((1, "nt", "c0"), (2, "c0", "c1"), (4, "c1", "c0"), (8, "c0", "c1")):
        own.link(g.tensor_copy(plan[dst][:, 0:sh], plan[src][:, 0:sh]))
        own.link(g.tensor_tensor(plan[dst][:, sh:E], plan[src][:, sh:E], plan[src][:, 0:E - sh], ALU.add))
    own.link(g.tensor_tensor(plan["off"][:], plan["c1"][:], plan["nt"][:], ALU.subtract))
    own.link(g.tensor_scalar(plan["off"][:], plan["off"][:], float(P), 0.0, ALU.mult, ALU.add))
    own.eng.sem_inc(sums_ok, 1)


def plan_places(nc, own, plan, keep):
    g = nc.gpsimd
    shape = [P, NT, TOPK, E]
    own.link(g.tensor_tensor(plan["pos"][:], keep["pre"][:], plan["off"][:].unsqueeze(1).to_broadcast([P, NT, E]),
                             ALU.add))
    own.link(g.tensor_tensor(plan["prod"][:], keep["mk"][:], plan["pos"][:].unsqueeze(2).to_broadcast(shape),
                             ALU.mult))
    halve(nc, own, plan["prod"][:], E)
    own.link(g.tensor_copy(keep["where"][:].rearrange("p (n k) -> p n k", k=TOPK), plan["prod"][:, :, :, 0]))


def plan_tiles(nc, own, plan, keep, sums_ok):
    shape = [1, NX, E]
    own.eng.wait_ge(sums_ok, 1)
    own.link(nc.vector.tensor_tensor(plan["le"][:], plan["c1"][0:1, :].unsqueeze(1).to_broadcast(shape),
                                     plan["tile"][0:1, :].unsqueeze(2).to_broadcast(shape), ALU.is_le))
    own.link(nc.vector.tensor_reduce(plan["eidf"][:], plan["le"][:], AX.X, ALU.add))
    own.link(nc.vector.tensor_scalar(keep["eid"][:], plan["eidf"][:], float(E - 1), None, ALU.min))


Q_RUNS = [(0, 1, 3), (1, 1, 2), (2, 1, 1)]
K_RUNS = [(0, 3, 1), (0, 2, 1), (0, 1, 1)]


def stage_b(nc, s_q, s_k, s_v, s_o, s_idx, w13, w2, w_out, b_out, keep):
    with ExitStack() as ctx:
        sb = lambda n, s, d=F32: ctx.enter_context(nc.sbuf_tensor(n, s, d))
        sem = lambda n: ctx.enter_context(nc.semaphore(n))
        qt = [sb(f"qt{i}", [P, 2, HG, QH], BF16) for i in range(2)]
        kt = [sb(f"kt{i}", [P, HG, T], BF16) for i in range(2)]
        vt = [sb(f"vt{i}", [P, KC, HG * VW]) for i in range(2)]
        pr = sb("pr", [P, 8, QH])
        mx = sb("mx", [P, 2, 16])
        mrest = sb("mrest", [P, 16])
        mp = sb("mp", [P, 2, 3, 16], BF16)
        mrow = sb("mrow", [48, 2, P], BF16)
        osb = sb("osb", [P, QH])
        rec = sb("rec", [P, 16])
        on = sb("on", [P, 2, 4, HG, D])
        identb = sb("identb", [P, P], BF16)
        ident = sb("ident_b", [P, P])

        pm = [ctx.enter_context(nc.psum_tensor(f"pm{i}", [P, 2, 512], F32)) for i in range(2)]
        pst = [ctx.enter_context(nc.psum_tensor(f"pst{i}", [P, 512], F32)) for i in range(2)]
        po = [ctx.enter_context(nc.psum_tensor(f"po{i}", [P, 512], F32)) for i in range(2)]

        id_ok, row1_ok, po_ok = sem("idb_ok"), sem("row1_ok"), sem("po_ok")
        qk_in = [sem(f"qk_in{i}") for i in range(2)]
        v_in = [sem(f"v_in{i}") for i in range(2)]
        st_ok, exp_ok, pv_ok = sem("st_ok"), sem("exp_ok"), sem("pv_ok")
        mx_full, mx_free = sem("mx_full"), sem("mx_free")
        mp_ok = sem("mp_ok")
        mrow_in = [sem(f"mrow_in{i}") for i in range(2)]
        osb_ok, rec_ok = sem("osb_ok"), sem("rec_ok")
        o_out = [sem(f"o_out{i}") for i in range(2)]
        pool_own, passed = sem("pool_own_b"), sem("passed_b")
        plan = {n: sb("p_" + n, sh, d) for n, sh, d in (
            ("zero", [P, NX], F32), ("itok", [P, NT], I32), ("tok", [P, NT], F32), ("itile", [P, NX], I32),
            ("tile", [P, NX], F32), ("full", [P, E, NT], F32), ("c0", [P, E], F32), ("c1", [P, E], F32),
            ("nt", [P, E], F32), ("off", [P, E], F32), ("pos", [P, NT, E], F32), ("prod", [P, NT, TOPK, E], F32),
            ("le", [1, NX, E], F32), ("eidf", [1, NX], F32), ("filled", [P, NT], F32), ("slot", [P, 2, TOPK], U32), ("data", [P, 2], F32))}
        plan_own, zero_out, slot_ok = sem("plan_own"), sem("zero_out"), sem("slot_ok")
        counters_ok, nt_ok, sums_ok, plan_dve = sem("counters_ok"), sem("nt_ok"), sem("sums_ok"), sem("plan_dve")
        plan_out = [sem(f"plan_out{i}") for i in range(2)]
        block = ctx.enter_context(nc.Block())

        def uses(k):
            tasks = [(AHEAD + 2 * k + i) % 32 for i in range(2)]
            more = {2: ["out"], 10: ["out"], ROWS1: ["rows"], ROWS0: ["rows"]}.get(k, [])
            return tasks + more
        FIRST = AHEAD + 1
        FIRST_ROWS = 18
        before = [sum(len(uses(i)) for i in range(k)) for k in range(QUADS + 1)]
        PER = before[QUADS]

        def place(g, k, i):
            return FIRST + g * PER + before[k] + i

        @block.sync
        def _(sp):
            def load(buf, gi):
                for src, dst, runs in ((s_q[0], qt[buf][:, 0, :, :], Q_RUNS), (s_q[1], qt[buf][:, 1, :, :], Q_RUNS),
                                       (s_k, kt[buf], K_RUNS)):
                    row = 0
                    for part, count, rep in runs:
                        parts = src[bass.ds(gi // 4, 1), part:part + count, :, bass.ds(gi % 4 * HG, HG), :]\
                            .rearrange("b a d h t -> (b a) d (h t)")
                        if rep > 1:
                            parts = parts.to_broadcast([rep, D, parts.shape[2]])
                        end = row + count * rep * D
                        sp.dma_start(dst[row:end], parts).then_inc(qk_in[buf], 16)
                        row = end

            def load_v(buf, j, gg):
                sp.dma_start(vt[buf][:, :, :],
                             s_v[bass.ds((j // 2) * T, T), bass.ds((j % 2) * 2 * HG + gg * HG, HG), :]
                             .rearrange("(n p) h w -> p n (h w)", p=P)).then_inc(v_in[buf], 16)

            def rows(use, half, buf):
                sp.wait_ge(mx_free, use + 1)
                sp.dma_start(qt[buf][KR:KR + MR, half, :, :], mrow[:, half, :]).then_inc(mrow_in[half], 16)

            def store(use, half, j, gg):
                sp.wait_ge(mx_free, use + 1)
                dst = s_o[bass.ds((j // 2) * T + half * QH, QH), bass.ds((j % 2) * 2 * GR + gg * GR, GR)]
                sp.dma_start(dst.rearrange("(n p) c -> p n c", p=P),
                             on[:, half, :, :, :].rearrange("p n h d -> p n (h d)")).then_inc(o_out[half], 16)

            load(0, 0)
            load_v(0, 0, 0)
            rows(FIRST_ROWS, 0, 0)

            def body(j):
                for gg in range(2):
                    g = j * 2 + gg
                    need(sp, st_ok, g * 64)
                    load(1 - gg, (g + 1) % NG)
                    need(sp, pv_ok, g * QUADS)
                    if gg == 0:
                        load_v(1, j, 1)
                    else:
                        load_v(0, (j + 1) % (NG // 2), 0)
                    if gg == 1:
                        store(place(g, 2, 2), 1, j, 0)
                    elif not (isinstance(j, int) and j == 0):
                        store(place(g, 2, 2), 1, j - 1, 1)
                    rows(place(g, ROWS1, 2), 1, gg)
                    store(place(g, 10, 2), 0, j, gg)
                    rows(place(g, ROWS0, 2), 0, 1 - gg)
                    if isinstance(g, int) and g == 1:
                        weights()

            def weights():
                w_in = keep["w_in"]
                sp.dma_start(keep["w13"][:], w13.rearrange("(c p) e n -> p c e n", p=P)).then_inc(w_in, 16)
                sp.dma_start(keep["w2"][:], w2).then_inc(w_in, 16)
                sp.dma_start(keep["w_out"][:], w_out.rearrange("(c p) n -> p c n", p=P)).then_inc(w_in, 16)
                sp.dma_start(keep["b_out"][:], b_out.rearrange("(a c) -> a c", a=1).to_broadcast([P, C]))\
                    .then_inc(w_in, 16)

            rounds(sp, NG // 2, body)
            store(FIRST + NG * PER, 1, NG // 2 - 1, 1)
            for i in range(2):
                sp.wait_ge(o_out[i], 16 * NG)
            sp.wait_ge(mrow_in[0], 16 * (NG + 1))

        @block.gpsimd
        def _(pool):
            own = Chain(pool, pool_own, passed)
            own.link(nc.gpsimd.memset(ident[:], 0.0))
            nc.gpsimd.affine_select(out=ident[:], in_=ident[:], compare_op=ALU.not_equal, fill=1.0, base=0,
                                    pattern=[[-1, P]], channel_multiplier=1).then_inc(id_ok, 1)
            own.link(nc.gpsimd.memset(identb[:], 0.0))
            nc.gpsimd.affine_select(out=identb[:], in_=identb[:], compare_op=ALU.not_equal, fill=1.0, base=0,
                                    pattern=[[-1, P]], channel_multiplier=1).then_inc(id_ok, 1)
            start = own.n
            planned = Chain(pool, plan_own, passed)
            plan_counters(nc, planned, plan, s_idx, zero_out, counters_ok)

            def split(n, half, last_use):
                own.base, own.n = start + n * 4, 0
                wait_alone(pool, mx_free, last_use + 1, passed)
                own.link(nc.gpsimd.tensor_scalar(mp[:, half, 0, :], mx[:, half, :], -1.0, 0.0, ALU.mult, ALU.add))
                own.link(nc.gpsimd.tensor_tensor(mrest[:], mx[:, half, :], mp[:, half, 0, :], ALU.add))
                own.link(nc.gpsimd.tensor_scalar(mp[:, half, 1, :], mrest[:], -1.0, 0.0, ALU.mult, ALU.add))
                own.link(nc.gpsimd.tensor_tensor(mrest[:], mrest[:], mp[:, half, 1, :], ALU.add))
                nc.gpsimd.tensor_scalar(mp[:, half, 2, :], mrest[:], -1.0, 0.0, ALU.mult, ALU.add).then_inc(mp_ok, 1)


            def send(n, sl, uses):
                if not (isinstance(uses, int) and uses == 0):
                    wait_alone(pool, plan_out[sl], 64 * uses, passed)
                nc.gpsimd.tensor_copy(plan["slot"][:, sl, :], keep["where"][:, bass.ds(n * TOPK, TOPK)])\
                    .then_inc(slot_ok, 1)
                nc.gpsimd.tensor_copy(plan["data"][:, sl:sl + 1], plan["tok"][:, bass.ds(n, 1)]).then_inc(slot_ok, 1)
                wait_alone(pool, slot_ok, 2 * (n + 1), passed)
                for k in range(TOPK):
                    pool.indirect_dma_start(
                        out=s_idx, out_offset=bass.IndirectOffsetOnAxis(ap=plan["slot"][:, sl, k:k + 1], axis=0),
                        in_=plan["data"][:, sl:sl + 1], in_offset=None).then_inc(plan_out[sl], 16)

            split(0, 0, 15)
            plan_offsets(nc, planned, plan, nt_ok, sums_ok)

            def body(j):
                for gg in range(2):
                    g = j * 2 + gg
                    for half in (1, 0):
                        i = gg * 2 + 1 - half
                        split(2 * g + 2 - half, half, place(g, SWITCH - 1 if half else SWITCH + 7, 1))
                        if not isinstance(j, int):
                            send(4 * j + i, i % 2, 2 * j + i // 2)
                        elif i == 0:
                            plan_places(nc, planned, plan, keep)
                        elif i == 1:
                            wait_alone(pool, zero_out, 16, passed)
                        else:
                            for n in (2 * i - 4, 2 * i - 3):
                                send(n, n % 2, n // 2)
            rounds(pool, NG // 2, body)
            for i in range(2):
                wait_alone(pool, plan_out[i], 64 * NT // 2, passed)

        @block.scalar
        def _(act):
            def body(j):
                for gg in range(2):
                    g = j * 2 + gg
                    for k in range(QUADS):
                        q = g * QUADS + k
                        need(act, pv_ok, q - 1)
                        for i in range(4):
                            act.wait_ge(st_ok, q * 4 + i + 1)
                            nc.scalar.activation(pr[:, (k % 2) * 4 + i, :], pst[i % 2][:, :], ACT.Exp, scale=SCALE)\
                                .then_inc(exp_ok, 1)
                            if k % 8 == 1 and i == 1:
                                u = 2 * g + k // 8 - 1
                                if not (isinstance(u, int) and u < 0):
                                    take_o(u, (k // 8 + 1) % 2)

            def take_o(u, half):
                act.wait_ge(pv_ok, 8 * (u + 1))
                nc.scalar.activation(osb[:, :], po[half][:, :], ACT.Copy).then_inc(osb_ok, 1)

            act.wait_ge(po_ok, 1)
            rounds(act, NG // 2, body)
            take_o(2 * NG - 1, 1)

        @block.vector
        def _(dve):
            for i in range(2):
                nc.vector.memset(kt[i][KR:KR + MR, :, :], 1.0).then_inc(row1_ok, 1)
            nc.vector.memset(po[0][:, :], 0.0)
            nc.vector.memset(po[1][:, :], 0.0).then_inc(po_ok, 1)

            def maximum(use, slot, half, col):
                dve.wait_ge(mx_full, use + 1)
                nc.vector.tensor_reduce(mx[:, half, col:col + 1], pm[slot][:, :, :].rearrange("p a n -> p (a n)"),
                                        AX.X, ALU.max).then_inc(mx_free, 1)

            def maxrows(use, slot, half, sent):
                dve.wait_ge(mx_full, use + 1)
                need(dve, mrow_in[half], 16 * sent)
                nc.vector.tensor_copy(mrow[:, half, :], pm[slot][0:48, 0, 0:P]).then_inc(mx_free, 1)

            def normalise(use, slot, half, u, outs):
                dve.wait_ge(mx_full, use + 1)
                o = pm[slot][:, 0, :].rearrange("p (m w) -> p m w", w=32)
                nc.vector.reciprocal(rec[:].unsqueeze(2), o[:, :, D:VW]).then_inc(rec_ok, 1)
                dve.wait_ge(rec_ok, u + 1)
                need(dve, o_out[half], outs * 16)
                nc.vector.tensor_tensor(on[:, half, :, :, :].rearrange("p n h d -> p (n h) d"), o[:, :, 0:D],
                                        rec[:].unsqueeze(2).to_broadcast([P, 16, D]), ALU.mult).then_inc(mx_free, 1)

            planned = Chain(dve, plan_dve)
            plan_counts(nc, planned, plan, keep, counters_ok, nt_ok)
            for use in range(FIRST):
                n = use - (use > FIRST_ROWS)
                if use == FIRST_ROWS:
                    maxrows(use, use % 2, 0, 0)
                else:
                    maximum(use, use % 2, n // 16, n % 16)

            def body(j):
                for gg in range(2):
                    g = j * 2 + gg
                    for k in range(QUADS):
                        if k in (SWITCH, SWITCH + 8):
                            need(dve, mp_ok, 2 * g + 1 + k // 8)
                        if isinstance(j, int) and gg == 0 and k == 9:
                            plan_tiles(nc, planned, plan, keep, sums_ok)
                        for i, what in enumerate(uses(k)):
                            use = place(g, k, i)
                            slot = (FIRST + before[k] + i) % 2
                            if what == "out":
                                u = 2 * g + k // 8 - 1
                                half = (k // 8 + 1) % 2
                                if isinstance(u, int) and u < 0:
                                    dve.wait_ge(mx_full, use + 1)
                                    nc.vector.memset(rec[:], 1.0).then_inc(mx_free, 1)
                                    continue
                                normalise(use, slot, half, u, g - (1 if half else 0))
                            elif what == "rows":
                                half = 1 if k == ROWS1 else 0
                                maxrows(use, slot, half, g if half else g + 1)
                            else:
                                maximum(use, slot, what // 16, what % 16)
            rounds(dve, NG // 2, body)
            normalise(FIRST + NG * PER, (FIRST + NG * PER) % 2, 1, 2 * NG - 1, NG - 1)

        @block.tensor
        def _(pe):
            def scores_max(buf, task, slot, use):
                for kk in range(2):
                    max_half(buf, task, slot, use, kk)

            def max_half(buf, task, slot, use, kk):
                half, h, qi = task // 16, task % 16 // 4, task % 4
                if kk == 0:
                    need(pe, mx_free, use - 1)
                mm = pe.matmul(pm[slot][:, kk, :], qt[buf][0:KR, half, h, qi * P:(qi + 1) * P],
                               kt[buf][0:KR, h, kk * 512:(kk + 1) * 512], start=True, stop=True)
                if kk == 1:
                    mm.then_inc(mx_full, 1)

            def turn_rows(slot, use, half, n):
                need(pe, mx_free, use - 1)
                pe.wait_ge(mp_ok, n + 1)
                pe.matmul(pm[slot][0:48, 0, 0:P], mp[:, half, :, :].rearrange("p a c -> p (a c)"), identb[:],
                          start=True, stop=True).then_inc(mx_full, 1)

            def turn_out(slot, use, u):
                need(pe, mx_free, use - 1)
                pe.wait_ge(osb_ok, u + 1)
                for n in range(4):
                    mm = pe.transpose(pm[slot][:, 0, n * P:(n + 1) * P], osb[:, n * P:(n + 1) * P], ident[:])
                mm.then_inc(mx_full, 1)

            def scores(buf, half, kc, h, s):
                need(pe, exp_ok, s - 1)
                pe.matmul(pst[h % 2][:, :], kt[buf][0:KR + MR, h, kc * P:(kc + 1) * P],
                          qt[buf][0:KR + MR, half, h, :], start=True, stop=True)\
                    .then_inc(st_ok, 1)

            def pv(buf, k, q, u):
                pe.wait_ge(exp_ok, 4 * (q + 1))
                if k % 8 == 0:
                    need(pe, osb_ok, u - 1)
                for h in range(HG):
                    mm = pe.matmul(po[k // 8][32 * h:32 * h + VW, :], vt[buf][:, k % 8, h * VW:(h + 1) * VW],
                                   pr[:, (k % 2) * 4 + h, :], start=(k % 8 == 0), stop=(k % 8 == 7),
                                   tile_position=(0, 32 * h))
                mm.then_inc(pv_ok, 1)

            pe.wait_ge(id_ok, 2)
            pe.wait_ge(row1_ok, 2)
            pe.wait_ge(qk_in[0], LOAD)
            for use in range(FIRST):
                if use == FIRST_ROWS:
                    turn_rows(use % 2, use, 0, 0)
                else:
                    scores_max(0, use - (use > FIRST_ROWS), use % 2, use)
            pe.wait_ge(po_ok, 1)

            def body(j):
                for gg in range(2):
                    g = j * 2 + gg
                    for k in range(QUADS):
                        q = g * QUADS + k
                        half, kc = k // 8, k % 8
                        if k == 0:
                            pe.wait_ge(mrow_in[0], 16 * (g + 1))
                            pe.wait_ge(v_in[gg], 16 * (j + 1))
                        if k == 8:
                            pe.wait_ge(mrow_in[1], 16 * (g + 1))
                        if k == SWITCH:
                            pe.wait_ge(qk_in[1 - gg], LOAD * (j + 1 + gg))
                        mbuf = gg if k < SWITCH else 1 - gg
                        us = uses(k)
                        slots = [(FIRST + before[k] + i) % 2 for i in range(len(us))]
                        scores(gg, half, kc, 0, 4 * q)
                        scores(gg, half, kc, 1, 4 * q + 1)
                        max_half(mbuf, us[0], slots[0], place(g, k, 0), 0)
                        max_half(mbuf, us[0], slots[0], place(g, k, 0), 1)
                        max_half(mbuf, us[1], slots[1], place(g, k, 1), 0)
                        scores(gg, half, kc, 2, 4 * q + 2)
                        max_half(mbuf, us[1], slots[1], place(g, k, 1), 1)
                        scores(gg, half, kc, 3, 4 * q + 3)
                        if not (isinstance(q, int) and q == 0):
                            pb, pk = (gg, k - 1) if k else (1 - gg, QUADS - 1)
                            pv(pb, pk, q - 1, 2 * g + pk // 8 if k else 2 * g - 1)
                        if len(us) == 3:
                            if us[2] == "out":
                                u = 2 * g + k // 8 - 1
                                if isinstance(u, int) and u < 0:
                                    need(pe, mx_free, place(g, k, 2) - 1)
                                    pe.matmul(pm[slots[2]][:, 0, 0:P], identb[:], identb[:], start=True,
                                              stop=True).then_inc(mx_full, 1)
                                else:
                                    turn_out(slots[2], place(g, k, 2), u)
                            else:
                                turn_rows(slots[2], place(g, k, 2), 1 if k == ROWS1 else 0,
                                          2 * g + (1 if k == ROWS1 else 2))
            rounds(pe, NG // 2, body)
            pv(1, QUADS - 1, NG * QUADS - 1, 2 * NG - 1)
            end = FIRST + NG * PER
            turn_out(end % 2, end, 2 * NG - 1)


def stage_c(nc, s_xn, s_idx, s_y, keep):
    PER, HALF = 8, 4
    with ExitStack() as ctx:
        sb = lambda n, s, d=F32: ctx.enter_context(nc.sbuf_tensor(n, s, d))
        sem = lambda n: ctx.enter_context(nc.semaphore(n))
        w13, w2, eid = keep["w13"], keep["w2"], keep["eid"]
        idf = sb("idf", [NX // 2, 2, P])
        idx = sb("idx", [P, NX], U32)
        slot = sb("slot_c", [P, 2, HALF], U32)
        xg = sb("xg", [P, PER, C])
        xt = sb("xt_c", [P, 2, CC, P])
        sg = sb("sg_c", [P, 2, F])
        hb = sb("hb_c", [P, 2, F])
        ht = sb("ht_c", [P, 2, P])
        ys = sb("ys_c", [P, 4, C])
        ident = sb("ident_c", [P, P])
        pT, pG, pH, pY = ([ctx.enter_context(nc.psum_tensor(f"c_{n}{i}", [P, 512], F32)) for i in range(2)]
                          for n in ("pT", "pG", "pH", "pY"))
        id_ok, idf_in, idT_ok, idx_ok, slot_ok = (sem("c_" + n) for n in ("id_ok", "idf_in", "idT_ok", "idx_ok", "slot_ok"))
        g_in = [sem(f"g_in{i}") for i in range(PER)]
        y_out = [sem(f"yc_out{i}") for i in range(4)]
        xT_ok, xt_ok, gu_ok, sg_ok, hb_ok, hT_ok, ht_ok, yy_ok, ys_ok = (
            sem("c_" + n) for n in ("xT_ok", "xt_ok", "gu_ok", "sg_ok", "hb_ok", "hT_ok", "ht_ok", "yy_ok", "ys_ok"))
        pool_own, passed = sem("pool_own_c"), sem("passed_c")
        block = ctx.enter_context(nc.Block())
        UP, HT, DOWN = 1, 3, 4

        @block.sync
        def _(sp):
            sp.dma_start(idf[:], s_idx.rearrange("(q a p) o -> a q (p o)", q=2, p=P)).then_inc(idf_in, 16)

            def store(k, t, j):
                sp.wait_ge(ys_ok, k + 1)
                sp.dma_start(s_y[bass.ds(k * P, P), :], ys[:, t % 4, :]).then_inc(y_out[t % 4], 16)
            steps(sp, NX // PER, PER, NX, [(DOWN, store)])
            for i in range(4):
                sp.wait_ge(y_out[i], 16 * NX // 4)

        @block.gpsimd
        def _(pool):
            own = Chain(pool, pool_own)
            own.link(nc.gpsimd.memset(ident[:], 0.0))
            nc.gpsimd.affine_select(out=ident[:], in_=ident[:], compare_op=ALU.not_equal, fill=1.0, base=0,
                                    pattern=[[-1, P]], channel_multiplier=1).then_inc(id_ok, 1)
            pool.wait_ge(idx_ok, 1)

            def gather(k, t, j):
                half = t // HALF
                if t % HALF == 0:
                    if not isinstance(j, int):
                        for i in range(HALF):
                            wait_alone(pool, g_in[t + i], 16 * j, passed)
                    nc.gpsimd.tensor_copy(slot[:, half, :], idx[:, bass.ds(k, HALF)]).then_inc(slot_ok, 1)
                    wait_alone(pool, slot_ok, 2 * j + half + 1, passed)
                if not isinstance(j, int):
                    wait_alone(pool, xT_ok, k - PER + 1, passed)
                pool.indirect_dma_start(
                    out=xg[:, t, :], out_offset=None, in_=s_xn,
                    in_offset=bass.IndirectOffsetOnAxis(ap=slot[:, half, t % HALF:t % HALF + 1], axis=0))\
                    .then_inc(g_in[t], 16)
            steps(pool, NX // PER, PER, NX, [(0, gather)])

        @block.scalar
        def _(act):
            def turned(k, t, j):
                act.wait_ge(xT_ok, k + 1)
                need(act, gu_ok, k - 1)
                nc.scalar.activation(xt[:, t % 2, :, :], pT[t % 2][:, 0:C].rearrange("p (c n) -> p c n", c=CC),
                                     ACT.Copy).then_inc(xt_ok, 1)

            def silu(k, t, j):
                act.wait_ge(gu_ok, k + 1)
                need(act, hb_ok, k - 1)
                nc.scalar.activation(sg[:, t % 2, :], pG[t % 2][:, 0:F], ACT.Silu).then_inc(sg_ok, 1)
            steps(act, NX // PER, PER, NX, [(0, turned), (UP, silu)])

        @block.vector
        def _(dve):
            dve.wait_ge(idT_ok, 2)
            for q in range(2):
                last = nc.vector.tensor_copy(idx[:, q * NX // 2:(q + 1) * NX // 2], pT[q][:, 0:NX // 2])
            last.then_inc(idx_ok, 1)

            def output(k, t, j):
                dve.wait_ge(yy_ok, k + 1)
                need(dve, y_out[t % 4], (2 * j + t // 4) * 16)
                nc.vector.tensor_copy(ys[:, t % 4, :], pY[t % 2][:, 0:C]).then_inc(ys_ok, 1)

            def turned(k, t, j):
                dve.wait_ge(hT_ok, k + 1)
                need(dve, yy_ok, k - 1)
                nc.vector.tensor_copy(ht[:, t % 2, :], pH[t % 2][:, 0:P]).then_inc(ht_ok, 1)

            def gated(k, t, j):
                dve.wait_ge(sg_ok, k + 1)
                need(dve, hT_ok, k - 1)
                nc.vector.tensor_tensor(hb[:, t % 2, :], pG[t % 2][:, F:2 * F], sg[:, t % 2, :], ALU.mult)\
                    .then_inc(hb_ok, 1)
            steps(dve, NX // PER, PER, NX, [(DOWN, output), (HT, turned), (UP, gated)])

        @block.tensor
        def _(pe):
            pe.wait_ge(id_ok, 1)
            pe.wait_ge(keep["w_in"], 64)
            pe.wait_ge(idf_in, 16)
            for q in range(2):
                pe.transpose(pT[q][:, 0:NX // 2], idf[:, q, :], ident[0:NX // 2, 0:NX // 2]).then_inc(idT_ok, 1)
            pe.wait_ge(idx_ok, 1)

            LOOK = 4
            expert = [pe.alloc_register(f"expert{t}") for t in range(PER)]

            def look_up(k, t, j):
                if t % LOOK == 0:
                    pe.load(expert[t:t + LOOK], eid[0:1, bass.ds(k, LOOK)])

            def chosen(t):
                return bass.ds(pe.snap(expert[t], min_val=0, max_val=E - 1), 1)

            def turn(k, t, j):
                pe.wait_ge(g_in[t], 16 * (j + 1))
                need(pe, xt_ok, k - 1)
                for c in range(CC):
                    mm = pe.transpose(pT[t % 2][:, c * P:(c + 1) * P], xg[:, t, c * P:(c + 1) * P], ident[:])
                mm.then_inc(xT_ok, 1)

            def up(k, t, j):
                pe.wait_ge(xt_ok, k + 1)
                need(pe, hb_ok, k - 1)
                for c in range(CC):
                    mm = pe.matmul(pG[t % 2][:, 0:2 * F], xt[:, t % 2, c, :],
                                   w13[:, c, chosen(t), :].rearrange("p a n -> p (a n)"),
                                   start=(c == 0), stop=(c == CC - 1))
                mm.then_inc(gu_ok, 1)

            def turn_h(k, t, j):
                pe.wait_ge(hb_ok, k + 1)
                need(pe, ht_ok, k - 1)
                pe.transpose(pH[t % 2][:, 0:P], hb[:, t % 2, :], ident[:]).then_inc(hT_ok, 1)

            def down(k, t, j):
                pe.wait_ge(ht_ok, k + 1)
                need(pe, ys_ok, k - 1)
                pe.matmul(pY[t % 2][:, 0:C], ht[:, t % 2, :],
                          w2[:, chosen(t), :].rearrange("p a n -> p (a n)"),
                          start=True, stop=True).then_inc(yy_ok, 1)
            steps(pe, NX // PER, PER, NX, [(0, look_up), (0, turn), (DOWN, down), (HT, turn_h), (UP, up)])


def stage_d(nc, x, s_xn, s_o, s_y, out, keep):
    PER = 4
    with ExitStack() as ctx:
        sb = lambda n, s, d=F32: ctx.enter_context(nc.sbuf_tensor(n, s, d))
        sem = lambda n: ctx.enter_context(nc.semaphore(n))
        w13, w2, wo, bo = keep["w13"], keep["w2"], keep["w_out"], keep["b_out"]
        xr = sb("xr", [P, PER, C])
        xo = sb("xo", [P, PER, 2, C])
        xot = sb("xot", [P, PER, 4, P])
        slot = sb("slot_d", [P, 2, TOPK], U32)
        yg = sb("yg", [P, 2, TOPK, C])
        acc = sb("acc", [P, 2, C])
        sg = sb("sg_d", [P, 2, NS, F])
        hb = sb("hb_d", [P, 2, NS, F])
        ht = sb("ht_d", [P, 2, NS, P])
        ys = sb("ys_d", [P, 2, C])
        ident = sb("ident_d", [P, P])
        pT, pG, pH, pA = ([ctx.enter_context(nc.psum_tensor(f"d_{n}{i}", [P, 512], F32)) for i in range(2)]
                          for n in ("pT", "pG", "pH", "pA"))
        in_ok = [sem(f"in_ok{i}") for i in range(PER)]
        yg_in = [sem(f"yg_in{i}") for i in range(2)]
        y_out = [sem(f"yd_out{i}") for i in range(2)]
        id_ok, slot_ok, xT_ok, xt_ok, gu_ok, sg_ok, hb_ok, hT_ok, ht_ok, pa_ok, acc_ok, ys_ok = (
            sem("d_" + n) for n in ("id_ok", "slot_ok", "xT_ok", "xt_ok", "gu_ok", "sg_ok", "hb_ok", "hT_ok", "ht_ok",
                                    "pa_ok", "acc_ok", "ys_ok"))
        pool_own, dve_own, passed = sem("pool_own_d"), sem("dve_own_d"), sem("passed_d")
        block = ctx.enter_context(nc.Block())
        xd = x.rearrange("b t c -> (b t) c")
        od = out.rearrange("b t c -> (b t) c")
        UP, HT, DOWN = 1, 2, 3

        @block.sync
        def _(sp):
            def load(k, t, j):
                need(sp, pa_ok, k - PER + 1)
                need(sp, acc_ok, k - PER + 1)
                rows = bass.ds(k * P, P)
                sp.dma_start(xr[:, t, :], xd[rows, :]).then_inc(in_ok[t], 16)
                sp.dma_start(xo[:, t, 0, :], s_xn[rows, :]).then_inc(in_ok[t], 16)
                sp.dma_start(xo[:, t, 1, :], s_o[rows, :]).then_inc(in_ok[t], 16)

            def store(k, t, j):
                sp.wait_ge(ys_ok, k + 1)
                sp.dma_start(od[bass.ds(k * P, P), :], ys[:, t % 2, :]).then_inc(y_out[t % 2], 16)
            steps(sp, NT // PER, PER, NT, [(0, load), (DOWN + 1, store)])
            for i in range(2):
                sp.wait_ge(y_out[i], 16 * NT // 2)

        @block.gpsimd
        def _(pool):
            own = Chain(pool, pool_own)
            own.link(nc.gpsimd.memset(ident[:], 0.0))
            nc.gpsimd.affine_select(out=ident[:], in_=ident[:], compare_op=ALU.not_equal, fill=1.0, base=0,
                                    pattern=[[-1, P]], channel_multiplier=1).then_inc(id_ok, 1)

            def gather(k, t, j):
                if not (isinstance(k, int) and k < 2):
                    wait_alone(pool, acc_ok, k - 1, passed)
                nc.gpsimd.tensor_copy(slot[:, t % 2, :], keep["where"][:, bass.ds(k * TOPK, TOPK)]).then_inc(slot_ok, 1)
                wait_alone(pool, slot_ok, k + 1, passed)
                for n in range(TOPK):
                    pool.indirect_dma_start(
                        out=yg[:, t % 2, n, :], out_offset=None, in_=s_y,
                        in_offset=bass.IndirectOffsetOnAxis(ap=slot[:, t % 2, n:n + 1], axis=0))\
                        .then_inc(yg_in[t % 2], 16)
            steps(pool, NT // PER, PER, NT, [(0, gather)])

        @block.scalar
        def _(act):
            def turned(k, t, j):
                act.wait_ge(xT_ok, k + 1)
                need(act, pa_ok, k - PER + 1)
                nc.scalar.activation(xot[:, t, :, :], pT[t % 2][:, :].rearrange("p (k n) -> p k n", k=4), ACT.Copy)\
                    .then_inc(xt_ok, 1)

            def silu(k, t, j):
                act.wait_ge(gu_ok, k + 1)
                need(act, hb_ok, k - 1)
                nc.scalar.activation(sg[:, t % 2, :, :],
                                     pG[t % 2][:, :].rearrange("p (s g f) -> p s g f", s=NS, g=2)[:, :, 0, :], ACT.Silu)\
                    .then_inc(sg_ok, 1)
            steps(act, NT // PER, PER, NT, [(0, turned), (UP, silu)])

        @block.vector
        def _(dve):
            own = Chain(dve, dve_own)
            v = nc.vector

            def output(k, t, j):
                dve.wait_ge(pa_ok, k + 1)
                dve.wait_ge(acc_ok, k + 1)
                need(dve, y_out[t % 2], (2 * j + t // 2) * 16)
                v.tensor_tensor(ys[:, t % 2, :], pA[t % 2][:, 0:C], acc[:, t % 2, :], ALU.add).then_inc(ys_ok, 1)

            def turned(k, t, j):
                dve.wait_ge(hT_ok, k + 1)
                need(dve, pa_ok, k - 1)
                v.tensor_copy(ht[:, t % 2, :, :], pH[t % 2][:, 0:NS * P].rearrange("p (s n) -> p s n", s=NS))\
                    .then_inc(ht_ok, 1)

            def gated(k, t, j):
                dve.wait_ge(sg_ok, k + 1)
                need(dve, hT_ok, k - 1)
                v.tensor_tensor(hb[:, t % 2, :, :],
                                pG[t % 2][:, :].rearrange("p (s g f) -> p s g f", s=NS, g=2)[:, :, 1, :],
                                sg[:, t % 2, :, :], ALU.mult).then_inc(hb_ok, 1)

            def combine(k, t, j):
                own.base, own.n = k * TOPK, 0
                dve.wait_ge(in_ok[t], 48 * (j + 1))
                need(dve, ys_ok, k - 1)
                own.link(v.tensor_tensor(acc[:, t % 2, :], xr[:, t, :], bo[:], ALU.add))
                dve.wait_ge(yg_in[t % 2], 64 * (2 * j + t // 2 + 1))
                for n in range(TOPK):
                    w = keep["wk"][:, bass.ds(k, 1), n:n + 1].rearrange("p a b -> p (a b)")
                    ins = v.scalar_tensor_tensor(out=acc[:, t % 2, :], in0=yg[:, t % 2, n, :], scalar=w,
                                                 in1=acc[:, t % 2, :], op0=ALU.mult, op1=ALU.add)
                    if n < TOPK - 1:
                        own.link(ins)
                ins.then_inc(acc_ok, 1)
            steps(dve, NT // PER, PER, NT, [(DOWN, output), (HT, turned), (UP, gated), (HT, combine)])

        @block.tensor
        def _(pe):
            pe.wait_ge(id_ok, 1)

            def turn(k, t, j):
                pe.wait_ge(in_ok[t], 48 * (j + 1))
                need(pe, xt_ok, k - 1)
                for n in range(4):
                    mm = pe.transpose(pT[t % 2][:, n * P:(n + 1) * P], xo[:, t, n // 2, (n % 2) * P:(n % 2 + 1) * P],
                                      ident[:])
                mm.then_inc(xT_ok, 1)

            def up(k, t, j):
                pe.wait_ge(xt_ok, k + 1)
                need(pe, hb_ok, k - 1)
                for c in range(CC):
                    mm = pe.matmul(pG[t % 2][:, :], xot[:, t, c, :],
                                   w13[:, c, E:E + NS, :].rearrange("p s n -> p (s n)"),
                                   start=(c == 0), stop=(c == CC - 1))
                mm.then_inc(gu_ok, 1)

            def turn_h(k, t, j):
                pe.wait_ge(hb_ok, k + 1)
                need(pe, ht_ok, k - 1)
                for n in range(NS):
                    mm = pe.transpose(pH[t % 2][:, n * P:(n + 1) * P], hb[:, t % 2, n, :], ident[:])
                mm.then_inc(hT_ok, 1)

            def down(k, t, j):
                pe.wait_ge(ht_ok, k + 1)
                need(pe, ys_ok, k - 1)
                for c in range(CC):
                    pe.matmul(pA[t % 2][:, 0:C], xot[:, t, 2 + c, :], wo[:, c, :], start=(c == 0), stop=False)
                for n in range(NS):
                    mm = pe.matmul(pA[t % 2][:, 0:C], ht[:, t % 2, n, :], w2[:, E + n, :], start=False,
                                   stop=(n == NS - 1))
                mm.then_inc(pa_ok, 1)
            steps(pe, NT // PER, PER, NT, [(0, turn), (DOWN, down), (HT, turn_h), (UP, up)])


def program(nc, x, w_qkvg, b_qkv, rope, w13, w2, w_out, b_out, out):
    s_q = nc.dram_tensor("s_q", [2, B, 3, D, H, QH], BF16).ap()
    s_k = nc.dram_tensor("s_k", [B, 3, D, H, T], BF16).ap()
    s_v = nc.dram_tensor("s_v", [N, H, VW], F32).ap()
    s_xn = nc.dram_tensor("s_xn", [N, C], F32).ap()
    s_o = nc.dram_tensor("s_o", [N, C], F32).ap()
    s_idx = nc.dram_tensor("s_idx", [NX * P, 1], F32).ap()
    s_y = nc.dram_tensor("s_y", [NX * P, C], F32).ap()
    with ExitStack() as ctx:
        sb = lambda n, shape, d=F32: ctx.enter_context(nc.sbuf_tensor(n, shape, d))
        keep = dict(
            sel=sb("sel", [P, NT, E], BF16),
            mk=sb("mk", [P, NT, TOPK, E]),
            wk=sb("wk", [P, NT, TOPK]),
            pre=sb("pre", [P, NT, E]),
            tot=sb("tot", [P, E]),
            cntf=sb("cntf", [P, E]),
            where=sb("where", [P, NT * TOPK], U32),
            eid=sb("eid", [1, NX], I32),
            w13=sb("w13s", [P, CC, E + NS, 2 * F]), w2=sb("w2s", [P, E + NS, C]),
            w_out=sb("wos", [P, CC, C]), b_out=sb("bos", [P, C]),
            w_in=ctx.enter_context(nc.semaphore("w_in_c")))
        stage_a(nc, x, w_qkvg, b_qkv, rope, s_q, s_k, s_v, s_xn, keep)
        stage_b(nc, s_q, s_k, s_v, s_o, s_idx, w13, w2, w_out, b_out, keep)
        stage_c(nc, s_xn, s_idx, s_y, keep)
        stage_d(nc, x, s_xn, s_o, s_y, out, keep)


def rope_table():
    inv = (1.0 / ROPE_BASE ** (np.arange(0, D, 2, dtype=np.float32) / np.float32(D))).astype(np.float32)
    angle = (np.arange(T, dtype=np.float32)[:, None] * inv[None, :]).astype(np.float64)
    cos, sin = np.cos(angle), np.sin(angle)
    return np.stack([np.concatenate([cos, cos], 1), np.concatenate([-sin, sin], 1)], 1).astype(np.float32)


def kernel(L0_attn_x, L0_attn_W_qkv, L0_attn_b_qkv, L0_attn_W_out, L0_attn_b_out, L0_ffn_w_gate, L0_ffn_w1_e,
           L0_ffn_w3_e, L0_ffn_w2_e, L0_ffn_w1_s, L0_ffn_w3_s, L0_ffn_w2_s):
    import concourse.bacc as bacc
    from concourse.bass_utils import run_bass_kernel_spmd

    a = lambda v: np.ascontiguousarray(v)
    up = lambda e, s: np.concatenate([np.asarray(e), np.asarray(s).reshape(NS, F, C)], 0).transpose(2, 0, 1)
    arrays = {
        "x": a(L0_attn_x),
        "w_qkvg": a(np.concatenate([np.asarray(L0_attn_W_qkv), np.asarray(L0_ffn_w_gate).T], 1)),
        "b_qkv": a(L0_attn_b_qkv),
        "rope": rope_table(),
        "w13": a(np.concatenate([up(L0_ffn_w1_e, L0_ffn_w1_s), up(L0_ffn_w3_e, L0_ffn_w3_s)], 2)),
        "w2": a(np.concatenate([np.asarray(L0_ffn_w2_e).transpose(2, 0, 1),
                                np.asarray(L0_ffn_w2_s).reshape(C, NS, F).transpose(2, 1, 0)], 1)),
        "w_out": a(L0_attn_W_out),
        "b_out": a(L0_attn_b_out),
    }
    nc = bacc.Bacc("TRN2", target_bir_lowering=False, num_devices=1)
    aps = {n: nc.dram_tensor(n, v.shape, mybir.dt.from_np(v.dtype), kind="ExternalInput").ap()
           for n, v in arrays.items()}
    out = nc.dram_tensor("out", [B, T, C], F32, kind="ExternalOutput").ap()
    program(nc, **aps, out=out)
    return run_bass_kernel_spmd(nc, [arrays], core_ids=[0]).results[0]["out"]
```

```python
from contextlib import ExitStack

import numpy as np

import concourse.bass as bass
from concourse import mybir

F32 = mybir.dt.float32
BF16 = mybir.dt.bfloat16
I32, U32 = mybir.dt.int32, mybir.dt.uint32
ALU = mybir.AluOpType
ACT = mybir.ActivationFunctionType
AX = mybir.AxisListType

P = 128
B, T, C = 4, 1024, 256
N = B * T
H, D = 16, 16
NT = N // P
TPB = T // P
CC = C // P
E, F = 16, 128
NS = 2
G, TOPG, TOPK = 4, 2, 4
NX = N * TOPK // P + E
EPS = 1e-5
ROPE_BASE = 10000.0

HG = 4
NG = B * H // HG
GR = HG * D
QH = T // 2
VW = D + 1
Q_PART = [0, 0, 0, 1, 1, 2]
K_PART = [0, 1, 2, 0, 1, 0]
TERMS = len(Q_PART)
KR = TERMS * D
MR = 3
SCALE = D ** -0.5


def need(eng, sem, n):
    if isinstance(n, int) and n <= 0:
        return
    eng.wait_ge(sem, n)


def wait_alone(eng, sem, n, passed):
    eng.wait_ge(sem, n)
    eng.sem_inc(passed, 1)


class Chain:

    def __init__(self, eng, sem, passed=None):
        self.eng, self.sem, self.passed, self.base, self.n = eng, sem, passed, 0, 0

    def link(self, ins):
        self.n += 1
        ins.then_inc(self.sem, 1)
        self.follow(self.passed)

    def link_alone(self, ins, passed):
        self.n += 1
        ins.then_inc(self.sem, 1)
        self.follow(passed)

    def follow(self, passed):
        if passed is None:
            self.eng.wait_ge(self.sem, self.base + self.n)
        else:
            wait_alone(self.eng, self.sem, self.base + self.n, passed)


def rounds(eng, n, emit):
    emit(0)
    with eng.Fori(1, n) as j:
        emit(j)


def steps(eng, n, per, total, work):
    deepest = max(lag for lag, _ in work)

    def round_(j, count=per):
        for s in range(count):
            for lag, part in work:
                k = j * per + s - lag
                if isinstance(k, int) and not 0 <= k < total:
                    continue
                part(k, (s - lag) % per, j + (s - lag) // per)
    round_(0)
    with eng.Fori(1, n) as j:
        round_(j)
    round_(n, deepest)


def stage_a(nc, x, w_qkvg, b_qkv, rope, s_q, s_k, s_v, s_xn, keep, first):
    W = 3 * C + E
    with ExitStack() as ctx:
        sb = lambda n, s, d=F32: ctx.enter_context(nc.sbuf_tensor(n, s, d))
        ps = lambda n, s: ctx.enter_context(nc.psum_tensor(n, s, F32))
        sem = lambda n: ctx.enter_context(nc.semaphore(n))

        xs = sb("xs", [P, NT, C])
        wsb = sb("wsb", [P, CC, W])
        brow = sb("brow", [1, W])
        brest = sb("brest", [1, W])
        bparts = [sb(f"bpart{n}", [1, W], BF16) for n in range(3)]
        bias3 = sb("bias3", [3, W], BF16)
        ones3 = sb("ones3", [3, P], BF16)
        ropesb = sb("ropesb", [P, TPB, 2, D])
        ident = keep["ident"]
        bnst = sb("bnst", [P, NT, 6])
        mv = sb("mv", [P, NT, 2])
        var = sb("var", [P, NT])
        std = sb("std", [P, NT])
        rstd = sb("rstd", [P, NT])
        nwt = sb("nwt", [P, NT])
        xn = sb("xn_a", [P, 4, C])
        xt = sb("xt_a", [P, 2, CC, P])
        qks = sb("qks", [P, 2, 2 * C])
        rc = sb("rc", [P, 2, 2 * C])
        rs = sb("rs", [P, 2, 2 * C])
        qr = sb("qr", [P, 2, 2 * C])
        r1 = sb("r1", [P, 2, 4, P])
        stg = sb("stg", [P, 2, 3, 4, 4 * P], BF16)
        vst = sb("vst", [P, 2, H, VW])
        lg = sb("lg", [P, NT, E])
        gb = {n: sb("g_" + n, sh) for n, sh in dict(
            ex=[P, TPB, E], sc=[P, TPB, E], hi=[P, TPB * G, 2], lo=[P, TPB * G, 2], m1=[P, TPB * G],
            m2=[P, TPB * G], gs=[P, TPB, G], gt=[P, TPB, G, G], ge=[P, TPB, G, G], lt4=[P, G, G],
            rank=[P, TPB, G], ok=[P, TPB, G], ms=[P, TPB, E], top=[P, TPB, 8], a=[P, TPB, PAD + E], bq=[P, TPB, PAD + E],
            c=[P, TPB, PAD + E], ex2=[P, TPB, PAD + E], cnt=[P, TPB], ws=[P, TPB],
            kth=[P, TOPK], mw=[P, TPB, TOPK, E]).items()}

        pT = [ps(f"pT{i}", [P, 512]) for i in range(2)]
        pQ = [ps(f"pQ{i}", [P, 512]) for i in range(2)]
        pV = [ps(f"pV{i}", [P, 512]) for i in range(2)]
        pR = [ps(f"pR{i}", [P, 512]) for i in range(2)]

        x_in = [sem(f"x_in{b}") for b in range(B)]
        w_in, c_in, b_in, b3_in = sem("w_in"), sem("c_in"), sem("b_in"), sem("b3_in")
        id_ok, ones_ok, bp_ok = sem("id_ok"), sem("ones_ok"), sem("bp_ok")
        b0_ok, brest_ok, stats_ok = sem("b0_ok"), sem("brest_ok"), sem("stats_ok")
        dve_own, pool_own = sem("dve_own_a"), sem("pool_own_a")
        var_ok, std_ok = sem("var_ok"), sem("std_ok")
        xn_ok, xT_ok, xt_ok = sem("xn_ok"), sem("xT_ok"), sem("xt_ok")
        qk_ok, qks_ok, vg_ok, vs_ok = sem("qk_ok"), sem("qks_ok"), sem("vg_ok"), sem("vs_ok")
        rc_ok, rs_ok, qr_ok, qrT_ok = sem("rc_ok"), sem("rs_ok"), sem("qr_ok"), sem("qrT_ok")
        p1_ok, r1_ok, p2_ok, p3_ok = sem("p1_ok"), sem("r1_ok"), sem("p2_ok"), sem("p3_ok")
        st_out = [sem(f"st_out{i}") for i in range(2)]
        v_out = [sem(f"v_out{i}") for i in range(2)]
        xn_out = [sem(f"xn_out{i}") for i in range(4)]
        lg_ok, ex_ok, ex_used = sem("lg_ok"), sem("ex_ok"), sem("ex_used")
        sel_ok, mats_ok = sem("sel_ok"), sem("mats_ok")
        passed, passed_dve = sem("passed_a"), sem("passed_dve_a")
        block = ctx.enter_context(nc.Block())

        x_tiles = x.rearrange("b (n p) c -> b p n c", p=P)

        TURN, PROJ, ROT, BACK, SPLIT = 2, 3, 4, 6, 7

        @block.sync
        def _(sp):
            sp.dma_start(brow[:, 0:3 * C], b_qkv.rearrange("(a c) -> a c", a=1)).then_inc(b_in, 16)
            sp.dma_start(xs[:, 0:TPB, :], x_tiles[0]).then_inc(x_in[0], 16)
            sp.dma_start(wsb[:], w_qkvg.rearrange("(c p) n -> p c n", p=P)).then_inc(w_in, 16)
            for b in range(1, B):
                sp.dma_start(xs[:, b * TPB:(b + 1) * TPB, :], x_tiles[b]).then_inc(x_in[b], 16)
            sp.dma_start(ropesb[:], rope.rearrange("(n p) a d -> p n a d", p=P)).then_inc(c_in, 16)
            sp.wait_ge(bp_ok, 3)
            for n in range(3):
                sp.dma_start(bias3[n:n + 1, :], bparts[n][:]).then_inc(b3_in, 16)

            def store_xn(k, t, b):
                sp.wait_ge(xn_ok, k + 1)
                sp.dma_start(s_xn[bass.ds(k * P, P), :], xn[:, t % 4, :]).then_inc(xn_out[t % 4], 16)

            def store_v(k, t, b):
                sp.wait_ge(vs_ok, k + 1)
                sp.dma_start(s_v[bass.ds(k * P, P), :, :], vst[:, t % 2, :, :]).then_inc(v_out[t % 2], 16)

            def store_parts(k, t, b):
                if isinstance(k, int) and k == NT - SPLIT + 1:
                    for i in range(2):
                        sp.wait_ge(st_out[i], 12 * 16 * (B - 1))
                    load_operands(sp, s_q, s_k, first["qt"], first["kt"], 0, first["qk_in"])
                if t % 4 != 3:
                    return
                hh = t // 4
                sp.wait_ge(p3_ok, k + 1)
                sp.wait_ge(p2_ok, k + 1)
                for part in range(3):
                    for blk in range(4):
                        heads = slice((blk % 2) * H // 2, (blk % 2 + 1) * H // 2)
                        if blk < 2:
                            dst = s_q[hh, bass.ds(b, 1), part, :, heads, :]
                        else:
                            dst = s_k[bass.ds(b, 1), part, :, heads, hh * QH:(hh + 1) * QH]
                        sp.dma_start(dst.rearrange("b d h t -> (b h) d t"), stg[:, hh, part, blk, :])\
                            .then_inc(st_out[hh], 16)

            steps(sp, B, TPB, NT, [(0, store_xn), (PROJ, store_v), (SPLIT, store_parts)])
            for i in range(2):
                sp.wait_ge(v_out[i], 16 * NT // 2)
            load_values(sp, s_v, first["vt"], 0, 0, first["v_in"])
            for i in range(2):
                sp.wait_ge(st_out[i], 12 * 16 * B)
                sp.wait_ge(xn_out[2 * i], 16 * NT // 4)
                sp.wait_ge(xn_out[2 * i + 1], 16 * NT // 4)

        @block.gpsimd
        def _(pool):
            own = Chain(pool, pool_own)
            own.link(nc.gpsimd.memset(ident[:], 0.0))
            nc.gpsimd.affine_select(out=ident[:], in_=ident[:], compare_op=ALU.not_equal, fill=1.0, base=0,
                                    pattern=[[-1, P]], channel_multiplier=1).then_inc(id_ok, 1)
            nc.gpsimd.memset(ones3[:], 1.0).then_inc(ones_ok, 1)
            nc.gpsimd.memset(vst[:], 1.0).then_inc(ones_ok, 1)
            nc.gpsimd.memset(keep["ones"][:], 1.0).then_inc(mats_ok, 1)
            below = keep["below"]
            own.link(nc.gpsimd.memset(below[:], 1.0))
            nc.gpsimd.affine_select(out=below[:], in_=below[:], compare_op=ALU.is_gt, fill=0.0, base=0,
                                    pattern=[[1, P]], channel_multiplier=-1).then_inc(mats_ok, 1)
            pool.wait_ge(mats_ok, 2)
            nc.gpsimd.memset(first["kt"][KR:KR + MR, :, :], 1.0).then_inc(mats_ok, 1)
            pool.wait_ge(mats_ok, 3)
            pool.wait_ge(c_in, 16)

            def sines(k, t, b):
                sl = t % 2
                pool.wait_ge(qks_ok, k + 1)
                need(pool, qr_ok, k - 1)
                src = qks[:, sl, :].rearrange("p (h d) -> p h d", d=D)
                dst = rs[:, sl, :].rearrange("p (h d) -> p h d", d=D)
                sn = ropesb[:, t, 1:2, :]
                hd = D // 2
                nc.gpsimd.tensor_tensor(dst[:, :, 0:hd], src[:, :, hd:D],
                                        sn[:, :, 0:hd].to_broadcast([P, 2 * H, hd]), ALU.mult)
                nc.gpsimd.tensor_tensor(dst[:, :, hd:D], src[:, :, 0:hd],
                                        sn[:, :, hd:D].to_broadcast([P, 2 * H, hd]), ALU.mult).then_inc(rs_ok, 1)
                nc.gpsimd.tensor_tensor(rc[:, sl, :].rearrange("p (h d) -> p h d", d=D), src,
                                        ropesb[:, t, 0:1, :].to_broadcast([P, 2 * H, D]), ALU.mult).then_inc(rc_ok, 1)

            def part3(k, t, b):
                sl, hh, c0 = t % 2, t // 4, (t % 4) * P
                pool.wait_ge(p2_ok, k + 1)
                nc.gpsimd.tensor_tensor(stg[:, hh, 2, :, c0:c0 + P], r1[:, sl, :, :],
                                        stg[:, hh, 1, :, c0:c0 + P], ALU.subtract).then_inc(p3_ok, 1)

            steps(pool, B, TPB, NT, [(SPLIT, part3), (PROJ, sines)])

        @block.vector
        def _(dve):
            own = Chain(dve, dve_own)
            v = nc.vector
            v.memset(brow[:, 3 * C:W], 0.0).then_inc(b0_ok, 1)
            dve.wait_ge(bp_ok, 1)
            dve.wait_ge(b_in, 16)
            dve.wait_ge(b0_ok, 1)
            v.tensor_tensor(brest[:], brow[:], bparts[0][:], ALU.subtract).then_inc(brest_ok, 1)
            dve.wait_ge(bp_ok, 2)
            dve.wait_ge(brest_ok, 1)
            v.tensor_tensor(bparts[2][:], brest[:], bparts[1][:], ALU.subtract).then_inc(bp_ok, 1)

            def spread(t0, t1):
                for t in range(t0, t1):
                    last = v.bn_aggr(mv[:, t, :], bnst[:, t, :])
                own.link(last)
                v.tensor_scalar(var[:, t0:t1], mv[:, t0:t1, 1], EPS, None, ALU.add).then_inc(var_ok, 1)

            def inverse_root(t0, t1, n):
                dve.wait_ge(std_ok, n)
                r_, w_, v_ = rstd[:, t0:t1], nwt[:, t0:t1], var[:, t0:t1]
                own.link(v.reciprocal(r_, std[:, t0:t1]))
                own.link(v.tensor_tensor(w_, r_, r_, ALU.mult))
                own.link(v.tensor_tensor(w_, w_, v_, ALU.mult))
                own.link(v.tensor_scalar(w_, w_, -0.5, 1.5, ALU.mult, ALU.add))
                own.link(v.tensor_tensor(r_, r_, w_, ALU.mult))

            dve.wait_ge(x_in[0], 16)
            for t in range(TPB):
                last = v.bn_stats(bnst[:, t, :], xs[:, t, :])
            own.link(last)
            spread(0, TPB)
            inverse_root(0, TPB, 1)
            own.link(v.memset(gb["lt4"][:], 0.0))
            for n in ("bq", "a", "c", "ex2"):
                own.link(v.memset(gb[n][:, :, 0:PAD], 0.0))
            for g in range(1, G):
                own.link(v.memset(gb["lt4"][:, g, 0:g], 1.0))
            for n in range(TOPK):
                own.link(v.memset(gb["kth"][:, n:n + 1], n + 1.0))
            dve.wait_ge(c_in, 16)
            setup = own.n

            def other_stats(k, t, b):
                if not isinstance(k, int):
                    return
                if t < 6:
                    for n in range(TPB + 4 * t, TPB + 4 * t + 4):
                        dve.wait_ge(x_in[n // TPB], 16)
                        last = v.bn_stats(bnst[:, n, :], xs[:, n, :])
                    if t == 5:
                        last.then_inc(stats_ok, 1)
                if t == 6:
                    dve.wait_ge(stats_ok, 1)
                    for n in range(TPB, NT):
                        last = v.bn_aggr(mv[:, n, :], bnst[:, n, :])
                    last.then_inc(stats_ok, 1)
                    dve.wait_ge(stats_ok, 2)
                    v.tensor_scalar(var[:, TPB:NT], mv[:, TPB:NT, 1], EPS, None, ALU.add).then_inc(var_ok, 1)
                if t == 7:
                    own.base, own.n = setup, 0
                    inverse_root(TPB, NT, 2)

            def normalise(k, t, b):
                need(dve, xT_ok, k - 3)
                need(dve, xn_out[t % 4], (b * TPB // 4 + t // 4) * 16)
                pick = lambda a: a.rearrange("p a b -> p (a b)")
                v.tensor_scalar(xn[:, t % 4, :], pick(xs[:, bass.ds(k, 1), :]),
                                pick(mv[:, bass.ds(k, 1), 0:1]), rstd[:, bass.ds(k, 1)],
                                ALU.subtract, ALU.mult).then_inc(xn_ok, 1)

            def rotate(k, t, b):
                dve.wait_ge(rc_ok, k + 1)
                dve.wait_ge(rs_ok, k + 1)
                need(dve, qrT_ok, k - 1)
                v.tensor_tensor(qr[:, t % 2, :], rc[:, t % 2, :], rs[:, t % 2, :], ALU.add).then_inc(qr_ok, 1)

            def rest(k, t, b):
                dve.wait_ge(p1_ok, k + 1)
                need(dve, p3_ok, k - 1)
                need(dve, p2_ok, k - 1)
                c0 = (t % 4) * P
                v.tensor_tensor(r1[:, t % 2, :, :], pR[t % 2][:, :].rearrange("p (k n) -> p k n", k=4),
                                stg[:, t // 4, 0, :, c0:c0 + P], ALU.subtract).then_inc(r1_ok, 1)

            def routing(k, t, b):
                if t == 3:
                    own.base, own.n = setup + ROOT_LINKS + b * ROUTE_LINKS, 0
                for piece in {3: (0, 1), 4: (2, 3), 5: (4, 5), 6: (6,), 7: (7,)}.get(t, ()):
                    route(nc, dve, own, gb, keep, b, piece, ex_ok, ex_used, sel_ok, passed_dve)
                assert t != TPB - 1 or own.n == ROUTE_LINKS, own.n

            steps(dve, B, TPB, NT, [(0, normalise), (0, other_stats), (BACK, rest), (ROT, rotate), (TPB, routing)])
            own.base, own.n = setup + ROOT_LINKS + B * ROUTE_LINKS, 0
            dve.wait_ge(sel_ok, B)
            own.link(v.tensor_reduce(keep["cntf"][:], keep["sel"][:].rearrange("p n e -> p e n"), AX.X, ALU.add))
            v.tensor_copy(keep["cnt"][:], keep["cntf"][:])

        @block.scalar
        def _(act):
            act.wait_ge(b_in, 16)
            act.wait_ge(b0_ok, 1)
            nc.scalar.activation(bparts[0][:], brow[:], ACT.Copy).then_inc(bp_ok, 1)
            act.wait_ge(brest_ok, 1)
            nc.scalar.activation(bparts[1][:], brest[:], ACT.Copy).then_inc(bp_ok, 1)
            act.wait_ge(ones_ok, 2)
            act.wait_ge(var_ok, 1)
            nc.scalar.activation(std[:, 0:TPB], var[:, 0:TPB], ACT.Sqrt).then_inc(std_ok, 1)

            def root(k, t, b):
                if isinstance(k, int) and t == 6:
                    act.wait_ge(var_ok, 2)
                    nc.scalar.activation(std[:, TPB:NT], var[:, TPB:NT], ACT.Sqrt).then_inc(std_ok, 1)

            def turn(k, t, b):
                act.wait_ge(xT_ok, k + 1)
                need(act, vg_ok, k - 1)
                nc.scalar.activation(xt[:, t % 2, :, :], pT[t % 2][:, 0:C].rearrange("p (c n) -> p c n", c=CC),
                                     ACT.Copy).then_inc(xt_ok, 1)

            def take(k, t, b):
                act.wait_ge(qk_ok, k + 1)
                need(act, qr_ok, k - 1)
                nc.scalar.activation(qks[:, t % 2, :], pQ[t % 2][:, :], ACT.Copy).then_inc(qks_ok, 1)
                act.wait_ge(vg_ok, k + 1)
                need(act, v_out[t % 2], (b * TPB // 2 + t // 2) * 16)
                nc.scalar.activation(vst[:, t % 2, :, 0:D],
                                     pV[t % 2][:, 0:C].rearrange("p (h d) -> p h d", d=D), ACT.Copy)\
                    .then_inc(vs_ok, 1)
                nc.scalar.activation(lg[:, bass.ds(k, 1), :], pV[t % 2][:, C:C + E].unsqueeze(1), ACT.Copy)\
                    .then_inc(lg_ok, 1)
                if t == TPB - 1:
                    act.wait_ge(lg_ok, k + 1)
                    need(act, ex_used, b)
                    nc.scalar.activation(gb["ex"][:], lg[:, bass.ds(b * TPB, TPB), :], ACT.Exp, scale=-1.0)\
                        .then_inc(ex_ok, 1)

            def part1(k, t, b):
                act.wait_ge(qrT_ok, k + 1)
                if t % 4 == 0:
                    need(act, st_out[t // 4], b * 12 * 16)
                c0 = (t % 4) * P
                nc.scalar.activation(stg[:, t // 4, 0, :, c0:c0 + P],
                                     pR[t % 2][:, :].rearrange("p (k n) -> p k n", k=4), ACT.Copy)\
                    .then_inc(p1_ok, 1)

            def part2(k, t, b):
                act.wait_ge(r1_ok, k + 1)
                c0 = (t % 4) * P
                nc.scalar.activation(stg[:, t // 4, 1, :, c0:c0 + P], r1[:, t % 2, :, :], ACT.Copy).then_inc(p2_ok, 1)

            steps(act, B, TPB, NT, [(0, root), (BACK, part1), (TURN, turn), (SPLIT, part2), (PROJ, take)])

        @block.tensor
        def _(pe):
            pe.wait_ge(id_ok, 1)
            pe.wait_ge(ones_ok, 1)
            pe.wait_ge(w_in, 16)
            pe.wait_ge(b3_in, 48)

            def turn(k, t, b):
                pe.wait_ge(xn_ok, k + 1)
                need(pe, xt_ok, k - 1)
                for c in range(CC):
                    mm = pe.transpose(pT[t % 2][:, c * P:(c + 1) * P], xn[:, t % 4, c * P:(c + 1) * P], ident[:])
                mm.then_inc(xT_ok, 1)

            def project(k, t, b):
                pe.wait_ge(xt_ok, k + 1)
                need(pe, qks_ok, k - 1)
                pe.matmul(pQ[t % 2][:, :], ones3[:], bias3[:, 0:2 * C], start=True, stop=False)
                for c in range(CC):
                    mm = pe.matmul(pQ[t % 2][:, :], xt[:, t % 2, c, :], wsb[:, c, 0:2 * C],
                                   start=False, stop=(c == CC - 1))
                mm.then_inc(qk_ok, 1)
                need(pe, lg_ok, k - 1)
                pe.matmul(pV[t % 2][:, 0:C + E], ones3[:], bias3[:, 2 * C:W], start=True, stop=False)
                for c in range(CC):
                    mm = pe.matmul(pV[t % 2][:, 0:C + E], xt[:, t % 2, c, :], wsb[:, c, 2 * C:W],
                                   start=False, stop=(c == CC - 1))
                mm.then_inc(vg_ok, 1)

            def back(k, t, b):
                pe.wait_ge(qr_ok, k + 1)
                need(pe, r1_ok, k - 1)
                for blk in range(4):
                    mm = pe.transpose(pR[t % 2][:, blk * P:(blk + 1) * P], qr[:, t % 2, blk * P:(blk + 1) * P],
                                      ident[:])
                mm.then_inc(qrT_ok, 1)

            steps(pe, B, TPB, NT, [(BACK, back), (TURN, turn), (PROJ, project)])


ROOT_LINKS, ROUTE_LINKS = 5, 42


PAD = 8


def route(nc, dve, own, gb, keep, b, piece, ex_ok, ex_used, sel_ok, passed):
    v = nc.vector
    tt = lambda o, x, y, op: own.link(v.tensor_tensor(o, x, y, op))
    bc = lambda a, shape: a.to_broadcast(shape)
    hi, lo, gs = gb["hi"], gb["lo"], gb["gs"]
    rows = bass.ds(b * TPB, TPB)
    if piece == 0:
        dve.wait_ge(ex_ok, b + 1)
        own.link(v.tensor_scalar(gb["sc"][:], gb["ex"][:], 1.0, None, ALU.add))
        v.reciprocal(gb["sc"][:], gb["sc"][:]).then_inc(ex_used, 1)
        dve.wait_ge(ex_used, b + 1)
        s2 = gb["sc"][:].rearrange("p n (g q r) -> p (n g) q r", g=G, q=2)
        tt(hi[:], s2[:, :, :, 0], s2[:, :, :, 1], ALU.max)
        tt(lo[:], s2[:, :, :, 0], s2[:, :, :, 1], ALU.min)
    if piece == 1:
        tt(gb["m1"][:], hi[:, :, 0], hi[:, :, 1], ALU.max)
        tt(gb["m2"][:], hi[:, :, 0], hi[:, :, 1], ALU.min)
        tt(lo[:, :, 0], lo[:, :, 0], lo[:, :, 1], ALU.max)
        tt(gb["m2"][:], gb["m2"][:], lo[:, :, 0], ALU.max)
        tt(gs[:].rearrange("p n g -> p (n g)"), gb["m1"][:], gb["m2"][:], ALU.add)
    if piece == 2:
        mine = bc(gs[:].unsqueeze(3), [P, TPB, G, G])
        other = bc(gs[:].unsqueeze(2), [P, TPB, G, G])
        tt(gb["gt"][:], other, mine, ALU.is_gt)
        tt(gb["ge"][:], other, mine, ALU.is_equal)
        tt(gb["ge"][:], gb["ge"][:], bc(gb["lt4"][:].unsqueeze(1), [P, TPB, G, G]), ALU.mult)
        tt(gb["gt"][:], gb["gt"][:], gb["ge"][:], ALU.add)
        own.link(v.tensor_reduce(gb["rank"][:], gb["gt"][:], AX.X, ALU.add))
        own.link(v.tensor_scalar(gb["ok"][:], gb["rank"][:], float(TOPG), None, ALU.is_lt))
    if piece == 3:
        ok = bc(gb["ok"][:].unsqueeze(3), [P, TPB, G, E // G])
        g4 = lambda n: gb[n][:].rearrange("p n (g q) -> p n g q", g=G)
        tt(g4("ms"), g4("sc"), ok, ALU.mult)
        own.link(v.tensor_scalar(gb["ok"][:], gb["ok"][:], -1.0, None, ALU.add))
        own.link_alone(v.tensor_tensor(g4("ms"), g4("ms"), ok, ALU.add), passed)
        for t in range(TPB):
            last = v.max(gb["top"][:, t, :], gb["ms"][:, t, :])
        own.link(last)
    if piece == 4:
        fourth = bc(gb["top"][:, :, TOPK - 1:TOPK], [P, TPB, E])
        tt(gb["a"][:, :, PAD:], gb["ms"][:], fourth, ALU.is_gt)
        tt(gb["bq"][:, :, PAD:], gb["ms"][:], fourth, ALU.is_equal)
        own.link(v.tensor_reduce(gb["cnt"][:], gb["a"][:, :, PAD:], AX.X, ALU.add))
        own.link(v.tensor_scalar(gb["cnt"][:], gb["cnt"][:], -1.0, float(TOPK), ALU.mult, ALU.add))
    if piece == 5:
        running_count(v, own, gb, "bq")
        tt(gb["c"][:, :, PAD:], gb["ms"][:], bc(gb["cnt"][:].unsqueeze(2), [P, TPB, E]), ALU.is_le)
        tt(gb["bq"][:, :, PAD:], gb["bq"][:, :, PAD:], gb["c"][:, :, PAD:], ALU.mult)
        tt(gb["a"][:, :, PAD:], gb["a"][:, :, PAD:], gb["bq"][:, :, PAD:], ALU.add)
        v.tensor_copy(keep["sel"][:, rows, :], gb["a"][:, :, PAD:]).then_inc(sel_ok, 1)
    if piece == 6:
        running_count(v, own, gb, "a")
        mk, k3 = keep["mk"][:, rows, :, :], [P, TPB, TOPK, E]
        own.link(v.tensor_tensor(gb["mw"][:], bc(gb["ms"][:].unsqueeze(2), k3),
                                 bc(gb["kth"][:].unsqueeze(1).unsqueeze(3), k3), ALU.is_equal))
        tt(mk, gb["mw"][:], bc(gb["a"][:, :, PAD:].unsqueeze(2), k3), ALU.mult)
    if piece == 7:
        k3 = [P, TPB, TOPK, E]
        tt(gb["a"][:, :, PAD:], gb["a"][:, :, PAD:], gb["sc"][:], ALU.mult)
        own.link(v.tensor_reduce(gb["ws"][:], gb["a"][:, :, PAD:], AX.X, ALU.add))
        own.link(v.tensor_scalar(gb["ws"][:], gb["ws"][:], 1e-6, None, ALU.add))
        own.link(v.reciprocal(gb["ws"][:], gb["ws"][:]))
        tt(gb["a"][:, :, PAD:], gb["a"][:, :, PAD:], bc(gb["ws"][:].unsqueeze(2), [P, TPB, E]), ALU.mult)
        tt(gb["mw"][:], keep["mk"][:, rows, :, :], bc(gb["a"][:, :, PAD:].unsqueeze(2), k3), ALU.mult)
        own.link(v.tensor_reduce(keep["wk"][:, rows, :], gb["mw"][:], AX.X, ALU.add))


def running_count(v, own, gb, name):
    for sh, src, dst in ((1, name, "c"), (2, "c", "ex2"), (4, "ex2", "c"), (8, "c", "ms")):
        to = gb[dst][:] if dst == "ms" else gb[dst][:, :, PAD:]
        own.link(v.tensor_tensor(to, gb[src][:, :, PAD:], gb[src][:, :, PAD - sh:PAD - sh + E], ALU.add))


QUADS = 16
KC = T // P
LOAD = 16 * 9


AHEAD = 20
SWITCH = (32 - AHEAD) // 2
ROWS1, ROWS0 = SWITCH, SWITCH + 8
def halve(nc, own, a, width):
    while width > 1:
        width //= 2
        own.link(nc.gpsimd.tensor_tensor(a[..., 0:width], a[..., 0:width], a[..., width:2 * width], ALU.add))


def plan_counters(nc, own, plan, s_idx, zero_out, counters_ok):
    g = nc.gpsimd
    own.link(g.memset(plan["zero"][:], 0.0))
    g.dma_start(s_idx.rearrange("(p n) a -> p (n a)", p=P), plan["zero"][:]).then_inc(zero_out, 16)
    own.link(g.iota(plan["itok"][:], [[P, NT]], base=0, channel_multiplier=1))
    own.link(g.tensor_copy(plan["tok"][:], plan["itok"][:]))
    own.link(g.iota(plan["itile"][:], [[P, 2]], base=0, channel_multiplier=1))
    own.link(g.tensor_copy(plan["tile"][:], plan["itile"][:]))
    own.link(g.iota(plan["ifull"][:], [[P, NT]], base=0, channel_multiplier=0))
    g.tensor_copy(plan["filled"][:], plan["ifull"][:]).then_inc(counters_ok, 1)


def plan_counts(nc, own, plan, keep, counters_ok, nt_ok):
    full = [P, E, NT]
    own.eng.wait_ge(counters_ok, 1)
    own.link(nc.vector.tensor_tensor(plan["full"][:], keep["tot"][:].unsqueeze(2).to_broadcast(full),
                                     plan["filled"][:].unsqueeze(1).to_broadcast(full), ALU.is_gt))
    nc.vector.tensor_reduce(plan["nt"][:], plan["full"][:], AX.X, ALU.add).then_inc(nt_ok, 1)


def plan_offsets(nc, own, plan, nt_ok, sums_ok):
    g = nc.gpsimd
    wait_alone(own.eng, nt_ok, 1, own.passed)
    for sh, src, dst in ((1, "nt", "c0"), (2, "c0", "c1"), (4, "c1", "c0"), (8, "c0", "c1")):
        own.link(g.tensor_copy(plan[dst][:, 0:sh], plan[src][:, 0:sh]))
        own.link(g.tensor_tensor(plan[dst][:, sh:E], plan[src][:, sh:E], plan[src][:, 0:E - sh], ALU.add))
    own.link(g.tensor_tensor(plan["off"][:], plan["c1"][:], plan["nt"][:], ALU.subtract))
    own.link(g.tensor_scalar(plan["off"][:], plan["off"][:], float(P), 0.0, ALU.mult, ALU.add))
    own.eng.sem_inc(sums_ok, 1)


def plan_places(nc, own, plan, keep):
    g = nc.gpsimd
    shape = [P, NT, TOPK, E]
    own.link(g.tensor_tensor(plan["pos"][:], keep["pre"][:], plan["off"][:].unsqueeze(1).to_broadcast([P, NT, E]),
                             ALU.add))
    own.link(g.tensor_tensor(plan["prod"][:], keep["mk"][:], plan["pos"][:].unsqueeze(2).to_broadcast(shape),
                             ALU.mult))
    halve(nc, own, plan["prod"][:], E)
    own.link(g.tensor_copy(keep["where"][:].rearrange("p (n k) -> p n k", k=TOPK), plan["prod"][:, :, :, 0]))


def plan_tiles(nc, own, plan, sums_ok, eid_ok):
    shape = [P, 2, E]
    own.eng.wait_ge(sums_ok, 1)
    own.link(nc.vector.tensor_tensor(plan["le"][:], plan["c1"][:].unsqueeze(1).to_broadcast(shape),
                                     plan["tile"][:].unsqueeze(2).to_broadcast(shape), ALU.is_le))
    own.link(nc.vector.tensor_reduce(plan["eidf"][:], plan["le"][:], AX.X, ALU.add))
    nc.vector.tensor_scalar(plan["eidc"][:], plan["eidf"][:], float(E - 1), None, ALU.min).then_inc(eid_ok, 1)


Q_RUNS = [(0, 1, 3), (1, 1, 2), (2, 1, 1)]
K_RUNS = [(0, 3, 1), (0, 2, 1), (0, 1, 1)]


def load_operands(eng, s_q, s_k, qt, kt, gi, done):
    for src, dst, runs in ((s_q[0], qt[:, 0, :, :], Q_RUNS), (s_q[1], qt[:, 1, :, :], Q_RUNS), (s_k, kt, K_RUNS)):
        row = 0
        for part, count, rep in runs:
            heads = bass.ds(gi % 4 * HG, HG)
            parts = src[bass.ds(gi // 4, 1), part:part + count, :, heads, :].rearrange("b a d h t -> (b a) d (h t)")
            if rep > 1:
                parts = parts.to_broadcast([rep, D, parts.shape[2]])
            end = row + count * rep * D
            eng.dma_start(dst[row:end], parts).then_inc(done, 16)
            row = end


def load_values(eng, s_v, vt, j, gg, done):
    eng.dma_start(vt[:, :, :], s_v[bass.ds((j // 2) * T, T), bass.ds((j % 2) * 2 * HG + gg * HG, HG), :]
                  .rearrange("(n p) h w -> p n (h w)", p=P)).then_inc(done, 16)


def stage_b(nc, s_q, s_k, s_v, s_o, s_idx, w13, w2, w_out, b_out, keep, first):
    with ExitStack() as ctx:
        sb = lambda n, s, d=F32: ctx.enter_context(nc.sbuf_tensor(n, s, d))
        sem = lambda n: ctx.enter_context(nc.semaphore(n))
        qt = [first["qt"], sb("qt1", [P, 2, HG, QH], BF16)]
        kt = [first["kt"], sb("kt1", [P, HG, T], BF16)]
        vt = [first["vt"], sb("vt1", [P, KC, HG * VW])]
        pr = sb("pr", [P, 8, QH])
        mx = sb("mx", [P, 2, 16])
        mrest = sb("mrest", [P, 16])
        mp = sb("mp", [P, 2, 3, 16], BF16)
        mrow = sb("mrow", [48, 2, P], BF16)
        osb = sb("osb", [P, QH])
        rec = sb("rec", [P, 16])
        on = sb("on", [P, 2, 4, HG, D])
        identb = sb("identb", [P, P], BF16)
        ident = keep["ident"]

        pm = [ctx.enter_context(nc.psum_tensor(f"pm{i}", [P, 2, 512], F32)) for i in range(2)]
        pst = [ctx.enter_context(nc.psum_tensor(f"pst{i}", [P, 512], F32)) for i in range(2)]
        po = [ctx.enter_context(nc.psum_tensor(f"po{i}", [P, 512], F32)) for i in range(2)]

        id_ok, row1_ok, po_ok = sem("idb_ok"), sem("row1_ok"), sem("po_ok")
        qk_in = [first["qk_in"], sem("qk_in1")]
        v_in = [first["v_in"], sem("v_in1")]
        pre_ok, keep_ok = sem("pre_ok"), sem("keep_ok")
        st_ok, exp_ok, pv_ok = sem("st_ok"), sem("exp_ok"), sem("pv_ok")
        mx_full, mx_free = sem("mx_full"), sem("mx_free")
        mp_ok = sem("mp_ok")
        mrow_in = [sem(f"mrow_in{i}") for i in range(2)]
        osb_ok, rec_ok = sem("osb_ok"), sem("rec_ok")
        o_out = [sem(f"o_out{i}") for i in range(2)]
        pool_own, passed = sem("pool_own_b"), sem("passed_b")
        plan = {n: sb("p_" + n, sh, d) for n, sh, d in (
            ("zero", [P, NX], F32), ("itok", [P, NT], I32), ("tok", [P, NT], F32), ("itile", [P, 2], I32),
            ("tile", [P, 2], F32), ("ifull", [P, NT], I32), ("full", [P, E, NT], F32), ("c0", [P, E], F32),
            ("c1", [P, E], F32), ("nt", [P, E], F32), ("off", [P, E], F32), ("pos", [P, NT, E], F32),
            ("prod", [P, NT, TOPK, E], F32),
            ("le", [P, 2, E], F32), ("eidf", [P, 2], F32), ("eidc", [P, 2], I32), ("filled", [P, NT], F32),
            ("slot", [P, 2, TOPK], U32), ("data", [P, 2], F32))}
        plan_own, zero_out, slot_ok = sem("plan_own"), sem("zero_out"), sem("slot_ok")
        eid_ok, eid_in = sem("eid_ok"), sem("eid_in")
        counters_ok, nt_ok, sums_ok, plan_dve = sem("counters_ok"), sem("nt_ok"), sem("sums_ok"), sem("plan_dve")
        plan_out = [sem(f"plan_out{i}") for i in range(2)]
        block = ctx.enter_context(nc.Block())

        def uses(k):
            tasks = [(AHEAD + 2 * k + i) % 32 for i in range(2)]
            more = {2: ["out"], 10: ["out"], ROWS1: ["rows"], ROWS0: ["rows"]}.get(k, [])
            return tasks + more
        FIRST = AHEAD + 1
        FIRST_ROWS = 18
        before = [sum(len(uses(i)) for i in range(k)) for k in range(QUADS + 1)]
        PER = before[QUADS]

        def place(g, k, i):
            return FIRST + g * PER + before[k] + i

        @block.sync
        def _(sp):
            def load(buf, gi):
                load_operands(sp, s_q, s_k, qt[buf], kt[buf], gi, qk_in[buf])

            def load_v(buf, j, gg):
                load_values(sp, s_v, vt[buf], j, gg, v_in[buf])

            def rows(use, half, buf):
                sp.wait_ge(mx_free, use + 1)
                sp.dma_start(qt[buf][KR:KR + MR, half, :, :], mrow[:, half, :]).then_inc(mrow_in[half], 16)

            def store(use, half, j, gg):
                sp.wait_ge(mx_free, use + 1)
                dst = s_o[bass.ds((j // 2) * T + half * QH, QH), bass.ds((j % 2) * 2 * GR + gg * GR, GR)]
                sp.dma_start(dst.rearrange("(n p) c -> p n c", p=P),
                             on[:, half, :, :, :].rearrange("p n h d -> p n (h d)")).then_inc(o_out[half], 16)

            load(1, 1)
            load_v(1, 0, 1)
            rows(FIRST_ROWS, 0, 0)

            def body(j):
                for gg in range(2):
                    g = j * 2 + gg
                    if not (isinstance(g, int) and g == 0):
                        sp.wait_ge(st_ok, g * 64)
                        load(1 - gg, (g + 1) % NG)
                        sp.wait_ge(pv_ok, g * QUADS)
                        load_v(1 - gg, (j + gg) % (NG // 2), 1 - gg)
                    if gg == 1:
                        store(place(g, 2, 2), 1, j, 0)
                    elif not (isinstance(j, int) and j == 0):
                        store(place(g, 2, 2), 1, j - 1, 1)
                    rows(place(g, ROWS1, 2), 1, gg)
                    if isinstance(g, int):
                        weights(g)
                    store(place(g, 10, 2), 0, j, gg)
                    rows(place(g, ROWS0, 2), 0, 1 - gg)

            def weights(g):
                w_in = keep["w_in"]
                if g == 0:
                    sp.wait_ge(eid_ok, 1)
                    for n in range(2):
                        sp.dma_start(keep["eid"][0:1, n * P:(n + 1) * P], plan["eidc"][:, n:n + 1])\
                            .then_inc(eid_in, 16)
                    sp.dma_start(keep["w13"][:], w13.rearrange("(c p) e n -> p c e n", p=P)).then_inc(w_in, 16)
                    return
                sp.dma_start(keep["w2"][:], w2).then_inc(w_in, 16)
                sp.dma_start(keep["w_out"][:], w_out.rearrange("(c p) n -> p c n", p=P)).then_inc(w_in, 16)
                sp.dma_start(keep["b_out"][:], b_out.rearrange("(a c) -> a c", a=1).to_broadcast([P, C]))\
                    .then_inc(w_in, 16)

            rounds(sp, NG // 2, body)
            for i in range(2):
                sp.wait_ge(plan_out[i], 64 * NT // 2)
            sp.dma_start(keep["idf"][:], s_idx.rearrange("(q a p) o -> a q (p o)", q=2, p=P)).then_inc(keep["idf_in"], 16)
            store(FIRST + NG * PER, 1, NG // 2 - 1, 1)
            for i in range(2):
                sp.wait_ge(o_out[i], 16 * NG)
            sp.wait_ge(mrow_in[0], 16 * (NG + 1))
            sp.wait_ge(eid_in, 32)

        @block.gpsimd
        def _(pool):
            own = Chain(pool, pool_own, passed)
            own.link(nc.gpsimd.memset(identb[:], 0.0))
            nc.gpsimd.affine_select(out=identb[:], in_=identb[:], compare_op=ALU.not_equal, fill=1.0, base=0,
                                    pattern=[[-1, P]], channel_multiplier=1).then_inc(id_ok, 1)
            wait_alone(pool, id_ok, 1, passed)
            nc.gpsimd.memset(kt[1][KR:KR + MR, :, :], 1.0).then_inc(row1_ok, 1)
            wait_alone(pool, row1_ok, 1, passed)
            start = own.n
            planned = Chain(pool, plan_own, passed)
            plan_counters(nc, planned, plan, s_idx, zero_out, counters_ok)

            def split(n, half, last_use):
                own.base, own.n = start + n * 4, 0
                wait_alone(pool, mx_free, last_use + 1, passed)
                own.link(nc.gpsimd.tensor_scalar(mp[:, half, 0, :], mx[:, half, :], -1.0, 0.0, ALU.mult, ALU.add))
                own.link(nc.gpsimd.tensor_tensor(mrest[:], mx[:, half, :], mp[:, half, 0, :], ALU.add))
                own.link(nc.gpsimd.tensor_scalar(mp[:, half, 1, :], mrest[:], -1.0, 0.0, ALU.mult, ALU.add))
                own.link(nc.gpsimd.tensor_tensor(mrest[:], mrest[:], mp[:, half, 1, :], ALU.add))
                nc.gpsimd.tensor_scalar(mp[:, half, 2, :], mrest[:], -1.0, 0.0, ALU.mult, ALU.add).then_inc(mp_ok, 1)


            def send(n, sl, uses):
                if not (isinstance(uses, int) and uses == 0):
                    wait_alone(pool, plan_out[sl], 64 * uses, passed)
                nc.gpsimd.tensor_copy(plan["slot"][:, sl, :], keep["where"][:, bass.ds(n * TOPK, TOPK)])\
                    .then_inc(slot_ok, 1)
                nc.gpsimd.tensor_copy(plan["data"][:, sl:sl + 1], plan["tok"][:, bass.ds(n, 1)]).then_inc(slot_ok, 1)
                wait_alone(pool, slot_ok, 2 * (n + 1), passed)
                for k in range(TOPK):
                    pool.indirect_dma_start(
                        out=s_idx, out_offset=bass.IndirectOffsetOnAxis(ap=plan["slot"][:, sl, k:k + 1], axis=0),
                        in_=plan["data"][:, sl:sl + 1], in_offset=None).then_inc(plan_out[sl], 16)

            split(0, 0, 15)
            plan_offsets(nc, planned, plan, nt_ok, sums_ok)

            def body(j):
                for gg in range(2):
                    g = j * 2 + gg
                    for half in (1, 0):
                        i = gg * 2 + 1 - half
                        split(2 * g + 2 - half, half, place(g, SWITCH - 1 if half else SWITCH + 7, 1))
                        if not isinstance(j, int):
                            send(4 * j + i, i % 2, 2 * j + i // 2)
                        elif i == 0:
                            wait_alone(pool, keep_ok, 2, passed)
                            plan_places(nc, planned, plan, keep)
                        elif i == 1:
                            wait_alone(pool, zero_out, 16, passed)
                        else:
                            for n in (2 * i - 4, 2 * i - 3):
                                send(n, n % 2, n // 2)
            rounds(pool, NG // 2, body)
            for i in range(2):
                wait_alone(pool, plan_out[i], 64 * NT // 2, passed)

        @block.scalar
        def _(act):
            def body(j):
                for gg in range(2):
                    g = j * 2 + gg
                    for k in range(QUADS):
                        q = g * QUADS + k
                        need(act, pv_ok, q - 1)
                        for i in range(4):
                            act.wait_ge(st_ok, q * 4 + i + 1)
                            nc.scalar.activation(pr[:, (k % 2) * 4 + i, :], pst[i % 2][:, :], ACT.Exp, scale=SCALE)\
                                .then_inc(exp_ok, 1)
                            if k % 8 == 1 and i == 1:
                                u = 2 * g + k // 8 - 1
                                if not (isinstance(u, int) and u < 0):
                                    take_o(u, (k // 8 + 1) % 2)

            def take_o(u, half):
                act.wait_ge(pv_ok, 8 * (u + 1))
                nc.scalar.activation(osb[:, :], po[half][:, :], ACT.Copy).then_inc(osb_ok, 1)

            act.wait_ge(pre_ok, 1)
            nc.scalar.activation(keep["tot"][:], pst[1][:, 0:E], ACT.Copy).then_inc(keep_ok, 1)
            act.wait_ge(pre_ok, 2)
            nc.scalar.activation(keep["pre"][:].rearrange("p n e -> p (n e)"), po[1][:, :], ACT.Copy)\
                .then_inc(keep_ok, 1)
            act.wait_ge(po_ok, 1)
            rounds(act, NG // 2, body)
            take_o(2 * NG - 1, 1)

        @block.vector
        def _(dve):
            nc.vector.memset(po[0][:, :], 0.0).then_inc(po_ok, 1)

            def maximum(use, slot, half, col):
                dve.wait_ge(mx_full, use + 1)
                nc.vector.tensor_reduce(mx[:, half, col:col + 1], pm[slot][:, :, :].rearrange("p a n -> p (a n)"),
                                        AX.X, ALU.max).then_inc(mx_free, 1)

            def maxrows(use, slot, half, sent):
                dve.wait_ge(mx_full, use + 1)
                need(dve, mrow_in[half], 16 * sent)
                nc.vector.tensor_copy(mrow[:, half, :], pm[slot][0:48, 0, 0:P]).then_inc(mx_free, 1)

            def normalise(use, slot, half, u, outs):
                dve.wait_ge(mx_full, use + 1)
                o = pm[slot][:, 0, :].rearrange("p (m w) -> p m w", w=32)
                nc.vector.reciprocal(rec[:].unsqueeze(2), o[:, :, D:VW]).then_inc(rec_ok, 1)
                dve.wait_ge(rec_ok, u + 1)
                need(dve, o_out[half], outs * 16)
                nc.vector.tensor_tensor(on[:, half, :, :, :].rearrange("p n h d -> p (n h) d"), o[:, :, 0:D],
                                        rec[:].unsqueeze(2).to_broadcast([P, 16, D]), ALU.mult).then_inc(mx_free, 1)

            planned = Chain(dve, plan_dve)
            for use in range(FIRST):
                n = use - (use > FIRST_ROWS)
                if use == FIRST_ROWS - 3:
                    dve.wait_ge(keep_ok, 1)
                    plan_counts(nc, planned, plan, keep, counters_ok, nt_ok)
                if use == FIRST_ROWS:
                    maxrows(use, use % 2, 0, 0)
                else:
                    maximum(use, use % 2, n // 16, n % 16)

            def body(j):
                for gg in range(2):
                    g = j * 2 + gg
                    for k in range(QUADS):
                        if k in (SWITCH, SWITCH + 8):
                            need(dve, mp_ok, 2 * g + 1 + k // 8)
                        if isinstance(j, int) and gg == 0 and k == 3:
                            plan_tiles(nc, planned, plan, sums_ok, eid_ok)
                        for i, what in enumerate(uses(k)):
                            use = place(g, k, i)
                            slot = (FIRST + before[k] + i) % 2
                            if what == "out":
                                u = 2 * g + k // 8 - 1
                                half = (k // 8 + 1) % 2
                                if isinstance(u, int) and u < 0:
                                    dve.wait_ge(mx_full, use + 1)
                                    nc.vector.memset(rec[:], 1.0).then_inc(mx_free, 1)
                                    continue
                                normalise(use, slot, half, u, g - (1 if half else 0))
                            elif what == "rows":
                                half = 1 if k == ROWS1 else 0
                                maxrows(use, slot, half, g if half else g + 1)
                            else:
                                maximum(use, slot, what // 16, what % 16)
            rounds(dve, NG // 2, body)
            normalise(FIRST + NG * PER, (FIRST + NG * PER) % 2, 1, 2 * NG - 1, NG - 1)

        @block.tensor
        def _(pe):
            def scores_max(buf, task, slot, use):
                for kk in range(2):
                    max_half(buf, task, slot, use, kk)

            def max_half(buf, task, slot, use, kk):
                half, h, qi = task // 16, task % 16 // 4, task % 4
                if kk == 0:
                    need(pe, mx_free, use - 1)
                mm = pe.matmul(pm[slot][:, kk, :], qt[buf][0:KR, half, h, qi * P:(qi + 1) * P],
                               kt[buf][0:KR, h, kk * 512:(kk + 1) * 512], start=True, stop=True)
                if kk == 1:
                    mm.then_inc(mx_full, 1)

            def turn_rows(slot, use, half, n):
                need(pe, mx_free, use - 1)
                pe.wait_ge(mp_ok, n + 1)
                pe.matmul(pm[slot][0:48, 0, 0:P], mp[:, half, :, :].rearrange("p a c -> p (a c)"), identb[:],
                          start=True, stop=True).then_inc(mx_full, 1)

            def turn_out(slot, use, u):
                need(pe, mx_free, use - 1)
                pe.wait_ge(osb_ok, u + 1)
                for n in range(4):
                    mm = pe.transpose(pm[slot][:, 0, n * P:(n + 1) * P], osb[:, n * P:(n + 1) * P], ident[:])
                mm.then_inc(mx_full, 1)

            def scores(buf, half, kc, h, s):
                need(pe, exp_ok, s - 1)
                pe.matmul(pst[h % 2][:, :], kt[buf][0:KR + MR, h, kc * P:(kc + 1) * P],
                          qt[buf][0:KR + MR, half, h, :], start=True, stop=True)\
                    .then_inc(st_ok, 1)

            def pv(buf, k, q, u):
                pe.wait_ge(exp_ok, 4 * (q + 1))
                if k % 8 == 0:
                    need(pe, osb_ok, u - 1)
                for h in range(HG):
                    mm = pe.matmul(po[k // 8][32 * h:32 * h + VW, :], vt[buf][:, k % 8, h * VW:(h + 1) * VW],
                                   pr[:, (k % 2) * 4 + h, :], start=(k % 8 == 0), stop=(k % 8 == 7),
                                   tile_position=(0, 32 * h))
                mm.then_inc(pv_ok, 1)

            pe.wait_ge(id_ok, 1)
            pe.wait_ge(qk_in[0], LOAD)
            sel, pre = keep["sel"], po[1][:, :].rearrange("p (n e) -> p n e", e=E)

            def count_ahead(n):
                if n < 0:
                    pe.matmul(pst[1][:, 0:E], keep["ones"][:], keep["cnt"][:], start=True, stop=True).then_inc(pre_ok, 1)
                    pe.matmul(pre, keep["below"][:], sel[:], start=True, stop=True)
                elif n < NT - 1:
                    mm = pe.matmul(pre[:, n + 1:NT, :], keep["ones"][:],
                                   sel[:, n:n + 1, :].to_broadcast([P, NT - 1 - n, E]),
                                   start=False, stop=True, skip_group_check=True)
                    if n == NT - 2:
                        mm.then_inc(pre_ok, 1)

            for use in range(FIRST):
                for n in range(2 * use - 1, 2 * use + 1):
                    count_ahead(n)
                if use == FIRST_ROWS:
                    turn_rows(use % 2, use, 0, 0)
                else:
                    scores_max(0, use - (use > FIRST_ROWS), use % 2, use)
            pe.wait_ge(po_ok, 1)
            pe.wait_ge(keep_ok, 2)

            def body(j):
                for gg in range(2):
                    g = j * 2 + gg
                    for k in range(QUADS):
                        q = g * QUADS + k
                        half, kc = k // 8, k % 8
                        if k == 0:
                            pe.wait_ge(mrow_in[0], 16 * (g + 1))
                            pe.wait_ge(v_in[gg], 16 * (j + 1))
                        if k == 8:
                            pe.wait_ge(mrow_in[1], 16 * (g + 1))
                        if k == SWITCH:
                            if isinstance(g, int) and g == 0:
                                pe.wait_ge(row1_ok, 1)
                            pe.wait_ge(qk_in[1 - gg], LOAD * (j + 1 + gg))
                        mbuf = gg if k < SWITCH else 1 - gg
                        us = uses(k)
                        slots = [(FIRST + before[k] + i) % 2 for i in range(len(us))]
                        scores(gg, half, kc, 0, 4 * q)
                        scores(gg, half, kc, 1, 4 * q + 1)
                        max_half(mbuf, us[0], slots[0], place(g, k, 0), 0)
                        max_half(mbuf, us[0], slots[0], place(g, k, 0), 1)
                        max_half(mbuf, us[1], slots[1], place(g, k, 1), 0)
                        scores(gg, half, kc, 2, 4 * q + 2)
                        max_half(mbuf, us[1], slots[1], place(g, k, 1), 1)
                        scores(gg, half, kc, 3, 4 * q + 3)
                        if not (isinstance(q, int) and q == 0):
                            pb, pk = (gg, k - 1) if k else (1 - gg, QUADS - 1)
                            pv(pb, pk, q - 1, 2 * g + pk // 8 if k else 2 * g - 1)
                        if len(us) == 3:
                            if us[2] == "out":
                                u = 2 * g + k // 8 - 1
                                if isinstance(u, int) and u < 0:
                                    need(pe, mx_free, place(g, k, 2) - 1)
                                    pe.matmul(pm[slots[2]][:, 0, 0:P], identb[:], identb[:], start=True,
                                              stop=True).then_inc(mx_full, 1)
                                else:
                                    turn_out(slots[2], place(g, k, 2), u)
                            else:
                                turn_rows(slots[2], place(g, k, 2), 1 if k == ROWS1 else 0,
                                          2 * g + (1 if k == ROWS1 else 2))
            rounds(pe, NG // 2, body)
            pv(1, QUADS - 1, NG * QUADS - 1, 2 * NG - 1)
            end = FIRST + NG * PER
            turn_out(end % 2, end, 2 * NG - 1)


BUF_D, EARLY = 8, 4


def load_token_tile(eng, x, s_xn, s_o, keep, k, buf):
    rows = bass.ds(k * P, P)
    done = keep["in_ok"][buf]
    eng.dma_start(keep["xr"][:, buf, :], x.rearrange("b t c -> (b t) c")[rows, :]).then_inc(done, 16)
    eng.dma_start(keep["xo"][:, buf, 0, :], s_xn[rows, :]).then_inc(done, 16)
    eng.dma_start(keep["xo"][:, buf, 1, :], s_o[rows, :]).then_inc(done, 16)


def stage_c(nc, x, s_xn, s_o, s_idx, s_y, keep):
    PER, HALF = 8, 4
    with ExitStack() as ctx:
        sb = lambda n, s, d=F32: ctx.enter_context(nc.sbuf_tensor(n, s, d))
        sem = lambda n: ctx.enter_context(nc.semaphore(n))
        w13, w2, eid = keep["w13"], keep["w2"], keep["eid"]
        idf, idf_in = keep["idf"], keep["idf_in"]
        idx = sb("idx", [P, NX], U32)
        slot = sb("slot_c", [P, 2, HALF], U32)
        xg = sb("xg", [P, PER, C])
        xt = sb("xt_c", [P, 2, CC, P])
        sg = sb("sg_c", [P, 2, F])
        hb = sb("hb_c", [P, 2, F])
        ht = sb("ht_c", [P, 2, P])
        ys = sb("ys_c", [P, 4, C])
        ident = keep["ident"]
        pT, pG, pH, pY = ([ctx.enter_context(nc.psum_tensor(f"c_{n}{i}", [P, 512], F32)) for i in range(2)]
                          for n in ("pT", "pG", "pH", "pY"))
        idT_ok, idx_ok, slot_ok = (sem("c_" + n) for n in ("idT_ok", "idx_ok", "slot_ok"))
        g_in = [sem(f"g_in{i}") for i in range(PER)]
        y_out = [sem(f"yc_out{i}") for i in range(4)]
        xT_ok, xt_ok, gu_ok, sg_ok, hb_ok, hT_ok, ht_ok, yy_ok, ys_ok = (
            sem("c_" + n) for n in ("xT_ok", "xt_ok", "gu_ok", "sg_ok", "hb_ok", "hT_ok", "ht_ok", "yy_ok", "ys_ok"))
        passed = sem("passed_c")
        block = ctx.enter_context(nc.Block())
        UP, HT, DOWN = 1, 3, 4

        @block.sync
        def _(sp):
            for k in range(EARLY):
                load_token_tile(sp, x, s_xn, s_o, keep, k, k)

            def store(k, t, j):
                sp.wait_ge(ys_ok, k + 1)
                sp.dma_start(s_y[bass.ds(k * P, P), :], ys[:, t % 4, :]).then_inc(y_out[t % 4], 16)
            steps(sp, NX // PER, PER, NX, [(DOWN, store)])
            for i in range(4):
                sp.wait_ge(y_out[i], 16 * NX // 4)

        @block.gpsimd
        def _(pool):
            pool.wait_ge(idx_ok, 1)

            def gather(k, t, j):
                half = t // HALF
                if t % HALF == 0:
                    if not isinstance(j, int):
                        for i in range(HALF):
                            wait_alone(pool, g_in[t + i], 16 * j, passed)
                    nc.gpsimd.tensor_copy(slot[:, half, :], idx[:, bass.ds(k, HALF)]).then_inc(slot_ok, 1)
                    wait_alone(pool, slot_ok, 2 * j + half + 1, passed)
                if not isinstance(j, int):
                    wait_alone(pool, xT_ok, k - PER + 1, passed)
                pool.indirect_dma_start(
                    out=xg[:, t, :], out_offset=None, in_=s_xn,
                    in_offset=bass.IndirectOffsetOnAxis(ap=slot[:, half, t % HALF:t % HALF + 1], axis=0))\
                    .then_inc(g_in[t], 16)
            steps(pool, NX // PER, PER, NX, [(0, gather)])

        @block.scalar
        def _(act):
            def turned(k, t, j):
                act.wait_ge(xT_ok, k + 1)
                need(act, gu_ok, k - 1)
                nc.scalar.activation(xt[:, t % 2, :, :], pT[t % 2][:, 0:C].rearrange("p (c n) -> p c n", c=CC),
                                     ACT.Copy).then_inc(xt_ok, 1)

            def silu(k, t, j):
                act.wait_ge(gu_ok, k + 1)
                need(act, hb_ok, k - 1)
                nc.scalar.activation(sg[:, t % 2, :], pG[t % 2][:, 0:F], ACT.Silu).then_inc(sg_ok, 1)
            steps(act, NX // PER, PER, NX, [(0, turned), (UP, silu)])

        @block.vector
        def _(dve):
            dve.wait_ge(idT_ok, 2)
            for q in range(2):
                last = nc.vector.tensor_copy(idx[:, q * NX // 2:(q + 1) * NX // 2], pT[q][:, 0:NX // 2])
            last.then_inc(idx_ok, 1)

            def output(k, t, j):
                dve.wait_ge(yy_ok, k + 1)
                need(dve, y_out[t % 4], (2 * j + t // 4) * 16)
                nc.vector.tensor_copy(ys[:, t % 4, :], pY[t % 2][:, 0:C]).then_inc(ys_ok, 1)

            def turned(k, t, j):
                dve.wait_ge(hT_ok, k + 1)
                need(dve, yy_ok, k - 1)
                nc.vector.tensor_copy(ht[:, t % 2, :], pH[t % 2][:, 0:P]).then_inc(ht_ok, 1)

            def gated(k, t, j):
                dve.wait_ge(sg_ok, k + 1)
                need(dve, hT_ok, k - 1)
                nc.vector.tensor_tensor(hb[:, t % 2, :], pG[t % 2][:, F:2 * F], sg[:, t % 2, :], ALU.mult)\
                    .then_inc(hb_ok, 1)
            steps(dve, NX // PER, PER, NX, [(DOWN, output), (HT, turned), (UP, gated)])

        @block.tensor
        def _(pe):
            pe.wait_ge(keep["w_in"], 64)
            pe.wait_ge(idf_in, 16)
            for q in range(2):
                pe.transpose(pT[q][:, 0:NX // 2], idf[:, q, :], ident[0:NX // 2, 0:NX // 2]).then_inc(idT_ok, 1)
            pe.wait_ge(idx_ok, 1)

            LOOK = 4
            expert = [pe.alloc_register(f"expert{t}") for t in range(PER)]

            def look_up(k, t, j):
                if t % LOOK == 0:
                    pe.load(expert[t:t + LOOK], eid[0:1, bass.ds(k, LOOK)])

            def chosen(t):
                return bass.ds(pe.snap(expert[t], min_val=0, max_val=E - 1), 1)

            def turn(k, t, j):
                pe.wait_ge(g_in[t], 16 * (j + 1))
                need(pe, xt_ok, k - 1)
                for c in range(CC):
                    mm = pe.transpose(pT[t % 2][:, c * P:(c + 1) * P], xg[:, t, c * P:(c + 1) * P], ident[:])
                mm.then_inc(xT_ok, 1)

            def up(k, t, j):
                pe.wait_ge(xt_ok, k + 1)
                need(pe, hb_ok, k - 1)
                for c in range(CC):
                    mm = pe.matmul(pG[t % 2][:, 0:2 * F], xt[:, t % 2, c, :],
                                   w13[:, c, chosen(t), :].rearrange("p a n -> p (a n)"),
                                   start=(c == 0), stop=(c == CC - 1))
                mm.then_inc(gu_ok, 1)

            def turn_h(k, t, j):
                pe.wait_ge(hb_ok, k + 1)
                need(pe, ht_ok, k - 1)
                pe.transpose(pH[t % 2][:, 0:P], hb[:, t % 2, :], ident[:]).then_inc(hT_ok, 1)

            def down(k, t, j):
                pe.wait_ge(ht_ok, k + 1)
                need(pe, ys_ok, k - 1)
                pe.matmul(pY[t % 2][:, 0:C], ht[:, t % 2, :],
                          w2[:, chosen(t), :].rearrange("p a n -> p (a n)"),
                          start=True, stop=True).then_inc(yy_ok, 1)
            steps(pe, NX // PER, PER, NX, [(0, look_up), (0, turn), (DOWN, down), (HT, turn_h), (UP, up)])


def stage_d(nc, x, s_xn, s_o, s_y, out, keep):
    PER, HALF, BUF = 8, 4, BUF_D
    used = lambda t, j, n: j * PER // n + t // n
    with ExitStack() as ctx:
        sb = lambda n, s, d=F32: ctx.enter_context(nc.sbuf_tensor(n, s, d))
        sem = lambda n: ctx.enter_context(nc.semaphore(n))
        w13, w2, wo, bo = keep["w13"], keep["w2"], keep["w_out"], keep["b_out"]
        xr, xo, in_ok = keep["xr"], keep["xo"], keep["in_ok"]
        xot = sb("xot", [P, BUF, 4, P])
        slot = sb("slot_d", [P, 2, HALF * TOPK], U32)
        yg = sb("yg", [P, BUF, TOPK, C])
        acc = sb("acc", [P, 2, C])
        sg = sb("sg_d", [P, 2, NS, F])
        hb = sb("hb_d", [P, 2, NS, F])
        ht = sb("ht_d", [P, 2, NS, P])
        ys = sb("ys_d", [P, 2, C])
        ident = keep["ident"]
        pT, pG, pH, pA = ([ctx.enter_context(nc.psum_tensor(f"d_{n}{i}", [P, 512], F32)) for i in range(2)]
                          for n in ("pT", "pG", "pH", "pA"))
        yg_in = [sem(f"yg_in{i}") for i in range(BUF)]
        y_out = [sem(f"yd_out{i}") for i in range(2)]
        slot_ok, xT_ok, xt_ok, gu_ok, sg_ok, hb_ok, hT_ok, ht_ok, pa_ok, acc_ok, ys_ok = (
            sem("d_" + n) for n in ("slot_ok", "xT_ok", "xt_ok", "gu_ok", "sg_ok", "hb_ok", "hT_ok", "ht_ok",
                                    "pa_ok", "acc_ok", "ys_ok"))
        dve_own, passed = sem("dve_own_d"), sem("passed_d")
        block = ctx.enter_context(nc.Block())
        od = out.rearrange("b t c -> (b t) c")
        UP, HT, SUM, DOWN = 1, 3, 3, 4

        @block.sync
        def _(sp):
            def load(k, t, j):
                if isinstance(k, int) and k < EARLY:
                    return
                need(sp, xT_ok, k - BUF + 1)
                need(sp, acc_ok, k - BUF + 1)
                load_token_tile(sp, x, s_xn, s_o, keep, k, t % BUF)

            def store(k, t, j):
                sp.wait_ge(ys_ok, k + 1)
                sp.dma_start(od[bass.ds(k * P, P), :], ys[:, t % 2, :]).then_inc(y_out[t % 2], 16)
            steps(sp, NT // PER, PER, NT, [(0, load), (DOWN + 1, store)])
            for i in range(2):
                sp.wait_ge(y_out[i], 16 * NT // 2)

        @block.gpsimd
        def _(pool):

            def gather(k, t, j):
                half = t // HALF
                if t % HALF == 0:
                    if not isinstance(j, int):
                        wait_alone(pool, acc_ok, k - HALF, passed)
                    nc.gpsimd.tensor_copy(slot[:, half, :], keep["where"][:, bass.ds(k * TOPK, HALF * TOPK)])\
                        .then_inc(slot_ok, 1)
                    wait_alone(pool, slot_ok, 2 * j + half + 1, passed)
                for n in range(TOPK):
                    place = (t % HALF) * TOPK + n
                    pool.indirect_dma_start(
                        out=yg[:, t % BUF, n, :], out_offset=None, in_=s_y,
                        in_offset=bass.IndirectOffsetOnAxis(ap=slot[:, half, place:place + 1], axis=0))\
                        .then_inc(yg_in[t % BUF], 16)
            steps(pool, NT // PER, PER, NT, [(0, gather)])

        @block.scalar
        def _(act):
            def turned(k, t, j):
                act.wait_ge(xT_ok, k + 1)
                need(act, pa_ok, k - BUF + 1)
                nc.scalar.activation(xot[:, t % BUF, :, :], pT[t % 2][:, :].rearrange("p (k n) -> p k n", k=4), ACT.Copy)\
                    .then_inc(xt_ok, 1)

            def silu(k, t, j):
                act.wait_ge(gu_ok, k + 1)
                need(act, hb_ok, k - 1)
                nc.scalar.activation(sg[:, t % 2, :, :],
                                     pG[t % 2][:, :].rearrange("p (s g f) -> p s g f", s=NS, g=2)[:, :, 0, :], ACT.Silu)\
                    .then_inc(sg_ok, 1)
            steps(act, NT // PER, PER, NT, [(0, turned), (UP, silu)])

        @block.vector
        def _(dve):
            own = Chain(dve, dve_own)
            v = nc.vector

            def output(k, t, j):
                dve.wait_ge(pa_ok, k + 1)
                dve.wait_ge(acc_ok, k + 1)
                need(dve, y_out[t % 2], used(t, j, 2) * 16)
                v.tensor_tensor(ys[:, t % 2, :], pA[t % 2][:, 0:C], acc[:, t % 2, :], ALU.add).then_inc(ys_ok, 1)

            def turned(k, t, j):
                dve.wait_ge(hT_ok, k + 1)
                need(dve, pa_ok, k - 1)
                v.tensor_copy(ht[:, t % 2, :, :], pH[t % 2][:, 0:NS * P].rearrange("p (s n) -> p s n", s=NS))\
                    .then_inc(ht_ok, 1)

            def gated(k, t, j):
                dve.wait_ge(sg_ok, k + 1)
                need(dve, hT_ok, k - 1)
                v.tensor_tensor(hb[:, t % 2, :, :],
                                pG[t % 2][:, :].rearrange("p (s g f) -> p s g f", s=NS, g=2)[:, :, 1, :],
                                sg[:, t % 2, :, :], ALU.mult).then_inc(hb_ok, 1)

            def combine(k, t, j):
                own.base, own.n = k * TOPK, 0
                dve.wait_ge(in_ok[t % BUF], 48 * (used(t, j, BUF) + 1))
                need(dve, ys_ok, k - 1)
                own.link(v.tensor_tensor(acc[:, t % 2, :], xr[:, t % BUF, :], bo[:], ALU.add))
                dve.wait_ge(yg_in[t % BUF], 64 * (used(t, j, BUF) + 1))
                for n in range(TOPK):
                    w = keep["wk"][:, bass.ds(k, 1), n:n + 1].rearrange("p a b -> p (a b)")
                    ins = v.scalar_tensor_tensor(out=acc[:, t % 2, :], in0=yg[:, t % BUF, n, :], scalar=w,
                                                 in1=acc[:, t % 2, :], op0=ALU.mult, op1=ALU.add)
                    if n < TOPK - 1:
                        own.link(ins)
                ins.then_inc(acc_ok, 1)
            steps(dve, NT // PER, PER, NT, [(DOWN, output), (HT, turned), (UP, gated), (SUM, combine)])

        @block.tensor
        def _(pe):

            def turn(k, t, j):
                pe.wait_ge(in_ok[t % BUF], 48 * (used(t, j, BUF) + 1))
                need(pe, xt_ok, k - 1)
                for n in range(4):
                    mm = pe.transpose(pT[t % 2][:, n * P:(n + 1) * P],
                                      xo[:, t % BUF, n // 2, (n % 2) * P:(n % 2 + 1) * P], ident[:])
                mm.then_inc(xT_ok, 1)

            def up(k, t, j):
                pe.wait_ge(xt_ok, k + 1)
                need(pe, hb_ok, k - 1)
                for c in range(CC):
                    mm = pe.matmul(pG[t % 2][:, :], xot[:, t % BUF, c, :],
                                   w13[:, c, E:E + NS, :].rearrange("p s n -> p (s n)"),
                                   start=(c == 0), stop=(c == CC - 1))
                mm.then_inc(gu_ok, 1)

            def turn_h(k, t, j):
                pe.wait_ge(hb_ok, k + 1)
                need(pe, ht_ok, k - 1)
                for n in range(NS):
                    mm = pe.transpose(pH[t % 2][:, n * P:(n + 1) * P], hb[:, t % 2, n, :], ident[:])
                mm.then_inc(hT_ok, 1)

            def down(k, t, j):
                pe.wait_ge(ht_ok, k + 1)
                need(pe, ys_ok, k - 1)
                for c in range(CC):
                    pe.matmul(pA[t % 2][:, 0:C], xot[:, t % BUF, 2 + c, :], wo[:, c, :], start=(c == 0), stop=False)
                for n in range(NS):
                    mm = pe.matmul(pA[t % 2][:, 0:C], ht[:, t % 2, n, :], w2[:, E + n, :], start=False,
                                   stop=(n == NS - 1))
                mm.then_inc(pa_ok, 1)
            steps(pe, NT // PER, PER, NT, [(0, turn), (DOWN, down), (HT, turn_h), (UP, up)])


def program(nc, x, w_qkvg, b_qkv, rope, w13, w2, w_out, b_out, out):
    s_q = nc.dram_tensor("s_q", [2, B, 3, D, H, QH], BF16).ap()
    s_k = nc.dram_tensor("s_k", [B, 3, D, H, T], BF16).ap()
    s_v = nc.dram_tensor("s_v", [N, H, VW], F32).ap()
    s_xn = nc.dram_tensor("s_xn", [N, C], F32).ap()
    s_o = nc.dram_tensor("s_o", [N, C], F32).ap()
    s_idx = nc.dram_tensor("s_idx", [NX * P, 1], F32).ap()
    s_y = nc.dram_tensor("s_y", [NX * P, C], F32).ap()
    with ExitStack() as ctx:
        sb = lambda n, shape, d=F32: ctx.enter_context(nc.sbuf_tensor(n, shape, d))
        keep = dict(
            sel=sb("sel", [P, NT, E], BF16),
            mk=sb("mk", [P, NT, TOPK, E]),
            wk=sb("wk", [P, NT, TOPK]),
            pre=sb("pre", [P, NT, E]),
            tot=sb("tot", [P, E]),
            cntf=sb("cntf", [P, E]), cnt=sb("cnt", [P, E], BF16),
            ones=sb("ones", [P, P], BF16), below=sb("below", [P, P], BF16),
            where=sb("where", [P, NT * TOPK], U32),
            eid=sb("eid", [1, 2 * P], I32),
            ident=sb("ident", [P, P]),
            idf=sb("idf", [NX // 2, 2, P]), idf_in=ctx.enter_context(nc.semaphore("idf_in")),
            w13=sb("w13s", [P, CC, E + NS, 2 * F]), w2=sb("w2s", [P, E + NS, C]),
            w_out=sb("wos", [P, CC, C]), b_out=sb("bos", [P, C]),
            in_ok=[ctx.enter_context(nc.semaphore(f"in_ok{i}")) for i in range(BUF_D)],
            w_in=ctx.enter_context(nc.semaphore("w_in_c")))
        first = dict(
            qt=sb("qt0", [P, 2, HG, QH], BF16), kt=sb("kt0", [P, HG, T], BF16), vt=sb("vt0", [P, KC, HG * VW]),
            qk_in=ctx.enter_context(nc.semaphore("qk_in0")), v_in=ctx.enter_context(nc.semaphore("v_in0")))
        stage_a(nc, x, w_qkvg, b_qkv, rope, s_q, s_k, s_v, s_xn, keep, first)
        stage_b(nc, s_q, s_k, s_v, s_o, s_idx, w13, w2, w_out, b_out, keep, first)
        keep.update(xr=sb("xr", [P, BUF_D, C]), xo=sb("xo", [P, BUF_D, 2, C]))
        stage_c(nc, x, s_xn, s_o, s_idx, s_y, keep)
        stage_d(nc, x, s_xn, s_o, s_y, out, keep)


def rope_table():
    inv = (1.0 / ROPE_BASE ** (np.arange(0, D, 2, dtype=np.float32) / np.float32(D))).astype(np.float32)
    angle = (np.arange(T, dtype=np.float32)[:, None] * inv[None, :]).astype(np.float64)
    cos, sin = np.cos(angle), np.sin(angle)
    return np.stack([np.concatenate([cos, cos], 1), np.concatenate([-sin, sin], 1)], 1).astype(np.float32)


def kernel(L0_attn_x, L0_attn_W_qkv, L0_attn_b_qkv, L0_attn_W_out, L0_attn_b_out, L0_ffn_w_gate, L0_ffn_w1_e,
           L0_ffn_w3_e, L0_ffn_w2_e, L0_ffn_w1_s, L0_ffn_w3_s, L0_ffn_w2_s):
    import concourse.bacc as bacc
    from concourse.bass_utils import run_bass_kernel_spmd

    a = lambda v: np.ascontiguousarray(v)
    up = lambda e, s: np.concatenate([np.asarray(e), np.asarray(s).reshape(NS, F, C)], 0).transpose(2, 0, 1)
    arrays = {
        "x": a(L0_attn_x),
        "w_qkvg": a(np.concatenate([np.asarray(L0_attn_W_qkv), np.asarray(L0_ffn_w_gate).T], 1)),
        "b_qkv": a(L0_attn_b_qkv),
        "rope": rope_table(),
        "w13": a(np.concatenate([up(L0_ffn_w1_e, L0_ffn_w1_s), up(L0_ffn_w3_e, L0_ffn_w3_s)], 2)),
        "w2": a(np.concatenate([np.asarray(L0_ffn_w2_e).transpose(2, 0, 1),
                                np.asarray(L0_ffn_w2_s).reshape(C, NS, F).transpose(2, 1, 0)], 1)),
        "w_out": a(L0_attn_W_out),
        "b_out": a(L0_attn_b_out),
    }
    nc = bacc.Bacc("TRN2", target_bir_lowering=False, num_devices=1)
    aps = {n: nc.dram_tensor(n, v.shape, mybir.dt.from_np(v.dtype), kind="ExternalInput").ap()
           for n, v in arrays.items()}
    out = nc.dram_tensor("out", [B, T, C], F32, kind="ExternalOutput").ap()
    program(nc, **aps, out=out)
    return run_bass_kernel_spmd(nc, [arrays], core_ids=[0]).results[0]["out"]
```
